# Optimizing a Trainium2 kernel written in Bass

```python
import numpy as np
import jax
import jax.numpy as jnp

def _softmax(x, axis=-1):
    return jax.nn.softmax(x, axis=axis)

def _gelu(x):
    return jax.nn.gelu(x, approximate=True)

def _silu(x):
    return jax.nn.silu(x)

def _sigmoid(x):
    return jax.nn.sigmoid(x)

def _layernorm(x, axis=-1, eps=1e-05):
    m = jnp.mean(x, axis=axis, keepdims=True)
    v = jnp.var(x, axis=axis, keepdims=True)
    return (x - m) / jnp.sqrt(v + eps)

def _scatter_add(tgt, idx, src, axis=0):
    return tgt.at[idx].add(src)

def _segment_sum(src, seg, n):
    return jax.ops.segment_sum(src, seg, n)
kernel_name = 'mk_sandwich_d1_jaxref_r4_a88890'

def setup_inputs(seed: int=0):
    np.random.seed(seed)
    _w = jnp.asarray

    def _L0_attn_setup():
        import jax, jax.numpy as jnp
        import numpy as np
        EMBED = 256
        HEADS = 16
        HEAD_DIM = EMBED // HEADS
        B, T = (2, 512)
        ROPE_THETA = 10000.0

        def _rope(x):
            D = x.shape[-1]
            inv_freq = 1.0 / ROPE_THETA ** (jnp.arange(0, D, 2, dtype=jnp.float32) / D)
            freqs = jnp.arange(x.shape[2], dtype=jnp.float32)[:, None] * inv_freq[None, :]
            cos = jnp.cos(freqs).astype(x.dtype)
            sin = jnp.sin(freqs).astype(x.dtype)
            x1, x2 = (x[..., :D // 2], x[..., D // 2:])
            return jnp.concatenate([x1 * cos - x2 * sin, x2 * cos + x1 * sin], axis=-1)
        key = jax.random.key(seed)
        ks = jax.random.split(key, 5)
        s = 1.0 / np.sqrt(EMBED)
        return {'x': jax.random.normal(ks[0], (B, T, EMBED), dtype=jnp.float32), 'Wq': jax.random.normal(ks[1], (EMBED, EMBED), dtype=jnp.float32) * s, 'bq': jnp.zeros((EMBED,), dtype=jnp.float32), 'Wk': jax.random.normal(ks[2], (EMBED, EMBED), dtype=jnp.float32) * s, 'bk': jnp.zeros((EMBED,), dtype=jnp.float32), 'Wv': jax.random.normal(ks[3], (EMBED, EMBED), dtype=jnp.float32) * s, 'bv': jnp.zeros((EMBED,), dtype=jnp.float32), 'Wo': jax.random.normal(ks[4], (EMBED, EMBED), dtype=jnp.float32) * s, 'bo': jnp.zeros((EMBED,), dtype=jnp.float32)}
    _L0_attn_in = _L0_attn_setup()

    def _L0_ffn_setup():
        import jax, jax.numpy as jnp
        import numpy as np
        DIM = 256
        DEPTH = 2
        HEADS = 8
        DIM_HEAD = 64
        WINDOW = 128
        INNER = HEADS * DIM_HEAD
        HID = int(DIM * 4 * 2 / 3)
        B, N = (2, 2048)
        QK_SCALE = 8.0

        def shift_token(t):
            t1, t2 = jnp.split(t, 2, axis=-1)
            t2 = jnp.pad(t2, ((0, 0), (1, 0), (0, 0)))[:, :-1]
            return jnp.concatenate([t1, t2], axis=-1)

        def l2norm(t):
            return t / jnp.clip(jnp.linalg.norm(t, axis=-1, keepdims=True), 1e-12)

        def rotate_half(x):
            x1, x2 = jnp.split(x, 2, axis=-1)
            return jnp.concatenate([-x2, x1], axis=-1)

        def rotary_xpos(q, k):
            n = q.shape[-2]
            half_idx = jnp.arange(0, DIM_HEAD, 2, dtype=jnp.float32)
            inv_freq = 1.0 / 10000.0 ** (half_idx / DIM_HEAD)
            t = jnp.arange(n, dtype=jnp.float32)
            freqs = t[:, None] * inv_freq[None, :]
            freqs = jnp.concatenate([freqs, freqs], axis=-1)
            base = (half_idx + 0.4 * DIM_HEAD) / (1.4 * DIM_HEAD)
            power = (t - n // 2) / float(WINDOW // 2)
            scale = base[None, :] ** power[:, None]
            scale = jnp.concatenate([scale, scale], axis=-1)
            cos, sin = (jnp.cos(freqs), jnp.sin(freqs))
            q = q * cos * scale + rotate_half(q) * sin * scale
            k = k * cos / scale + rotate_half(k) * sin / scale
            return (q, k)

        def local_attention(q, k, v):
            b, h, n, d = q.shape
            w = n // WINDOW
            bq = q.reshape(b, h, w, WINDOW, d) * QK_SCALE
            bk = k.reshape(b, h, w, WINDOW, d)
            bv = v.reshape(b, h, w, WINDOW, d)

            def look_around(t):
                p = jnp.pad(t, ((0, 0), (0, 0), (1, 0), (0, 0), (0, 0)))
                return jnp.concatenate([p[:, :, :w], p[:, :, 1:]], axis=3)
            bk, bv = (look_around(bk), look_around(bv))
            bt = jnp.arange(n).reshape(w, WINDOW)
            btp = jnp.pad(bt, ((1, 0), (0, 0)), constant_values=-1)
            btk = jnp.concatenate([btp[:w], btp[1:]], axis=1)
            sim = jnp.einsum('bhwid,bhwjd->bhwij', bq, bk)
            i = bt[:, :, None]
            j = btk[:, None, :]
            mask = (i < j) | (i > j + WINDOW) | (j == -1)
            sim = jnp.where(mask, -jnp.finfo(sim.dtype).max, sim)
            attn = jax.nn.softmax(sim, axis=-1)
            out = jnp.einsum('bhwij,bhwjd->bhwid', attn, bv)
            return out.reshape(b, h, n, d)

        def _layer(x, wqkv, qs, ksc, wo, lg, lb, w1, b1, w2, b2):
            b, n, _ = x.shape
            h = shift_token(x)
            qkv = h @ wqkv
            q, k, v = jnp.split(qkv, 3, axis=-1)
            to_heads = lambda t: t.reshape(b, n, HEADS, DIM_HEAD).transpose(0, 2, 1, 3)
            q, k, v = (to_heads(q), to_heads(k), to_heads(v))
            q = l2norm(q) * qs
            k = l2norm(k) * ksc
            q, k = rotary_xpos(q, k)
            o = local_attention(q, k, v)
            o = o.transpose(0, 2, 1, 3).reshape(b, n, INNER)
            x = x + o @ wo
            h = shift_token(x)
            mu = h.mean(-1, keepdims=True)
            var = h.var(-1, keepdims=True)
            h = (h - mu) / jnp.sqrt(var + 1e-05) * lg + lb
            h = h @ w1 + b1
            a, g = jnp.split(h, 2, axis=-1)
            h = a * jax.nn.gelu(g, approximate=False)
            x = x + h @ w2 + b2
            return x
        key = jax.random.key(seed)
        ks = jax.random.split(key, 6)
        return {'x': jax.random.normal(ks[0], (B, N, DIM), jnp.float32), 'wqkv': jax.random.normal(ks[1], (DEPTH, DIM, 3 * INNER), jnp.float32) * 0.02, 'q_scale': jnp.ones((DEPTH, DIM_HEAD), jnp.float32), 'k_scale': jnp.ones((DEPTH, DIM_HEAD), jnp.float32), 'wo': jax.random.normal(ks[2], (DEPTH, INNER, DIM), jnp.float32) * 0.02, 'ln_g': jnp.ones((DEPTH, DIM), jnp.float32), 'ln_b': jnp.zeros((DEPTH, DIM), jnp.float32), 'w1': jax.random.normal(ks[3], (DEPTH, DIM, 2 * HID), jnp.float32) * 0.02, 'b1': jnp.zeros((DEPTH, 2 * HID), jnp.float32), 'w2': jax.random.normal(ks[4], (DEPTH, HID, DIM), jnp.float32) * 0.02, 'b2': jnp.zeros((DEPTH, DIM), jnp.float32)}
    _L0_ffn_in = _L0_ffn_setup()
    _d = {'L0_attn_x': _L0_attn_in['x'], 'L0_attn_Wq': _L0_attn_in['Wq'], 'L0_attn_bq': _L0_attn_in['bq'], 'L0_attn_Wk': _L0_attn_in['Wk'], 'L0_attn_bk': _L0_attn_in['bk'], 'L0_attn_Wv': _L0_attn_in['Wv'], 'L0_attn_bv': _L0_attn_in['bv'], 'L0_attn_Wo': _L0_attn_in['Wo'], 'L0_attn_bo': _L0_attn_in['bo'], 'L0_ffn_wqkv': _L0_ffn_in['wqkv'], 'L0_ffn_q_scale': _L0_ffn_in['q_scale'], 'L0_ffn_k_scale': _L0_ffn_in['k_scale'], 'L0_ffn_wo': _L0_ffn_in['wo'], 'L0_ffn_ln_g': _L0_ffn_in['ln_g'], 'L0_ffn_ln_b': _L0_ffn_in['ln_b'], 'L0_ffn_w1': _L0_ffn_in['w1'], 'L0_ffn_b1': _L0_ffn_in['b1'], 'L0_ffn_w2': _L0_ffn_in['w2'], 'L0_ffn_b2': _L0_ffn_in['b2']}
    _x0 = _d['L0_attn_x']
    _d['L0_attn_x'] = jax.random.normal(jax.random.fold_in(jax.random.key(seed), 1), (2, 2048, 256), dtype=_x0.dtype)
    del _x0
    return _d

def reference(L0_attn_x, L0_attn_Wq, L0_attn_bq, L0_attn_Wk, L0_attn_bk, L0_attn_Wv, L0_attn_bv, L0_attn_Wo, L0_attn_bo, L0_ffn_wqkv, L0_ffn_q_scale, L0_ffn_k_scale, L0_ffn_wo, L0_ffn_ln_g, L0_ffn_ln_b, L0_ffn_w1, L0_ffn_b1, L0_ffn_w2, L0_ffn_b2):

    def _L0_attn_ref(x, Wq, bq, Wk, bk, Wv, bv, Wo, bo):
        import jax, jax.numpy as jnp
        import numpy as np
        EMBED = 256
        HEADS = 16
        HEAD_DIM = EMBED // HEADS
        B, T = (2, 512)
        ROPE_THETA = 10000.0

        def _rope(x):
            D = x.shape[-1]
            inv_freq = 1.0 / ROPE_THETA ** (jnp.arange(0, D, 2, dtype=jnp.float32) / D)
            freqs = jnp.arange(x.shape[2], dtype=jnp.float32)[:, None] * inv_freq[None, :]
            cos = jnp.cos(freqs).astype(x.dtype)
            sin = jnp.sin(freqs).astype(x.dtype)
            x1, x2 = (x[..., :D // 2], x[..., D // 2:])
            return jnp.concatenate([x1 * cos - x2 * sin, x2 * cos + x1 * sin], axis=-1)
        Bb, Tt, C = x.shape
        H, D = (HEADS, HEAD_DIM)

        def proj(W, b):
            return (jnp.einsum('btc,oc->bto', x, W) + b).reshape(Bb, Tt, H, D).transpose(0, 2, 1, 3)
        q = _rope(proj(Wq, bq))
        k = _rope(proj(Wk, bk))
        v = proj(Wv, bv)
        scale = jnp.sqrt(jnp.asarray(D, dtype=x.dtype))
        scores = jnp.einsum('bhtd,bhsd->bhts', q, k) / scale
        attn = jax.nn.softmax(scores, axis=-1)
        out = jnp.einsum('bhts,bhsd->bhtd', attn, v)
        out = out.transpose(0, 2, 1, 3).reshape(Bb, Tt, C)
        return jnp.einsum('btc,oc->bto', out, Wo) + bo

    def _L0_ffn_ref(x, wqkv, q_scale, k_scale, wo, ln_g, ln_b, w1, b1, w2, b2):
        import jax, jax.numpy as jnp
        import numpy as np
        DIM = 256
        DEPTH = 2
        HEADS = 8
        DIM_HEAD = 64
        WINDOW = 128
        INNER = HEADS * DIM_HEAD
        HID = int(DIM * 4 * 2 / 3)
        B, N = (2, 2048)
        QK_SCALE = 8.0

        def shift_token(t):
            t1, t2 = jnp.split(t, 2, axis=-1)
            t2 = jnp.pad(t2, ((0, 0), (1, 0), (0, 0)))[:, :-1]
            return jnp.concatenate([t1, t2], axis=-1)

        def l2norm(t):
            return t / jnp.clip(jnp.linalg.norm(t, axis=-1, keepdims=True), 1e-12)

        def rotate_half(x):
            x1, x2 = jnp.split(x, 2, axis=-1)
            return jnp.concatenate([-x2, x1], axis=-1)

        def rotary_xpos(q, k):
            n = q.shape[-2]
            half_idx = jnp.arange(0, DIM_HEAD, 2, dtype=jnp.float32)
            inv_freq = 1.0 / 10000.0 ** (half_idx / DIM_HEAD)
            t = jnp.arange(n, dtype=jnp.float32)
            freqs = t[:, None] * inv_freq[None, :]
            freqs = jnp.concatenate([freqs, freqs], axis=-1)
            base = (half_idx + 0.4 * DIM_HEAD) / (1.4 * DIM_HEAD)
            power = (t - n // 2) / float(WINDOW // 2)
            scale = base[None, :] ** power[:, None]
            scale = jnp.concatenate([scale, scale], axis=-1)
            cos, sin = (jnp.cos(freqs), jnp.sin(freqs))
            q = q * cos * scale + rotate_half(q) * sin * scale
            k = k * cos / scale + rotate_half(k) * sin / scale
            return (q, k)

        def local_attention(q, k, v):
            b, h, n, d = q.shape
            w = n // WINDOW
            bq = q.reshape(b, h, w, WINDOW, d) * QK_SCALE
            bk = k.reshape(b, h, w, WINDOW, d)
            bv = v.reshape(b, h, w, WINDOW, d)

            def look_around(t):
                p = jnp.pad(t, ((0, 0), (0, 0), (1, 0), (0, 0), (0, 0)))
                return jnp.concatenate([p[:, :, :w], p[:, :, 1:]], axis=3)
            bk, bv = (look_around(bk), look_around(bv))
            bt = jnp.arange(n).reshape(w, WINDOW)
            btp = jnp.pad(bt, ((1, 0), (0, 0)), constant_values=-1)
            btk = jnp.concatenate([btp[:w], btp[1:]], axis=1)
            sim = jnp.einsum('bhwid,bhwjd->bhwij', bq, bk)
            i = bt[:, :, None]
            j = btk[:, None, :]
            mask = (i < j) | (i > j + WINDOW) | (j == -1)
            sim = jnp.where(mask, -jnp.finfo(sim.dtype).max, sim)
            attn = jax.nn.softmax(sim, axis=-1)
            out = jnp.einsum('bhwij,bhwjd->bhwid', attn, bv)
            return out.reshape(b, h, n, d)

        def _layer(x, wqkv, qs, ksc, wo, lg, lb, w1, b1, w2, b2):
            b, n, _ = x.shape
            h = shift_token(x)
            qkv = h @ wqkv
            q, k, v = jnp.split(qkv, 3, axis=-1)
            to_heads = lambda t: t.reshape(b, n, HEADS, DIM_HEAD).transpose(0, 2, 1, 3)
            q, k, v = (to_heads(q), to_heads(k), to_heads(v))
            q = l2norm(q) * qs
            k = l2norm(k) * ksc
            q, k = rotary_xpos(q, k)
            o = local_attention(q, k, v)
            o = o.transpose(0, 2, 1, 3).reshape(b, n, INNER)
            x = x + o @ wo
            h = shift_token(x)
            mu = h.mean(-1, keepdims=True)
            var = h.var(-1, keepdims=True)
            h = (h - mu) / jnp.sqrt(var + 1e-05) * lg + lb
            h = h @ w1 + b1
            a, g = jnp.split(h, 2, axis=-1)
            h = a * jax.nn.gelu(g, approximate=False)
            x = x + h @ w2 + b2
            return x
        for l in range(DEPTH):
            x = _layer(x, wqkv[l], q_scale[l], k_scale[l], wo[l], ln_g[l], ln_b[l], w1[l], b1[l], w2[l], b2[l])
        return x
    x = L0_attn_x
    x = x + _layernorm(_L0_attn_ref(_layernorm(x, axis=-1), L0_attn_Wq, L0_attn_bq, L0_attn_Wk, L0_attn_bk, L0_attn_Wv, L0_attn_bv, L0_attn_Wo, L0_attn_bo), axis=-1)
    x = x + _layernorm(_L0_ffn_ref(_layernorm(x, axis=-1), L0_ffn_wqkv, L0_ffn_q_scale, L0_ffn_k_scale, L0_ffn_wo, L0_ffn_ln_g, L0_ffn_ln_b, L0_ffn_w1, L0_ffn_b1, L0_ffn_w2, L0_ffn_b2), axis=-1)
    return x

_drawn_inputs = setup_inputs


def setup_inputs(seed=0):
    import zlib

    import numpy as np

    out = dict(_drawn_inputs(seed))
    spreads = {'L0_attn_bq': (0.0, 0.354),
     'L0_attn_bk': (0.0, 0.272),
     'L0_attn_bv': (0.0, 0.1),
     'L0_attn_bo': (0.0, 0.1),
     'L0_ffn_q_scale': (1.0, 0.6),
     'L0_ffn_k_scale': (1.0, 0.6),
     'L0_ffn_ln_g': (1.0, 0.6),
     'L0_ffn_ln_b': (0.0, 0.8),
     'L0_ffn_b1': (0.0, 0.8),
     'L0_ffn_b2': (0.0, 0.393)}
    factors = {'L0_ffn_w1': 2.918, 'L0_ffn_w2': 2.86}
    for name, (base, spread) in spreads.items():
        noise = np.random.default_rng([zlib.crc32(name.encode()), seed]).standard_normal(out[name].shape)
        drawn = base * np.exp(spread * noise) if base else spread * noise
        out[name] = jnp.asarray(drawn.astype(out[name].dtype))
    for name, factor in factors.items():
        out[name] = (out[name] * factor).astype(out[name].dtype)
    return out
```

```python
from contextlib import ExitStack

import concourse.bass as bass
from concourse import mybir

F32 = mybir.dt.float32
BF16 = mybir.dt.bfloat16
ACT = mybir.ActivationFunctionType
ALU = mybir.AluOpType
AX = mybir.AxisListType

P = 128
B, T, C = 2, 2048, 256
NT = B * T // P
TB = T // P
H1, D1 = 16, 16
NH = B * H1
NC = C // P
EPS = 1e-5



def identities(nc, block, ident, identb, made):
    @block.gpsimd
    def _(pool):
        nc.gpsimd.memset(ident[:], 0.0).then_inc(made, 1)
        pool.wait_ge(made, 1)
        nc.gpsimd.affine_select(out=ident[:], in_=ident[:], compare_op=ALU.not_equal, fill=1.0,
                                base=0, pattern=[[-1, P]], channel_multiplier=1).then_inc(made, 1)
        pool.wait_ge(made, 2)
        nc.gpsimd.tensor_copy(identb[:], ident[:]).then_inc(made, 1)


def project_phase(nc, ins, x_sb, QO, K1, V1, ident, identb):
    with ExitStack() as ctx:
        sb = lambda n, s, d=F32: ctx.enter_context(nc.sbuf_tensor(n, s, d))
        ps = lambda n, s, d=F32: ctx.enter_context(nc.psum_tensor(n, s, d))
        sem = nc.alloc_semaphore
        HD = D1 // 2
        w_sb = sb("wqkv1_sb", [P, NC, 3 * C])
        bias_sb = sb("bqkv1_sb", [P, 3 * C])
        cos_sb = sb("cos1_sb", [P, TB, HD])
        sin_sb = sb("sin1_sb", [P, TB, 2, HD])
        stats = sb("stats0", [P, NT, 6])
        mv = sb("mv0", [P, NT, 2])
        rstd = sb("rstd0", [P, NT])
        var_eps = sb("var_eps0", [P, NT])
        minus_half = sb("minus_half0", [P, NT])
        nmr = sb("nmr0", [P, NT])
        xn = sb("xn0", [P, 2, C])
        xnT = sb("xnT0", [P, 2, C])
        qk = sb("qk0", [P, 2, 2 * C])
        qk_cos = sb("qk_cos", [P, 2, 2 * C])
        qk_sin = sb("qk_sin", [P, 2, 2 * C])
        psT = ps("psT0", [P, 2, 512])
        psQK = ps("psQK0", [P, 2, 512])
        psV = ps("psV0", [P, 2, 512])
        LOADS = 4
        CH = NT // LOADS
        x_loaded = [sem(f"x_loaded{c}") for c in range(LOADS)]
        weights_loaded, tables_loaded, sin_loaded = sem("w1_loaded"), sem("tables1_loaded"), sem("sin1_loaded")
        ident_made, stats_made, mv_made, rstd_made, nmr_made, xn_made = (sem(n) for n in ("ident_made", "stats0_made", "mv0_made", "rstd0_made", "nmr0_made", "xn0_made"))
        var_made, half_made = sem("var0_made"), sem("half0_made")
        xnT_in_psum, xnT_copied = sem("xnT0_in_psum"), sem("xnT0_copied")
        proj_done, proj_read = sem("proj0_done"), sem("proj0_read")
        qk_biased, cos_done, sin_done, rope_done = sem("qk0_biased"), sem("cos0_done"), sem("sin0_done"), sem("rope0_done")

        block = ctx.enter_context(nc.Block())
        identities(nc, block, ident, identb, ident_made)
        x_tiles = ins["x"].rearrange("b (t p) c -> p (b t) c", p=P)

        @block.sync
        def _(sp):
            for c in range(LOADS):
                sp.dma_start(x_sb[:, c * CH:(c + 1) * CH, :], x_tiles[:, c * CH:(c + 1) * CH, :]).then_inc(x_loaded[c], 16)

        @block.vector
        def _(dve):
            for c in range(LOADS):
                chunk = slice(c * CH, (c + 1) * CH)
                dve.wait_ge(x_loaded[c], 16)
                for i in range(c * CH, (c + 1) * CH):
                    nc.vector.bn_stats(stats[:, i, :], x_sb[:, i, :]).then_inc(stats_made, 1)
                dve.wait_ge(stats_made, (c + 1) * CH)
                for i in range(c * CH, (c + 1) * CH):
                    nc.vector.bn_aggr(mv[:, i, :], stats[:, i, :]).then_inc(mv_made, 1)
                dve.wait_ge(rstd_made, c + 1)
                nc.vector.scalar_tensor_tensor(nmr[:, chunk], mv[:, chunk, 0], -1.0, rstd[:, chunk], ALU.mult, ALU.mult).then_inc(nmr_made, 1)
            dve.wait_ge(tables_loaded, 32)
            for b in range(B):
                heads = slice(b * H1, (b + 1) * H1)
                with dve.Fori(0, TB // 2) as g:
                    for s in range(2):
                        tb = 2 * g + s
                        dve.wait_ge(proj_done, 1 + s)
                        nc.vector.tensor_tensor(qk[:, s], psQK[:, s], bias_sb[:, 0:2 * C], ALU.add).then_inc(qk_biased, 1)
                        nc.vector.tensor_tensor(V1[:, heads, tb, :], psV[:, s, 0:C].rearrange("p (h d) -> p h d", h=H1),
                                                bias_sb[:, 2 * C:].rearrange("p (h d) -> p h d", h=H1), ALU.add).then_inc(proj_read, 1)
                        dve.wait_ge(qk_biased, 1 + s)
                        nc.vector.tensor_tensor(qk_cos[:, s].rearrange("p (h d) -> p h d", d=HD),
                                                qk[:, s].rearrange("p (h d) -> p h d", d=HD),
                                                cos_sb[:, tb, :].unsqueeze(1).to_broadcast([P, 4 * H1, HD]),
                                                ALU.mult).then_inc(cos_done, 1)
                        dve.wait_ge(sin_done, 1 + s)
                        for dst, a in ((QO, 0), (K1, C)):
                            last = nc.vector.tensor_tensor(dst[:, heads, tb, :],
                                                           qk_cos[:, s, a:a + C].rearrange("p (h d) -> p h d", h=H1),
                                                           qk_sin[:, s, a:a + C].rearrange("p (h d) -> p h d", h=H1), ALU.add)
                        last.then_inc(rope_done, 1)
                    for used in (proj_done, qk_biased, sin_done):
                        dve.sem_inc(used, -2)

        @block.gpsimd
        def _(pool):
            nc.gpsimd.memset(minus_half[:], -0.5).then_inc(half_made, 1)
            pool.wait_ge(half_made, 1)
            for c in range(LOADS):
                pool.wait_ge(mv_made, (c + 1) * CH)
                chunk = slice(c * CH, (c + 1) * CH)
                nc.gpsimd.tensor_scalar(var_eps[:, chunk], mv[:, chunk, 1], EPS, None, ALU.add).then_inc(var_made, 1)
                pool.wait_ge(var_made, c + 1)
                nc.gpsimd.tensor_tensor(out=rstd[:, chunk], in0=var_eps[:, chunk], in1=minus_half[:, chunk], op=ALU.pow).then_inc(rstd_made, 1)
            pool.sem_inc(rope_done, 2)
            pool.wait_ge(sin_loaded, 16)
            for b in range(B):
                with pool.Fori(0, TB // 2) as g:
                    for s in range(2):
                        pool.wait_ge(cos_done, 1 + s)
                        pool.wait_ge(rope_done, 1 + s)
                        v = qk[:, s].rearrange("p (h s d) -> p h s d", s=2, d=HD)
                        o = qk_sin[:, s].rearrange("p (h s d) -> p h s d", s=2, d=HD)
                        for half in range(2):
                            sn = sin_sb[:, 2 * g + s, half, :].unsqueeze(1).to_broadcast([P, 2 * H1, HD])
                            last = nc.gpsimd.tensor_tensor(out=o[:, :, half], in0=v[:, :, 1 - half], in1=sn, op=ALU.mult)
                        last.then_inc(sin_done, 1)
                    pool.sem_inc(cos_done, -2)
                    pool.sem_inc(rope_done, -2)

        @block.tensor
        def _(pe):
            pe.wait_ge(ident_made, 3)
            pe.wait_ge(weights_loaded, 16)
            pe.sem_inc(proj_read, 2)
            for b in range(B):
                with pe.Fori(0, TB // 2) as g:
                    for s in range(2):
                        pe.wait_ge(xn_made, 1 + s)
                        for k in range(NC):
                            last = nc.tensor.transpose(psT[:, s, k * P:(k + 1) * P], xn[:, s, k * P:(k + 1) * P], ident[:])
                        last.then_inc(xnT_in_psum, 1)
                    for s in range(2):
                        pe.wait_ge(xnT_copied, 1 + s)
                        pe.wait_ge(proj_read, 1 + s)
                        for k in range(NC):
                            nc.tensor.matmul(psQK[:, s], xnT[:, s, k * P:(k + 1) * P], w_sb[:, k, 0:2 * C], start=(k == 0), stop=(k == NC - 1))
                        for k in range(NC):
                            last = nc.tensor.matmul(psV[:, s, 0:C], xnT[:, s, k * P:(k + 1) * P], w_sb[:, k, 2 * C:], start=(k == 0), stop=(k == NC - 1))
                        last.then_inc(proj_done, 1)
                    pe.sem_inc(xn_made, -2)
                    pe.sem_inc(xnT_copied, -2)
                    pe.sem_inc(proj_read, -2)

        @block.scalar
        def _(act):
            act.dma_start(w_sb[:], ins["wqkv1"].rearrange("(k p) n -> p k n", p=P)).then_inc(weights_loaded, 16)
            act.dma_start(bias_sb[:], ins["bqkv1"].partition_broadcast(P)).then_inc(tables_loaded, 16)
            act.dma_start(cos_sb[:], ins["cos1"].rearrange("(t p) d -> p t d", p=P)).then_inc(tables_loaded, 16)
            act.dma_start(sin_sb[:], ins["sin1"].rearrange("(t p) (s d) -> p t s d", p=P, s=2)).then_inc(sin_loaded, 16)
            for c in range(LOADS):
                act.wait_ge(nmr_made, c + 1)
                with act.Fori(0, CH // 2) as g:
                    for s in range(2):
                        i = c * CH + 2 * g + s
                        nc.scalar.activation(xn[:, s], x_sb[:, i, :], ACT.Identity, bias=nmr[:, bass.ds(i, 1)], scale=rstd[:, bass.ds(i, 1)]).then_inc(xn_made, 1)
                    for s in range(2):
                        act.wait_ge(xnT_in_psum, 1 + s)
                        nc.scalar.copy(xnT[:, s], psT[:, s, 0:C]).then_inc(xnT_copied, 1)
                    act.sem_inc(xnT_in_psum, -2)


SLOTS = 6
STACK = SLOTS * D1
SPLIT_Q = (slice(0, 3), slice(3, 6, 2), slice(4, 5))
SPLIT_K = (slice(2, 5), slice(1, 6, 4), slice(0, 1))
AUX = 3
PROBS = 4
W2 = 1024
BODY = 3
VW = 32


def attention_phase(nc, QO, K1, V1, ident, identb):
    with ExitStack() as ctx:
        sb = lambda n, s, d=F32: ctx.enter_context(nc.sbuf_tensor(n, s, d))
        ps = lambda n, s, d=F32: ctx.enter_context(nc.psum_tensor(n, s, d))
        sem = nc.alloc_semaphore
        q_parts = sb("q_parts", [P, TB, P], BF16)
        k_parts = sb("k_parts", [P, TB, P], BF16)
        m_parts = sb("m_parts", [P, TB, 32], BF16)
        rest1 = sb("rest1", [P, 2, TB, D1])
        rest2 = sb("rest2", [P, 2, TB, D1])
        m_rest = sb("m_rest", [P, 2, TB])
        q_stack = sb("q_stack", [P, BODY, T], BF16)
        k_stack = sb("k_stack", [P, BODY, T], BF16)
        v_ones = sb("v_ones", [P, BODY, TB, VW])
        probs = sb("probs", [P, PROBS, W2])
        mx4 = sb("mx4", [P, BODY, TB, 4])
        negmax = sb("negmax", [P, BODY, TB])
        o_stage = sb("o_stage", [P, 512])
        rsum = sb("rsum", [P, BODY, TB])
        scores = ps("scores", [P, 4, 512])
        aux = ps("aux", [P, AUX, 512])
        pv = ps("pv", [P, 512])

        parts_made, parts_read = sem("parts_made"), sem("parts_read")
        consts_made, split_step = sem("consts_made"), sem("split_step")
        scores_ready, probs_ready = sem("scores_ready"), sem("probs_ready")
        pv_done, pv_copied, v_made = sem("pv_done"), sem("pv_copied"), sem("v_made")
        max_in_psum, max_taken = sem("max_in_psum"), sem("max_taken")
        head_max, m_parts_made = sem("head_max"), sem("m_parts_made")
        stack_in_psum, stack_copied = sem("stack_in_psum"), sem("stack_copied")
        rsum_made, maxima_written = sem("rsum_made"), sem("maxima_written")

        block = ctx.enter_context(nc.Block())

        K_STEPS, Q_STEPS, M_STEPS, O_STEP = (8, 9), (10, 11), (TB - 2, TB - 1), 2
        LEAD = 3
        DVE_ITEMS, ACT_ITEMS = 4 * TB + 1, 6

        def steps():
            return [(0, s) for s in range(LEAD, TB)] + [(1, s) for s in range(LEAD)]

        def ahead(d, s):
            return (d + 1, s + LEAD) if s < TB - LEAD else (d + 2, s + LEAD - TB)

        def aux_items(left):
            items = []
            for d, s in steps():
                a, tile = ahead(d, s)
                if d == 0 and left == 2 and s in K_STEPS + Q_STEPS:
                    items.append((d, s, "stack", (K_STEPS + Q_STEPS).index(s)))
                if d == 0 and left >= 1 and s in M_STEPS:
                    items.append((d, s, "maxrow", M_STEPS.index(s)))
                if left >= a:
                    items += [(d, s, "max", (a, tile, q)) for q in range(4)]
                if d == 1 and s == O_STEP:
                    items.append((d, s, "out", None))
            return items

        PROLOGUE_ITEMS = 4 + 4 * TB + 4 + 2 + 4 * 2 * LEAD

        def banks(r, left):
            first = PROLOGUE_ITEMS + (r * len(aux_items(2)) if left == 2 else len(aux_items(1)) if left == 0 else 0)
            return [(first + i) % AUX for i in range(len(aux_items(left)))]

        assert len(aux_items(2)) == DVE_ITEMS + ACT_ITEMS and BODY * len(aux_items(2)) % AUX == 0

        def all_heads(eng, head, per_head):
            with eng.Fori(0, (NH - 2) // BODY) as m:
                for r in range(BODY):
                    head(r, m * BODY + r, 2)
                for semaphore, rises in per_head:
                    eng.sem_inc(semaphore, -BODY * rises)
            head(0, NH - 2, 1)
            head(1, NH - 1, 0)

        @block.gpsimd
        def _(pool):
            for t in (q_parts, k_parts, m_parts, v_ones):
                nc.gpsimd.memset(t[:], 0.0).then_inc(consts_made, 1)
            pool.wait_ge(consts_made, 4)
            nc.gpsimd.memset(k_parts[:, :, STACK:STACK + 3], 1.0).then_inc(consts_made, 1)
            nc.gpsimd.memset(v_ones[:, :, :, D1:D1 + 1], 1.0).then_inc(consts_made, 1)
            pool.wait_ge(consts_made, 6)

            def chain(instruction):
                instruction.then_inc(split_step, 1)
                pool.wait_ge(split_step, 1)
                pool.sem_inc(split_step, -1)

            def split_qk(r, n):
                if r:
                    pool.wait_ge(parts_read, r)
                for j, (src, parts, (hi, mid, lo)) in enumerate(((QO, q_parts, SPLIT_Q), (K1, k_parts, SPLIT_K))):
                    slots = parts[:].rearrange("p t (s d) -> p t s d", d=D1)
                    x = src[:, n]
                    chain(nc.gpsimd.tensor_copy(slots[:, :, hi, :], x.unsqueeze(2).to_broadcast([P, TB, 3, D1])))
                    chain(nc.gpsimd.tensor_tensor(out=rest1[:, j], in0=x, in1=slots[:, :, hi.start, :], op=ALU.subtract))
                    chain(nc.gpsimd.tensor_copy(slots[:, :, mid, :], rest1[:, j].unsqueeze(2).to_broadcast([P, TB, 2, D1])))
                    chain(nc.gpsimd.tensor_tensor(out=rest2[:, j], in0=rest1[:, j], in1=slots[:, :, mid.start, :], op=ALU.subtract))
                    nc.gpsimd.tensor_copy(slots[:, :, lo.start, :], rest2[:, j]).then_inc(parts_made, 1)

            def split_max_and_v(r, slot, n):
                pool.wait_ge(head_max, r + 1)
                x = negmax[:, slot]
                chain(nc.gpsimd.tensor_copy(m_parts[:, :, 0], x))
                chain(nc.gpsimd.tensor_tensor(out=m_rest[:, 0], in0=x, in1=m_parts[:, :, 0], op=ALU.subtract))
                chain(nc.gpsimd.tensor_copy(m_parts[:, :, 1], m_rest[:, 0]))
                chain(nc.gpsimd.tensor_tensor(out=m_rest[:, 1], in0=m_rest[:, 0], in1=m_parts[:, :, 1], op=ALU.subtract))
                nc.gpsimd.tensor_copy(m_parts[:, :, 2], m_rest[:, 1]).then_inc(m_parts_made, 1)
                nc.gpsimd.tensor_copy(v_ones[:, slot, :, 0:D1], V1[:, n]).then_inc(v_made, 1)

            def head(r, n, left):
                if left > 1:
                    split_qk(r + 2, n + 2)
                if left > 0:
                    split_max_and_v(r + 1, (r + 1) % BODY, n + 1)

            split_qk(0, 0)
            split_qk(1, 1)
            split_max_and_v(0, 0, 0)
            all_heads(pool, head, ((parts_read, 1), (head_max, 1)))

        @block.tensor
        def _(pe):
            ring = dict(item=0, dve=0, act=0, last=[])

            def ring_bank():
                if len(ring["last"]) == AUX:
                    pe.wait_ge(*ring["last"].pop(0))
                ring["item"] += 1
                return (ring["item"] - 1) % AUX

            def for_dve():
                ring["dve"] += 1
                ring["last"].append((max_taken, ring["dve"]))

            def for_act():
                ring["act"] += 1
                ring["last"].append((stack_copied, ring["act"]))

            def stack_item(parts, rows, row0, half):
                bank = ring_bank()
                dst = aux[row0:row0 + rows, bank].bitcast(BF16).rearrange("k (t c) -> k t c", c=P)
                for t in range(8):
                    last = nc.tensor.transpose(dst[:, t], parts[:, half * 8 + t, 0:rows], identb[:])
                last.then_inc(stack_in_psum, 1)
                for_act()

            def stack_items(r, halves=(0, 1, 2, 3)):
                for h in halves:
                    if h % 2 == 0:
                        pe.wait_ge(parts_made, 2 * r + 2)
                    stack_item(k_parts if h < 2 else q_parts, P if h < 2 else STACK, 0, h % 2)

            def max_item(r, half):
                pe.wait_ge(m_parts_made, r + 1)
                stack_item(m_parts, 32, STACK, half)

            def score_for_max(r, t, quarters, first_half_signals=None):
                if t == 0:
                    pe.wait_ge(stack_copied, ring["act"])
                for q in quarters:
                    bank = ring_bank()
                    lhsT = q_stack[0:STACK, r % BODY, t * P:(t + 1) * P]
                    if first_half_signals is not None and q == 0:
                        nc.tensor.matmul(aux[:, bank, 0:256], lhsT, k_stack[0:STACK, r % BODY, 0:256],
                                         start=True, stop=True).then_inc(first_half_signals, 1)
                        nc.tensor.matmul(aux[:, bank, 256:512], lhsT, k_stack[0:STACK, r % BODY, 256:512],
                                         start=True, stop=True).then_inc(max_in_psum, 1)
                    else:
                        nc.tensor.matmul(aux[:, bank], lhsT, k_stack[0:STACK, r % BODY, q * 512:(q + 1) * 512],
                                         start=True, stop=True).then_inc(max_in_psum, 1)
                    for_dve()

            def score(r, s, h, signal=None):
                unit = 2 * TB * r + 2 * s + h
                if unit >= 2:
                    pe.wait_ge(probs_ready, unit - 1)
                if s == 0:
                    pe.wait_ge(stack_copied, ring["act"])
                for j in range(2):
                    last = nc.tensor.matmul(scores[:, 2 * h + j], k_stack[:, r % BODY, s * P:(s + 1) * P],
                                            q_stack[:, r % BODY, (2 * h + j) * 512:(2 * h + j + 1) * 512], start=True, stop=True)
                    if j == 0 and signal is not None:
                        last.then_inc(signal, 1)
                last.then_inc(scores_ready, 1)

            def weigh(r, s):
                if s == 0:
                    pe.wait_ge(v_made, r + 1)
                    if r:
                        pe.wait_ge(pv_copied, r)
                pe.wait_ge(probs_ready, 2 * TB * r + 2 * s + 2)
                for j in range(4):
                    last = nc.tensor.matmul(pv[VW * j:VW * (j + 1), :], v_ones[:, r % BODY, s, :],
                                            probs[:, (2 * s + j // 2) % PROBS, (j % 2) * 512:(j % 2 + 1) * 512],
                                            start=(s == 0), stop=(s == TB - 1), tile_position=(0, VW * j))
                last.then_inc(pv_done, 1)

            def output_item(r):
                pe.wait_ge(pv_copied, r + 1)
                bank = ring_bank()
                for c in range(4):
                    last = nc.tensor.transpose(aux[:, bank, c * P:(c + 1) * P], o_stage[:, c * P:(c + 1) * P], ident[:])
                last.then_inc(max_in_psum, 1)
                for_dve()

            def step(r, d, s, left):
                ahead_d, tile = ahead(d, s)
                scored, maxima = left >= d, left >= ahead_d
                here = r + d
                if d == 0 and left == 2 and s in K_STEPS + Q_STEPS:
                    stack_items(r + 2, [(K_STEPS + Q_STEPS).index(s)])
                if d == 0 and left >= 1 and s in M_STEPS:
                    max_item(r + 1, M_STEPS.index(s))
                if scored:
                    score(here, s, 0)
                if maxima:
                    score_for_max(r + ahead_d, tile, (0, 1))
                if scored:
                    score(here, s, 1, parts_read if d == 0 and left == 2 and s == Q_STEPS[1] else None)
                if maxima:
                    score_for_max(r + ahead_d, tile, (2, 3))
                if s == 0:
                    weigh(here - 1, TB - 1)
                elif scored:
                    weigh(here, s - 1)
                if d == 1 and s == O_STEP:
                    output_item(r)

            def head(r, n, left):
                if r == 0:
                    ring.update(start, last=list(start["last"]))
                assert ring["item"] % AUX == banks(r, left)[0]
                for d, s in steps():
                    step(r, d, s, left)

            stack_items(0)
            for t in range(TB):
                score_for_max(0, t, range(4), parts_read if t == 0 else None)
            stack_items(1)
            max_item(0, 0)
            max_item(0, 1)
            for t in range(LEAD):
                score_for_max(1, t, range(4))
            for s in range(LEAD):
                score(0, s, 0)
                score_for_max(1, s + LEAD, (0, 1))
                score(0, s, 1, parts_read if s == 0 else None)
                score_for_max(1, s + LEAD, (2, 3))
                if s:
                    weigh(0, s - 1)
            start = dict(ring, last=list(ring["last"]))
            all_heads(pe, head, ((parts_made, 2), (m_parts_made, 1), (v_made, 1), (pv_copied, 1), (probs_ready, 2 * TB),
                                 (max_taken, DVE_ITEMS), (stack_copied, ACT_ITEMS)))

        @block.scalar
        def _(act):
            copied = [0]

            def copy_stack_item(dst, bank, rows, row0):
                copied[0] += 1
                act.wait_ge(stack_in_psum, copied[0])
                nc.scalar.copy(dst, aux[row0:row0 + rows, bank].bitcast(BF16)).then_inc(stack_copied, 1)

            def copy_stack(slot, part, bank):
                stack, rows = (k_stack, P) if part < 2 else (q_stack, STACK)
                copy_stack_item(stack[0:rows, slot, part % 2 * W2:(part % 2 + 1) * W2], bank, rows, 0)

            def copy_maxima(slot, half, bank):
                copy_stack_item(q_stack[STACK:P, slot, half * W2:(half + 1) * W2], bank, P - STACK, STACK)

            def exponentiate(r, s, h):
                unit = 2 * TB * r + 2 * s + h
                act.wait_ge(scores_ready, unit + 1)
                if TB * r + s >= 2:
                    act.wait_ge(pv_done, TB * r + s - 1)
                nc.scalar.activation(probs[:, unit % PROBS], scores[:, 2 * h:2 * h + 2].rearrange("p a n -> p (a n)"),
                                     ACT.Exp, scale=float(D1) ** -0.5).then_inc(probs_ready, 1)

            def head(r, n, left):
                if r == 0:
                    copied[0] = start
                items, bank_of = aux_items(left), banks(r, left)
                for d, s in steps():
                    here = [(kind, what, bank) for (di, si, kind, what), bank in zip(items, bank_of) if (di, si) == (d, s)]
                    for kind, what, bank in here:
                        if kind == "stack":
                            copy_stack((r + 2) % BODY, what, bank)
                        if kind == "maxrow":
                            copy_maxima((r + 1) % BODY, what, bank)
                    if left >= d:
                        exponentiate(r + d, s, 0)
                        exponentiate(r + d, s, 1)
                    if (d, s) == (1, 0):
                        act.wait_ge(pv_done, TB * (r + 1))
                        nc.scalar.copy(o_stage[:], pv[:]).then_inc(pv_copied, 1)

            for part in range(4):
                copy_stack(0, part, part % AUX)
            after = 4 + 4 * TB
            for part in range(4):
                copy_stack(1, part, (after + part) % AUX)
            for half in range(2):
                copy_maxima(0, half, (after + 4 + half) % AUX)
            for s in range(LEAD):
                exponentiate(0, s, 0)
                exponentiate(0, s, 1)
            start = copied[0]
            all_heads(act, head, ((stack_in_psum, ACT_ITEMS), (scores_ready, 2 * TB), (pv_done, TB)))

        @block.vector
        def _(dve):
            taken = [0]

            def next_item():
                taken[0] += 1
                dve.wait_ge(max_in_psum, taken[0])

            def take_max(slot, tile, quarter, bank):
                next_item()
                nc.vector.reduce_max(mx4[:, slot, tile, quarter:quarter + 1], aux[:, bank], AX.X).then_inc(max_taken, 1)
                if (tile, quarter) == (TB - 1, 3):
                    dve.drain().then_inc(maxima_written, 1)
                    dve.wait_ge(maxima_written, 1)
                    dve.sem_inc(maxima_written, -1)
                    nc.vector.tensor_reduce(negmax[:, slot], mx4[:, slot], AX.X, ALU.max, negate=True).then_inc(head_max, 1)

            def write_output(r, n, bank):
                next_item()
                item = aux[:, bank].rearrange("p (c j d) -> p c j d", c=4, j=4)
                nc.vector.reciprocal(rsum[:, r].rearrange("p (c j) -> p c j", c=4), item[:, :, :, D1]).then_inc(rsum_made, 1)
                dve.wait_ge(rsum_made, 1)
                dve.sem_inc(rsum_made, -1)
                nc.vector.tensor_tensor(QO[:, n].rearrange("p (j c) d -> p c j d", j=4), item[:, :, :, 0:D1],
                                        rsum[:, r].rearrange("p (c j) -> p c j", c=4).unsqueeze(3).to_broadcast([P, 4, 4, D1]),
                                        ALU.mult).then_inc(max_taken, 1)

            def head(r, n, left):
                if r == 0:
                    taken[0] = start
                for (d, s, kind, what), bank in zip(aux_items(left), banks(r, left)):
                    if kind == "max":
                        take_max((r + what[0]) % BODY, what[1], what[2], bank)
                    if kind == "out":
                        write_output(r, n, bank)

            at = 4
            for t in range(TB):
                for q in range(4):
                    take_max(0, t, q, (at + 4 * t + q) % AUX)
            at += 4 * TB + 6
            for t in range(2 * LEAD):
                for q in range(4):
                    take_max(1, t, q, (at + 4 * t + q) % AUX)
            start = taken[0]
            all_heads(dve, head, ((max_in_psum, DVE_ITEMS),))


def output_phase(nc, ins, x_sb, QO, Y, ident, x1_dram):
    with ExitStack() as ctx:
        sb = lambda n, s, d=F32: ctx.enter_context(nc.sbuf_tensor(n, s, d))
        ps = lambda n, s, d=F32: ctx.enter_context(nc.psum_tensor(n, s, d))
        sem = nc.alloc_semaphore
        w_sb = sb("wo1_sb", [P, NC, C])
        bias_sb = sb("bo1_sb", [P, C])
        o_tile = sb("o_tile", [P, 2, C])
        oT = sb("oT2", [P, 2, C])
        stats = sb("stats2", [P, 2, NT, 6])
        mv = sb("mv2", [P, 2, NT, 2])
        var_eps = sb("var_eps2", [P, 2, NT])
        minus_half = sb("minus_half2", [P, NT])
        rstd = sb("rstd2", [P, 2, NT])
        nmr = sb("nmr2", [P, 2, NT])
        psT = ps("psT2", [P, 2, 512])
        psY = ps("psY2", [P, 2, 512])
        weights_loaded, bias_loaded = sem("wo1_loaded"), sem("bo1_loaded")
        o_made, o_read, oT_in_psum, oT_copied = sem("o2_made"), sem("o2_read"), sem("oT2_in_psum"), sem("oT2_copied")
        y_done, y_read, y_written, stats_made = sem("y2_done"), sem("y2_read"), sem("y2_written"), sem("stats2_made")
        half_made, mv_made, var_made, rstd_made, nmr_made = (sem(x) for x in ("half2_made", "mv2_made", "var2_made", "rstd2_made", "nmr2_made"))
        y_normed, x1_stored, xf_done = sem("y2_normed"), sem("x1_stored"), sem("xf_done")

        block = ctx.enter_context(nc.Block())

        @block.sync
        def _(sp):
            sp.dma_start(w_sb[:], ins["wo1"].rearrange("(k p) n -> p k n", p=P)).then_inc(weights_loaded, 16)
            sp.dma_start(bias_sb[:], ins["bo1"].partition_broadcast(P)).then_inc(bias_loaded, 16)
            sp.wait_ge(stats_made, 2)
            sp.dma_start(x1_dram, Y[:]).then_inc(x1_stored, 16)
            sp.wait_ge(x1_stored, 16)

        @block.gpsimd
        def _(pool):
            nc.gpsimd.memset(minus_half[:], -0.5).then_inc(half_made, 1)
            pool.sem_inc(o_read, 2)
            for b in range(B):
                with pool.Fori(0, TB // 2) as g:
                    for s in range(2):
                        pool.wait_ge(o_read, 1 + s)
                        nc.gpsimd.tensor_copy(o_tile[:, s].rearrange("p (h d) -> p h d", d=D1),
                                              QO[:, b * H1:(b + 1) * H1, 2 * g + s, :]).then_inc(o_made, 1)
                    pool.sem_inc(o_read, -2)
            pool.wait_ge(half_made, 1)
            for j in range(2):
                pool.wait_ge(mv_made, (j + 1) * NT)
                nc.gpsimd.tensor_scalar(var_eps[:, j], mv[:, j, :, 1], EPS, None, ALU.add).then_inc(var_made, 1)
                pool.wait_ge(var_made, j + 1)
                nc.gpsimd.tensor_tensor(out=rstd[:, j], in0=var_eps[:, j], in1=minus_half[:], op=ALU.pow).then_inc(rstd_made, 1)

        @block.tensor
        def _(pe):
            pe.wait_ge(weights_loaded, 16)
            pe.sem_inc(y_read, 2)
            with pe.Fori(0, NT // 2):
                for s in range(2):
                    pe.wait_ge(o_made, 1 + s)
                    for k in range(NC):
                        last = nc.tensor.transpose(psT[:, s, k * P:(k + 1) * P], o_tile[:, s, k * P:(k + 1) * P], ident[:])
                    last.then_inc(oT_in_psum, 1)
                for s in range(2):
                    pe.wait_ge(oT_copied, 1 + s)
                    pe.wait_ge(y_read, 1 + s)
                    nc.tensor.matmul(psY[:, s, 0:C], oT[:, s, 0:P], w_sb[:, 0], start=True, stop=False).then_inc(o_read, 1)
                    nc.tensor.matmul(psY[:, s, 0:C], oT[:, s, P:C], w_sb[:, 1], start=False, stop=True).then_inc(y_done, 1)
                for used in (o_made, oT_copied, y_read):
                    pe.sem_inc(used, -2)

        def rows_normed(act, j, i, dst, ready):
            nc.scalar.activation(dst[:, i, :], Y[:, i, :], ACT.Identity, bias=nmr[:, j, bass.ds(i, 1)],
                                 scale=rstd[:, j, bass.ds(i, 1)]).then_inc(ready, 1)

        @block.scalar
        def _(act):
            with act.Fori(0, NT // 2):
                for s in range(2):
                    act.wait_ge(oT_in_psum, 1 + s)
                    nc.scalar.copy(oT[:, s], psT[:, s, 0:C]).then_inc(oT_copied, 1)
                act.sem_inc(oT_in_psum, -2)
            act.wait_ge(nmr_made, 1)
            with act.Fori(0, NT) as i:
                rows_normed(act, 0, i, Y, y_normed)
            act.wait_ge(nmr_made, 2)
            with act.Fori(0, NT) as i:
                rows_normed(act, 1, i, x_sb, xf_done)

        @block.vector
        def _(dve):
            def all_stats(j):
                dve.drain().then_inc(stats_made, 1)
                dve.wait_ge(stats_made, j + 1)
                for i in range(NT):
                    nc.vector.bn_aggr(mv[:, j, i, :], stats[:, j, i, :]).then_inc(mv_made, 1)
                dve.wait_ge(rstd_made, j + 1)
                nc.vector.scalar_tensor_tensor(nmr[:, j], mv[:, j, :, 0], -1.0, rstd[:, j], ALU.mult, ALU.mult).then_inc(nmr_made, 1)

            dve.wait_ge(bias_loaded, 16)
            with dve.Fori(0, NT // 2) as g:
                for s in range(2):
                    i = 2 * g + s
                    dve.wait_ge(y_done, 1 + s)
                    nc.vector.tensor_tensor(Y[:, i, :], psY[:, s, 0:C], bias_sb[:], ALU.add).then_inc(y_written, 1)
                    dve.wait_ge(y_written, 1 + s)
                    nc.vector.bn_stats(stats[:, 0, i, :], Y[:, i, :]).then_inc(y_read, 1)
                dve.sem_inc(y_done, -2)
                dve.sem_inc(y_written, -2)
            all_stats(0)
            with dve.Fori(0, NT) as i:
                dve.wait_ge(y_normed, 1)
                nc.vector.tensor_tensor(Y[:, i, :], Y[:, i, :], x_sb[:, i, :], ALU.add).then_inc(y_written, 1)
                dve.wait_ge(y_written, 1)
                nc.vector.bn_stats(stats[:, 1, i, :], Y[:, i, :])
                dve.sem_inc(y_normed, -1)
                dve.sem_inc(y_written, -1)
            all_stats(1)


LAYERS = 2
H2, D2 = 8, 64
INNER = H2 * D2
HID = 682
HC = -(-HID // P)
NO_KEY = -1e30
PAIRS = ((0, 2), (4, 6), (1, 3), (5, 7))
PLACE = {h: (j, u) for j, pair in enumerate(PAIRS) for u, h in enumerate(pair)}
BANKS = 8
UNROLL = 4
ITEMS = ([("xT", 2, "act", 0), ("qT", 1, "act", 1), ("kT", 1, "act", 2), ("shift", -1, "dve", 3)]
         + [(f"PT{j}", 0, "act" if j % 2 == 0 else "dve", 4 + j) for j in range(4)]
         + [("q", 2, "act", 0), ("k", 2, "act", 1), ("v", 2, "act", 2), ("hT", -1, "act", 3), ("oT", 0, "act", 0)]
         + [(f"H{j}", -1, "act", 1 + j) for j in range(3)]
         + [(f"S{j}", 1, "dve", 4 + j) for j in range(4)]
         + [("Y", 0, "dve", 2), ("F", -1, "dve", 3)])
TILE_OF = {name: d for name, d, _, _ in ITEMS}
READY_FOR = {name: r for name, _, r, _ in ITEMS}
BANK_OF = {name: b for name, _, _, b in ITEMS}
FREES = {"act": ["xT", "qT", "kT", "PT0", "PT2", "hT", "oT", "v"],
         "dve": ["PT1", "PT3", "shift", "q", "k", "H0", "H1", "H2", "S0", "S1", "Y", "S2", "S3", "F"]}
FREED_BY = {name: r for r, names in FREES.items() for name in names}
SEGMENTS = ((-2, 5, 0), (3, UNROLL, 6), (27, 8, 0), (35, UNROLL, 6), (59, 6, 0))


class Step:

    def __init__(self, t, skipped, turn):
        self.t, self.skipped, self.turn = t, skipped, turn

    def exists(self, d):
        return 0 <= self.t + self.skipped + d < LAYERS * NT

    def layer(self, d):
        return (self.t + self.skipped + d) // NT

    def first(self, d):
        return self.turn is None and (self.t + self.skipped + d) % NT < 2

    def position(self, d):
        v = (self.t + self.skipped + d) % NT // 2
        return v if self.turn is None else v + UNROLL // 2 * self.turn

    def tile(self, d):
        return (self.t + self.skipped + d) % 2 * TB + self.position(d)

    def slot(self, d, n=4):
        return (self.t + d) % n


def item_counts():
    ready, freed, n = {}, {}, {"ready": {"act": 0, "dve": 0}, "freed": {"act": 0, "dve": 0}}
    t, skipped = SEGMENTS[0][0], 0
    for first, steps, turns in SEGMENTS:
        for _ in range(steps):
            step = Step(t, skipped, None)
            for name, d, reader, _ in ITEMS:
                if step.exists(d):
                    n["ready"][reader] += 1
                    ready[name, t + d] = n["ready"][reader]
            for reader, names in FREES.items():
                for name in names:
                    if step.exists(TILE_OF[name]):
                        n["freed"][reader] += 1
                        freed[name, t + TILE_OF[name]] = n["freed"][reader]
            t += 1
        skipped += (turns - 1) * steps if turns else 0
    return ready, freed


class Waiter:

    def __init__(self, eng):
        self.eng, self.sems, self.fallen = eng, {}, {}

    def on(self, sem, per_step):
        self.sems[sem.name] = (sem, per_step)
        self.fallen[sem.name] = 0
        return sem

    def upto(self, sem, count):
        self.eng.wait_ge(sem, count - self.fallen[sem.name])

    def fall(self):
        for sem, per_step in self.sems.values():
            self.eng.sem_inc(sem, -UNROLL * per_step)
            self.fallen[sem.name] += UNROLL * per_step


def walk(waiter):
    t, skipped = SEGMENTS[0][0], 0
    for first, steps, turns in SEGMENTS:
        assert first == t + skipped
        if turns:
            with waiter.eng.Fori(0, turns) as turn:
                for _ in range(steps):
                    yield Step(t, skipped, turn)
                    t += 1
                waiter.fall()
            skipped += (turns - 1) * steps
        else:
            for _ in range(steps):
                yield Step(t, skipped, None)
                t += 1


def feed_forward_phase(nc, ins, x_sb, ident, identb):
    with ExitStack() as ctx:
        sb = lambda n, s, d=F32: ctx.enter_context(nc.sbuf_tensor(n, s, d))
        sem = nc.alloc_semaphore
        wqkv_sb = sb("wqkv2_sb", [P, LAYERS, NC, 3 * INNER])
        wo_sb = sb("wo2_sb", [P, LAYERS, INNER // P, C])
        w1_sb = sb("w1_sb", [P, LAYERS, NC, 2 * HC * P])
        w2_sb = sb("w2_sb", [P, LAYERS, HC, C])
        qks_sb = sb("qk_scale_sb", [P, LAYERS, 2, D2])
        cos_sb = sb("cos2_sb", [P, TB, 2, D2])
        sin_sb = sb("sin2_sb", [P, TB, 2, D2])
        lng_sb = sb("ln_g_sb", [P, LAYERS, NC])
        lnb_sb = sb("ln_b_sb", [P, LAYERS, NC])
        b1_sb = sb("b1_sb", [P, LAYERS, 2 * HC])
        b2_sb = sb("b2_sb", [P, LAYERS, C])
        mask_sb = sb("mask_sb", [P, 2, 2 * P], BF16)
        shift_sb = sb("shift_sb", [P, 2, P])
        b1_dve = sb("b1_dve", [P, LAYERS, 2 * HC])
        qks8 = sb("qk_scale8_sb", [P, LAYERS, 2, D2])
        zero_col = sb("zero_col", [P, 1])
        minus_half = sb("minus_half3", [P, 2 * H2])
        x_stage = sb("x_stage", [P, 4, C])
        xT = sb("xT3", [P, 4, 2 * P + 1])
        squares = sb("squares", [P, 2, INNER])
        qk = sb("qk3", [P, 2, INNER])
        qk_cos = sb("qk_cos3", [P, 2, INNER])
        qk_sin = sb("qk_sin3", [P, 2, INNER])
        qk_rot = sb("qk_rot3", [P, 2, INNER])
        norm2 = sb("norm2", [P, 2 * H2])
        norm2_min = sb("norm2_min", [P, 2 * H2])
        rnorm = sb("rnorm", [P, 2 * H2])
        qT = sb("qT3", [P, 4, P])
        kT = sb("kT3", [P, 4, 4, P])
        v_sb = sb("v3", [P, 4, INNER])
        probs = sb("probs3", [P, 4, 2, 2 * P])
        negmax = sb("negmax3", [P, 4, 2])
        sums = sb("sums3", [P, 4, 2])
        rsums = sb("rsums3", [P, 4, 2])
        PT = sb("PT3", [P, 4, 2, 2, P])
        oT = sb("oT3", [P, 4, P])
        x_mid = sb("x_mid", [P, 4, C])
        x_b2 = sb("x_b2", [P, C])
        stats = sb("stats3", [P, 2, 6])
        mv = sb("mv3", [P, 2])
        var_eps = sb("var_eps3", [P, 1])
        rstd = sb("rstd3", [P, 1])
        hn = sb("hn3", [P, C])
        hT = sb("hT3", [P, NC, P])
        gate = sb("gate3", [P, HC, P])
        act_T = sb("act_T3", [P, HC, P])
        ps = [ctx.enter_context(nc.psum_tensor(f"bank{b}", [P, 512], F32)) for b in range(BANKS)]
        bank = lambda name: ps[BANK_OF[name]]

        for_act, for_dve = sem("items_for_act"), sem("items_for_dve")
        by_act, by_dve = sem("read_by_act"), sem("read_by_dve")
        ready_sem, freed_sem = {"act": for_act, "dve": for_dve}, {"act": by_act, "dve": by_dve}
        loaded_pe, loaded_act, loaded_dve, loaded_pool = (sem(f"loaded3_{x}") for x in ("pe", "act", "dve", "pool"))
        mask_made, shift_made, zero_made, half_made, qscale_made = (sem(f"{x}3_made") for x in ("mask", "shift", "zero", "half", "qscale"))
        x_staged, rotary_done = sem("x_staged"), sem("rotary_done")
        squares_made, norm2_made, sin_rnorm_made = sem("squares_made"), sem("norm2_made"), sem("sin_rnorm_made")
        cos_made, rot_made = sem("cos3_made"), sem("rot3_made")
        max_made, exps_made, rsums_made = sem("max3_made"), sem("exps3_made"), sem("rsums3_made")
        hstats_made, hmv_made, hrstd_made = sem("hstats_made"), sem("hmv_made"), sem("hrstd_made")
        gate_made, x_b2_made, norm2_floor, var_made = sem("gate_made"), sem("x_b2_made"), sem("norm2_floor_made"), sem("var3_made")
        ready, freed = item_counts()

        block = ctx.enter_context(nc.Block())

        @block.sync
        def _(sp):
            sp.dma_start(wqkv_sb[:, 0], ins["wqkv2"][0].rearrange("(k p) n -> p k n", p=P)).then_inc(loaded_pe, 16)
            sp.dma_start(cos_sb[:], ins["cos2"].rearrange("(t p) (a d) -> p t a d", p=P, a=2)).then_inc(loaded_dve, 16)
            sp.dma_start(sin_sb[:], ins["sin2"].rearrange("(t p) (a d) -> p t a d", p=P, a=2)).then_inc(loaded_pool, 16)
            for l in range(LAYERS):
                if l:
                    sp.dma_start(wqkv_sb[:, l], ins["wqkv2"][l].rearrange("(k p) n -> p k n", p=P)).then_inc(loaded_pe, 16)
                sp.dma_start(wo_sb[:, l], ins["wo2"][l].rearrange("(k p) n -> p k n", p=P)).then_inc(loaded_pe, 16)
                sp.dma_start(w1_sb[:, l], ins["w1"][l].rearrange("(k p) n -> p k n", p=P)).then_inc(loaded_pe, 16)
                sp.dma_start(w2_sb[:, l], ins["w2"][l].rearrange("(k p) n -> p k n", p=P)).then_inc(loaded_pe, 16)

        LOADS_PE = 16 * 4 * LAYERS

        @block.gpsimd
        def _(pool):
            w = Waiter(pool)
            w.on(norm2_made, 1), w.on(hmv_made, 1)
            own = [w.on(norm2_floor, 1), w.on(var_made, 1)]
            nc.gpsimd.memset(shift_sb[:], 0.0).then_inc(shift_made, 1)
            nc.gpsimd.memset(minus_half[:], -0.5).then_inc(half_made, 1)
            nc.gpsimd.memset(zero_col[:], 0.0).then_inc(zero_made, 1)
            pool.wait_ge(shift_made, 1)
            nc.gpsimd.affine_select(out=shift_sb[:, 0], in_=shift_sb[:, 0], compare_op=ALU.not_equal, fill=1.0,
                                    base=1, pattern=[[-1, P]], channel_multiplier=1).then_inc(shift_made, 1)
            nc.gpsimd.affine_select(out=shift_sb[:, 1], in_=shift_sb[:, 1], compare_op=ALU.not_equal, fill=1.0,
                                    base=-(P - 1), pattern=[[-1, P]], channel_multiplier=1).then_inc(shift_made, 1)
            nc.gpsimd.memset(mask_sb[:], 0.0).then_inc(mask_made, 1)
            pool.wait_ge(mask_made, 1)
            nc.gpsimd.affine_select(out=mask_sb[:, :, 0:P], in_=mask_sb[:, :, 0:P], compare_op=ALU.is_ge, fill=NO_KEY,
                                    base=0, pattern=[[0, 2], [1, P]], channel_multiplier=-1).then_inc(mask_made, 1)
            nc.gpsimd.affine_select(out=mask_sb[:, :, P:], in_=mask_sb[:, :, P:], compare_op=ALU.is_ge, fill=NO_KEY,
                                    base=0, pattern=[[0, 2], [-1, P]], channel_multiplier=1).then_inc(mask_made, 1)
            pool.wait_ge(half_made, 1)
            pool.wait_ge(loaded_pool, 16 * 2)
            nc.gpsimd.tensor_copy(x_stage[:, 0], x_sb[:, 0, :]).then_inc(x_staged, 1)
            for n, st in enumerate(walk(w)):
                t = st.t
                if st.exists(-1):
                    w.upto(hmv_made, t)
                    nc.gpsimd.tensor_scalar(var_eps[:], mv[:, 1:2], EPS, None, ALU.add).then_inc(var_made, 1)
                    w.upto(var_made, t)
                    nc.gpsimd.tensor_tensor(out=rstd[:], in0=var_eps[:], in1=minus_half[:, 0:1], op=ALU.pow).then_inc(hrstd_made, 1)
                    nc.gpsimd.tensor_tensor(out=x_b2[:], in0=x_mid[:, st.slot(-1)], in1=b2_sb[:, st.layer(-1)], op=ALU.add).then_inc(x_b2_made, 1)
                if st.exists(3):
                    nc.gpsimd.tensor_copy(x_stage[:, st.slot(3)], x_sb[:, st.tile(3), :]).then_inc(x_staged, 1)
                if st.exists(2):
                    w.upto(norm2_made, t + 3)
                    q4 = qk[:].rearrange("p a (h d) -> p a h d", d=D2)
                    o4 = qk_sin[:].rearrange("p a (h d) -> p a h d", d=D2)
                    for lo, hi in ((0, D2 // 2), (D2 // 2, 0)):
                        nc.gpsimd.tensor_tensor(out=o4[:, :, :, lo:lo + D2 // 2], in0=q4[:, :, :, hi:hi + D2 // 2],
                                                in1=sin_sb[:, st.position(2), :, lo:lo + D2 // 2].unsqueeze(2).to_broadcast([P, 2, H2, D2 // 2]),
                                                op=ALU.mult).then_inc(sin_rnorm_made, 1)
                    nc.gpsimd.tensor_scalar(norm2_min[:], norm2[:], 1e-24, None, ALU.max).then_inc(norm2_floor, 1)
                    w.upto(norm2_floor, t + 3)
                    nc.gpsimd.tensor_tensor(out=rnorm[:], in0=norm2_min[:], in1=minus_half[:], op=ALU.pow).then_inc(sin_rnorm_made, 1)

        @block.tensor
        def _(pe):
            w = Waiter(pe)
            w.on(by_act, len(FREES["act"])), w.on(by_dve, len(FREES["dve"]))
            w.on(x_staged, 1), w.on(rotary_done, 1)
            last_in_bank = {}
            pe.wait_ge(shift_made, 3)
            pe.wait_ge(mask_made, 3)
            pe.wait_ge(loaded_pe, LOADS_PE)

            def read(name, v):
                w.upto(freed_sem[FREED_BY[name]], freed[name, v])

            def begin(name, v):
                before = last_in_bank.get(BANK_OF[name])
                if before:
                    read(*before)
                last_in_bank[BANK_OF[name]] = (name, v)
                return bank(name)

            def end(instruction, name):
                instruction.then_inc(ready_sem[READY_FOR[name]], 1)

            for st in walk(w):
                t = st.t
                if st.exists(2):
                    w.upto(x_staged, t + 3)
                    out = begin("xT", t + 2)
                    for k in range(NC):
                        last = nc.tensor.transpose(out[:, k * P:(k + 1) * P], x_stage[:, st.slot(2), k * P:(k + 1) * P], ident[:])
                    end(last, "xT")
                if st.exists(1):
                    w.upto(rotary_done, t + 2)
                    for a, name in enumerate(("qT", "kT")):
                        out = begin(name, t + 1)
                        for c in range(4):
                            last = nc.tensor.transpose(out[:, c * P:(c + 1) * P], qk_rot[:, a, c * P:(c + 1) * P], ident[:])
                        end(last, name)
                if st.exists(-1):
                    read("Y", t - 1)
                    out = begin("shift", t - 1)
                    last = nc.tensor.matmul(out[:, 0:P], shift_sb[:, 0], x_mid[:, st.slot(-1), P:C], start=True, stop=st.first(-1))
                    if not st.first(-1):
                        last = nc.tensor.matmul(out[:, 0:P], shift_sb[:, 1], x_mid[:, st.slot(-3), P:C], start=False, stop=True)
                    end(last, "shift")
                if st.exists(0):
                    for j in range(4):
                        read(f"S{j}", t)
                        out = begin(f"PT{j}", t)
                        for u in range(2):
                            for kb in range(1 if st.first(0) else 0, 2):
                                last = nc.tensor.transpose(out[:, (2 * u + kb) * P:(2 * u + kb + 1) * P], probs[:, j, u, kb * P:(kb + 1) * P], ident[:])
                        end(last, f"PT{j}")
                if st.exists(2):
                    read("xT", t + 2)
                    L = st.layer(2)
                    for a, name in enumerate(("q", "k", "v")):
                        out = begin(name, t + 2)
                        for k in range(NC):
                            last = nc.tensor.matmul(out[:], xT[:, st.slot(2), k * P:(k + 1) * P], wqkv_sb[:, L, k, a * INNER:(a + 1) * INNER],
                                                    start=(k == 0), stop=(k == NC - 1))
                        end(last, name)
                if st.exists(-1):
                    read("shift", t - 1)
                    out = begin("hT", t - 1)
                    for k in range(NC):
                        last = nc.tensor.transpose(out[:, k * P:(k + 1) * P], hn[:, k * P:(k + 1) * P], ident[:])
                    end(last, "hT")
                if st.exists(0):
                    for j in range(4):
                        read(f"PT{j}", t)
                    out = begin("oT", t)
                    for c in range(4):
                        for kb in range(1 if st.first(0) else 0, 2):
                            for half in range(2):
                                j, u = PLACE[2 * c + half]
                                last = nc.tensor.matmul(out[half * D2:(half + 1) * D2, c * P:(c + 1) * P],
                                                        v_sb[:, st.slot(0 if kb else -2), (2 * c + half) * D2:(2 * c + half + 1) * D2], PT[:, j, u, kb],
                                                        start=(kb == 0 or st.first(0)), stop=(kb == 1), tile_position=(0, half * D2))
                    end(last, "oT")
                if st.exists(-1):
                    read("hT", t - 1)
                    for j in range(3):
                        out = begin(f"H{j}", t - 1)
                        for i, chunk in enumerate((2 * j, 2 * j + 1, HC + 2 * j, HC + 2 * j + 1)):
                            for k in range(NC):
                                last = nc.tensor.matmul(out[:, i * P:(i + 1) * P], w1_sb[:, st.layer(-1), k, chunk * P:(chunk + 1) * P], hT[:, k],
                                                        start=(k == 0), stop=(k == NC - 1))
                        end(last, f"H{j}")
                if st.exists(1):
                    read("qT", t + 1)
                    read("kT", t + 1)
                    for j in range(4):
                        out = begin(f"S{j}", t + 1)
                        nc.tensor.matmul(out[:], identb[:], mask_sb[:].rearrange("p a k -> p (a k)"), start=True, stop=False, skip_group_check=True)
                        for u, h in enumerate(PAIRS[j]):
                            rows = slice(h % 2 * D2, (h % 2 + 1) * D2)
                            for kb in range(1 if st.first(1) else 0, 2):
                                last = nc.tensor.matmul(out[:, (2 * u + kb) * P:(2 * u + kb + 1) * P], qT[rows, h // 2, :],
                                                        kT[rows, st.slot(1 if kb else -1), h // 2, :], start=False, stop=(u == 1 and kb == 1), skip_group_check=True)
                        end(last, f"S{j}")
                if st.exists(0):
                    read("oT", t)
                    out = begin("Y", t)
                    for c in range(4):
                        last = nc.tensor.matmul(out[:, 0:C], oT[:, c], wo_sb[:, st.layer(0), c], start=(c == 0), stop=(c == 3))
                    end(last, "Y")
                if st.exists(-1):
                    for j in range(3):
                        read(f"H{j}", t - 1)
                    out = begin("F", t - 1)
                    for c in range(HC):
                        last = nc.tensor.matmul(out[:, 0:C], act_T[:, c], w2_sb[:, st.layer(-1), c], start=(c == 0), stop=(c == HC - 1))
                    end(last, "F")

        @block.scalar
        def _(act):
            for name, tile_, s_ in (("qk_scale", qks_sb, loaded_dve), ("b2", b2_sb, loaded_pool)):
                act.dma_start(tile_[:], ins[name].partition_broadcast(P)).then_inc(s_, 16)
            for name, tile_ in (("ln_g", lng_sb), ("ln_b", lnb_sb), ("b1", b1_sb)):
                act.dma_start(tile_[:], ins[name]).then_inc(loaded_act, 16)
            act.dma_start(b1_dve[:], ins["b1"]).then_inc(loaded_dve, 16)
            w = Waiter(act)
            w.on(for_act, sum(r == "act" for r in READY_FOR.values())), w.on(max_made, 4)
            act.wait_ge(loaded_act, 48)
            act.wait_ge(zero_made, 1)

            def item(name, v):
                w.upto(for_act, ready[name, v])
                return bank(name)

            for st in walk(w):
                t = st.t
                if st.exists(2):
                    src = item("xT", t + 2)
                    s = st.slot(2)
                    nc.scalar.copy(xT[:, s, P:P + 1], zero_col[:] if st.first(2) else xT[:, st.slot(0), 2 * P:2 * P + 1])
                    nc.scalar.copy(xT[:, s, 0:P], src[:, 0:P])
                    nc.scalar.copy(xT[:, s, P + 1:2 * P + 1], src[:, P:C]).then_inc(by_act, 1)
                if st.exists(1):
                    src = item("qT", t + 1)
                    nc.scalar.copy(qT[:].rearrange("p c t -> p (c t)"), src[:]).then_inc(by_act, 1)
                    src = item("kT", t + 1)
                    nc.scalar.copy(kT[:, st.slot(1)].rearrange("p c t -> p (c t)"), src[:]).then_inc(by_act, 1)
                if st.exists(0):
                    for j in (0, 2):
                        src = item(f"PT{j}", t).rearrange("p (u b q) -> p u b q", u=2, b=2)
                        b0 = 1 if st.first(0) else 0
                        nc.scalar.copy(PT[:, j, :, b0:], src[:, :, b0:]).then_inc(by_act, 1)
                if st.exists(2):
                    for a, name in enumerate(("q", "k")):
                        src = item(name, t + 2)
                        nc.scalar.activation(squares[:, a], src[:], ACT.Square).then_inc(squares_made, 1)
                if st.exists(-1):
                    src = item("hT", t - 1)
                    for k in range(NC):
                        last = nc.scalar.activation(hT[:, k], src[:, k * P:(k + 1) * P], ACT.Identity,
                                                    bias=lnb_sb[:, st.layer(-1), k:k + 1], scale=lng_sb[:, st.layer(-1), k:k + 1])
                    last.then_inc(by_act, 1)
                if st.exists(0):
                    src = item("oT", t)
                    nc.scalar.copy(oT[:].rearrange("p c t -> p (c t)"), src[:]).then_inc(by_act, 1)
                if st.exists(2):
                    src = item("v", t + 2)
                    nc.scalar.copy(v_sb[:, st.slot(2)], src[:]).then_inc(by_act, 1)
                if st.exists(-1):
                    for j in range(3):
                        src = item(f"H{j}", t - 1)
                        for i in range(2):
                            chunk = 2 * j + i
                            last = nc.scalar.activation(gate[:, chunk], src[:, (2 + i) * P:(3 + i) * P], ACT.Gelu,
                                                        bias=b1_sb[:, st.layer(-1), HC + chunk:HC + chunk + 1])
                        last.then_inc(gate_made, 1)
                if st.exists(1):
                    for j in range(4):
                        w.upto(max_made, 4 * (t + 1) + j + 1)
                        src = bank(f"S{j}")
                        b0 = P if st.first(1) else 0
                        for u, h in enumerate(PAIRS[j]):
                            last = nc.scalar.activation(probs[:, j, u, b0:], src[:, u * 2 * P + b0:(u + 1) * 2 * P], ACT.Exp,
                                                        bias=negmax[:, j, u:u + 1], accum_out=sums[:, j, u:u + 1])
                        last.then_inc(exps_made, 1)

        @block.vector
        def _(dve):
            w = Waiter(dve)
            w.on(for_dve, sum(r == "dve" for r in READY_FOR.values()))
            for s_, n in ((squares_made, 2), (sin_rnorm_made, 3), (gate_made, 3), (hrstd_made, 1), (x_b2_made, 1),
                          (hstats_made, 1), (cos_made, 1), (rot_made, 1), (exps_made, 4), (rsums_made, 4)):
                w.on(s_, n)
            dve.wait_ge(loaded_dve, 48)
            for l in range(LAYERS):
                nc.vector.tensor_scalar(qks8[:, l, 0], qks_sb[:, l, 0], 8.0, None, ALU.mult)
                nc.vector.tensor_scalar(qks8[:, l, 1], qks_sb[:, l, 1], 1.0, None, ALU.mult).then_inc(qscale_made, 1)
            dve.wait_ge(qscale_made, LAYERS)

            def item(name, v):
                w.upto(for_dve, ready[name, v])
                return bank(name)

            def hidden(st, j):
                t = st.t
                w.upto(gate_made, 3 * (t - 1) + j + 1)
                for i in range(2):
                    chunk = 2 * j + i
                    last = nc.vector.scalar_tensor_tensor(act_T[:, chunk], bank(f"H{j}")[:, i * P:(i + 1) * P],
                                                          b1_dve[:, st.layer(-1), chunk:chunk + 1], gate[:, chunk], ALU.add, ALU.mult)
                last.then_inc(by_dve, 1)

            for st in walk(w):
                t = st.t
                if st.exists(-1):
                    mid, up = x_mid[:, st.slot(-1)], item("shift", t - 1)
                    nc.vector.bn_stats(stats[:, 0], mid[:, 0:P])
                    nc.vector.bn_stats(stats[:, 1], up[:, 0:P]).then_inc(hstats_made, 1)
                    w.upto(hstats_made, t)
                    nc.vector.bn_aggr(mv[:], stats[:]).then_inc(hmv_made, 1)
                if st.exists(0):
                    for j in (1, 3):
                        src = item(f"PT{j}", t).rearrange("p (u b q) -> p u b q", u=2, b=2)
                        b0 = 1 if st.first(0) else 0
                        nc.vector.tensor_copy(PT[:, j, :, b0:], src[:, :, b0:]).then_inc(by_dve, 1)
                if st.exists(-1):
                    w.upto(hrstd_made, t)
                    nc.vector.tensor_scalar(hn[:, 0:P], mid[:, 0:P], mv[:, 0:1], rstd[:], ALU.subtract, ALU.mult)
                    nc.vector.tensor_scalar(hn[:, P:C], up[:, 0:P], mv[:, 0:1], rstd[:], ALU.subtract, ALU.mult).then_inc(by_dve, 1)
                if st.exists(2):
                    for a, name in enumerate(("q", "k")):
                        w.upto(squares_made, 2 * (t + 2) + a + 1)
                        nc.vector.tensor_tensor(qk[:, a].rearrange("p (h d) -> p h d", d=D2), bank(name)[:].rearrange("p (h d) -> p h d", d=D2),
                                                qks8[:, st.layer(2), a].unsqueeze(1).to_broadcast([P, H2, D2]), ALU.mult).then_inc(by_dve, 1)
                    nc.vector.tensor_reduce(norm2[:], squares[:].rearrange("p a (h d) -> p (a h) d", d=D2), AX.X, ALU.add).then_inc(norm2_made, 1)
                if st.exists(2):
                    w.upto(sin_rnorm_made, 3 * (t + 2) + 1)
                    nc.vector.tensor_tensor(qk_cos[:].rearrange("p a (h d) -> p a h d", d=D2), qk[:].rearrange("p a (h d) -> p a h d", d=D2),
                                            cos_sb[:, st.position(2)].unsqueeze(2).to_broadcast([P, 2, H2, D2]), ALU.mult).then_inc(cos_made, 1)
                    w.upto(cos_made, t + 3)
                    w.upto(sin_rnorm_made, 3 * (t + 2) + 2)
                    nc.vector.tensor_tensor(qk_cos[:], qk_cos[:], qk_sin[:], ALU.add).then_inc(rot_made, 1)
                if st.exists(-1):
                    for j in range(3):
                        hidden(st, j)
                for j in range(4):
                    if st.exists(1):
                        src = item(f"S{j}", t + 1).rearrange("p (u k) -> p u k", u=2)
                        nc.vector.tensor_reduce(negmax[:, j], src[:, :, P if st.first(1) else 0:], AX.X, ALU.max, negate=True).then_inc(max_made, 1)
                    if j == 1 and st.exists(2):
                        w.upto(rot_made, t + 3)
                        w.upto(sin_rnorm_made, 3 * (t + 2) + 3)
                        nc.vector.tensor_tensor(qk_rot[:].rearrange("p a (h d) -> p (a h) d", d=D2), qk_cos[:].rearrange("p a (h d) -> p (a h) d", d=D2),
                                                rnorm[:].unsqueeze(2).to_broadcast([P, 2 * H2, D2]), ALU.mult).then_inc(rotary_done, 1)
                for j in range(4):
                    if st.exists(1):
                        w.upto(exps_made, 4 * (t + 1) + j + 1)
                        nc.vector.reciprocal(rsums[:, j], sums[:, j]).then_inc(rsums_made, 1)
                        w.upto(rsums_made, 4 * (t + 1) + j + 1)
                        p4 = probs[:, j, :, P if st.first(1) else 0:]
                        nc.vector.tensor_tensor(p4, p4, rsums[:, j].unsqueeze(2).to_broadcast([P, 2, P if st.first(1) else 2 * P]), ALU.mult).then_inc(by_dve, 1)
                    if j == 1 and st.exists(0):
                        src = item("Y", t)
                        nc.vector.tensor_tensor(x_mid[:, st.slot(0)], src[:, 0:C], x_sb[:, st.tile(0), :], ALU.add).then_inc(by_dve, 1)
                if st.exists(-1):
                    src = item("F", t - 1)
                    w.upto(x_b2_made, t)
                    nc.vector.tensor_tensor(x_sb[:, st.tile(-1), :], src[:, 0:C], x_b2[:], ALU.add).then_inc(by_dve, 1)


def final_phase(nc, x_sb, x1_dram, out):
    with ExitStack() as ctx:
        sb = lambda n, s, d=F32: ctx.enter_context(nc.sbuf_tensor(n, s, d))
        sem = nc.alloc_semaphore
        x1_sb = sb("x1_sb", [P, NT, C])
        stats = sb("stats4", [P, NT, 6])
        mv = sb("mv4", [P, NT, 2])
        var_eps = sb("var_eps4", [P, NT])
        minus_half = sb("minus_half4", [P, NT])
        rstd = sb("rstd4", [P, NT])
        nmr = sb("nmr4", [P, NT])
        x1_loaded, out_stored = sem("x1_loaded"), sem("out_stored")
        stats_made, mv_made, half_made, var_made, rstd_made, nmr_made = (sem(f"{x}4_made") for x in ("stats", "mv", "half", "var", "rstd", "nmr"))
        normed, out_made = sem("x4_normed"), sem("out4_made")
        STORES = 4
        CH = NT // STORES
        block = ctx.enter_context(nc.Block())
        out_tiles = out.rearrange("b (t p) c -> p (b t) c", p=P)

        @block.sync
        def _(sp):
            sp.dma_start(x1_sb[:], x1_dram).then_inc(x1_loaded, 16)
            for c in range(STORES):
                sp.wait_ge(out_made, c + 1)
                sp.dma_start(out_tiles[:, c * CH:(c + 1) * CH, :], x1_sb[:, c * CH:(c + 1) * CH, :]).then_inc(out_stored, 16)
            sp.wait_ge(out_stored, 16 * STORES)

        @block.gpsimd
        def _(pool):
            nc.gpsimd.memset(minus_half[:], -0.5).then_inc(half_made, 1)
            pool.wait_ge(half_made, 1)
            pool.wait_ge(mv_made, NT)
            nc.gpsimd.tensor_scalar(var_eps[:], mv[:, :, 1], EPS, None, ALU.add).then_inc(var_made, 1)
            pool.wait_ge(var_made, 1)
            nc.gpsimd.tensor_tensor(out=rstd[:], in0=var_eps[:], in1=minus_half[:], op=ALU.pow).then_inc(rstd_made, 1)

        @block.scalar
        def _(act):
            act.wait_ge(nmr_made, 1)
            with act.Fori(0, NT) as i:
                nc.scalar.activation(x_sb[:, i, :], x_sb[:, i, :], ACT.Identity, bias=nmr[:, bass.ds(i, 1)], scale=rstd[:, bass.ds(i, 1)]).then_inc(normed, 1)

        @block.vector
        def _(dve):
            with dve.Fori(0, NT) as i:
                nc.vector.bn_stats(stats[:, i, :], x_sb[:, i, :]).then_inc(stats_made, 1)
            dve.wait_ge(stats_made, NT)
            for i in range(NT):
                nc.vector.bn_aggr(mv[:, i, :], stats[:, i, :]).then_inc(mv_made, 1)
            dve.wait_ge(rstd_made, 1)
            nc.vector.scalar_tensor_tensor(nmr[:], mv[:, :, 0], -1.0, rstd[:], ALU.mult, ALU.mult).then_inc(nmr_made, 1)
            dve.wait_ge(x1_loaded, 16)
            for c in range(STORES):
                with dve.Fori(0, CH - 1) as g:
                    dve.wait_ge(normed, 1)
                    nc.vector.tensor_tensor(x1_sb[:, c * CH + g, :], x1_sb[:, c * CH + g, :], x_sb[:, c * CH + g, :], ALU.add)
                    dve.sem_inc(normed, -1)
                i = (c + 1) * CH - 1
                dve.wait_ge(normed, 1)
                nc.vector.tensor_tensor(x1_sb[:, i, :], x1_sb[:, i, :], x_sb[:, i, :], ALU.add).then_inc(out_made, 1)
                dve.sem_inc(normed, -1)


def program(nc, ins, out):
    with ExitStack() as ctx:
        sb = lambda n, s, d=F32: ctx.enter_context(nc.sbuf_tensor(n, s, d))
        x_sb = sb("x_sb", [P, NT, C])
        ident = sb("ident", [P, P])
        identb = sb("identb", [P, P], BF16)
        x1_dram = nc.dram_tensor("x1_dram", (P, NT, C), F32).ap()
        with ExitStack() as heads:
            hb = lambda n: heads.enter_context(nc.sbuf_tensor(n, [P, NH, TB, D1], F32))
            QO, K1, V1 = hb("QO"), hb("K1"), hb("V1")
            project_phase(nc, ins, x_sb, QO, K1, V1, ident, identb)
            attention_phase(nc, QO, K1, V1, ident, identb)
            Y = K1[:].rearrange("p n t d -> p (n t d)").rearrange("p (i c) -> p i c", c=C)
            output_phase(nc, ins, x_sb, QO, Y, ident, x1_dram)
        feed_forward_phase(nc, ins, x_sb, ident, identb)
        final_phase(nc, x_sb, x1_dram, out)


def kernel(**inputs):
    import numpy as np
    import concourse.bacc as bacc
    from concourse.bass_utils import run_bass_kernel_spmd

    i = {k.replace("L0_", ""): np.asarray(v) for k, v in inputs.items()}
    f32 = np.float32
    pos = np.arange(T, dtype=f32)
    inv = (f32(1.0) / f32(10000.0) ** (np.arange(0, D1, 2, dtype=f32) / f32(D1))).astype(f32)
    fr = pos[:, None] * inv[None, :]
    half = np.arange(0, D2, 2, dtype=f32)
    inv2 = (f32(1.0) / f32(10000.0) ** (half / f32(D2))).astype(f32)
    fr2 = pos[:, None] * inv2[None, :]
    base = (half + f32(0.4 * D2)) / f32(1.4 * D2)
    power = (pos - f32(T // 2)) / f32(P // 2)
    scale = (base[None, :] ** power[:, None]).astype(f32)
    cos2, sin2 = np.cos(fr2), np.sin(fr2)
    qc, qs, kc, ks = cos2 * scale, sin2 * scale, cos2 / scale, sin2 / scale

    def halves(w, axis):
        parts = np.split(w, 2, axis=axis)
        pad = [(0, 0)] * w.ndim
        pad[axis] = (0, HC * P - HID)
        return np.concatenate([np.pad(p, pad) for p in parts], axis=axis)

    def by_partition(w):
        return w.reshape(LAYERS, -1, P).transpose(2, 0, 1)

    arrays = {
        "x": i["attn_x"],
        "wqkv1": np.concatenate([i["attn_Wq"].T, i["attn_Wk"].T, i["attn_Wv"].T], axis=1),
        "bqkv1": np.concatenate([i["attn_bq"], i["attn_bk"], i["attn_bv"]]),
        "cos1": np.cos(fr).astype(f32),
        "sin1": np.concatenate([-np.sin(fr), np.sin(fr)], axis=1).astype(f32),
        "wo1": i["attn_Wo"].T,
        "bo1": i["attn_bo"],
        "wqkv2": i["ffn_wqkv"],
        "wo2": i["ffn_wo"],
        "w1": halves(i["ffn_w1"], 2),
        "w2": np.pad(i["ffn_w2"], ((0, 0), (0, HC * P - HID), (0, 0))),
        "qk_scale": np.stack([i["ffn_q_scale"], i["ffn_k_scale"]], axis=1),
        "b2": i["ffn_b2"],
        "ln_g": by_partition(i["ffn_ln_g"]),
        "ln_b": by_partition(i["ffn_ln_b"]),
        "b1": by_partition(halves(i["ffn_b1"], 1)),
        "cos2": np.concatenate([qc, qc, kc, kc], axis=1).astype(f32),
        "sin2": np.concatenate([-qs, qs, -ks, ks], axis=1).astype(f32),
    }
    arrays = {k: np.ascontiguousarray(v) for k, v in arrays.items()}
    nc = bacc.Bacc("TRN2", target_bir_lowering=False, num_devices=1)
    ins = {k: nc.dram_tensor("in_" + k, v.shape, mybir.dt.from_np(v.dtype), kind="ExternalInput").ap()
           for k, v in arrays.items()}
    out = nc.dram_tensor("out_0", (B, T, C), F32, kind="ExternalOutput").ap()
    program(nc, ins, out)
    r = run_bass_kernel_spmd(nc, [{"in_" + k: v for k, v in arrays.items()}], core_ids=[0])
    return r.results[0]["out_0"]
```

```python
from contextlib import ExitStack

import concourse.bass as bass
import numpy as np
from concourse import mybir

F32 = mybir.dt.float32
BF16 = mybir.dt.bfloat16
ACT = mybir.ActivationFunctionType
ALU = mybir.AluOpType
AX = mybir.AxisListType

P = 128
B, T, C = 2, 2048, 256
NT = B * T // P
TB = T // P
H1, D1 = 16, 16
NH = B * H1
NC = C // P
EPS = 1e-5



def identities(nc, block, ident, identb, made):
    @block.gpsimd
    def _(pool):
        nc.gpsimd.memset(ident[:], 0.0).then_inc(made, 1)
        pool.wait_ge(made, 1)
        nc.gpsimd.affine_select(out=ident[:], in_=ident[:], compare_op=ALU.not_equal, fill=1.0,
                                base=0, pattern=[[-1, P]], channel_multiplier=1).then_inc(made, 1)
        pool.wait_ge(made, 2)
        nc.gpsimd.tensor_copy(identb[:], ident[:]).then_inc(made, 1)


UNROLL = 4


class Step:

    def __init__(self, t, skipped, turn, tiles):
        self.t, self.skipped, self.turn = t, skipped, turn
        self.tiles = tiles

    def exists(self, d):
        return 0 <= self.t + self.skipped + d < self.tiles

    def layer(self, d):
        return (self.t + self.skipped + d) // NT

    def first(self, d):
        return self.turn is None and (self.t + self.skipped + d) % NT < 2

    def position(self, d):
        v = (self.t + self.skipped + d) % NT // 2
        return v if self.turn is None else v + UNROLL // 2 * self.turn

    def tile(self, d):
        return (self.t + self.skipped + d) % 2 * TB + self.position(d)

    def slot(self, d, n=4):
        return (self.t + d) % n


class Waiter:

    def __init__(self, eng):
        self.eng, self.sems, self.fallen = eng, {}, {}

    def on(self, sem, per_step):
        self.sems[sem.name] = (sem, per_step)
        self.fallen[sem.name] = 0
        return sem

    def upto(self, sem, count):
        self.eng.wait_ge(sem, count - self.fallen[sem.name])

    def fall(self):
        for sem, per_step in self.sems.values():
            self.eng.sem_inc(sem, -UNROLL * per_step)
            self.fallen[sem.name] += UNROLL * per_step


def walk(waiter, segments, tiles):
    t, skipped = segments[0][0], 0
    for first, steps, turns in segments:
        assert first == t + skipped
        if turns:
            with waiter.eng.Fori(0, turns) as turn:
                for _ in range(steps):
                    yield Step(t, skipped, turn, tiles)
                    t += 1
                waiter.fall()
            skipped += (turns - 1) * steps
        else:
            for _ in range(steps):
                yield Step(t, skipped, None, tiles)
                t += 1


PROJECT_SEGMENTS = ((-4, 8, 0), (4, UNROLL, 6), (28, 5, 0))


def project_phase(nc, ins, x_sb, QO, K1, V1, ident, identb):
    with ExitStack() as ctx:
        sb = lambda n, s, d=F32: ctx.enter_context(nc.sbuf_tensor(n, s, d))
        ps = lambda n, s, d=F32: ctx.enter_context(nc.psum_tensor(n, s, d))
        sem = nc.alloc_semaphore
        HD = D1 // 2
        w_sb = sb("wqkv1_sb", [P, NC, 3 * C])
        bias_sb = sb("bqkv1_sb", [P, 3 * C])
        cos_sb = sb("cos1_sb", [P, TB, HD])
        sin_sb = sb("sin1_sb", [P, TB, 2, HD])
        stats = sb("stats0", [P, 4, 6])
        mv = sb("mv0", [P, 4, 2])
        rstd = sb("rstd0", [P, 4])
        var_eps = sb("var_eps0", [P, 4])
        minus_half = sb("minus_half0", [P, 1])
        nmr = sb("nmr0", [P, 4])
        xn = sb("xn0", [P, 4, C])
        xnT = sb("xnT0", [P, 4, C])
        qk = sb("qk0", [P, 2, 2 * C])
        qk_cos = sb("qk_cos", [P, 2, 2 * C])
        qk_sin = sb("qk_sin", [P, 2, 2 * C])
        psT = ps("psT0", [P, 2, 512])
        psQK = ps("psQK0", [P, 4, 512])
        psV = ps("psV0", [P, 2, 512])
        x_loaded = [sem(f"x_loaded{c}") for c in range(3)]
        weights_loaded, tables_loaded, sin_loaded = sem("w1_loaded"), sem("tables1_loaded"), sem("sin1_loaded")
        ident_made, stats_made, mv_made, rstd_made, nmr_made, xn_made = (sem(n) for n in ("ident_made", "stats0_made", "mv0_made", "rstd0_made", "nmr0_made", "xn0_made"))
        var_made, half_made = sem("var0_made"), sem("half0_made")
        xnT_in_psum, xnT_copied, proj_done, v_read = sem("xnT0_in_psum"), sem("xnT0_copied"), sem("proj0_done"), sem("v0_read")
        qk_biased, cos_done, sin_done = sem("qk0_biased"), sem("cos0_done"), sem("sin0_done")

        block = ctx.enter_context(nc.Block())
        identities(nc, block, ident, identb, ident_made)
        x_tiles = ins["x"].rearrange("b (t p) c -> p b t c", p=P)
        x_batches = x_sb[:].rearrange("p (b t) c -> p b t c", b=B)
        heads_of = lambda v: slice(v % 2 * H1, (v % 2 + 1) * H1)

        @block.sync
        def _(sp):
            for c, here in enumerate((slice(0, 1), slice(1, 4), slice(4, TB))):
                for b in range(B):
                    sp.dma_start(x_batches[:, b, here], x_tiles[:, b, here]).then_inc(x_loaded[c], 16)

        @block.vector
        def _(dve):
            w = Waiter(dve)
            for s_ in (stats_made, rstd_made, proj_done, qk_biased, sin_done):
                w.on(s_, 1)
            for st in walk(w, PROJECT_SEGMENTS, NT):
                t = st.t
                if st.turn is None and t in (-4, -2, 3):
                    dve.wait_ge(x_loaded[(-4, -2, 3).index(t)], 16 * B)
                if st.exists(3):
                    v, s = t + 3, st.slot(3)
                    w.upto(rstd_made, v + 1)
                    nc.vector.scalar_tensor_tensor(nmr[:, s:s + 1], mv[:, s, 0:1], -1.0, rstd[:, s:s + 1], ALU.mult, ALU.mult).then_inc(nmr_made, 1)
                if st.exists(0):
                    if t == 0 and st.turn is None:
                        dve.wait_ge(tables_loaded, 32)
                    w.upto(proj_done, t + 1)
                    nc.vector.tensor_tensor(qk[:, t % 2], psQK[:, st.slot(0)], bias_sb[:, 0:2 * C], ALU.add).then_inc(qk_biased, 1)
                    nc.vector.tensor_tensor(V1[:, heads_of(t), st.position(0), :], psV[:, t % 2, 0:C].rearrange("p (h d) -> p h d", h=H1),
                                            bias_sb[:, 2 * C:].rearrange("p (h d) -> p h d", h=H1), ALU.add).then_inc(v_read, 1)
                if st.exists(4):
                    nc.vector.bn_stats(stats[:, st.slot(4), :], x_sb[:, st.tile(4), :]).then_inc(stats_made, 1)
                if st.exists(0):
                    w.upto(qk_biased, t + 1)
                    nc.vector.tensor_tensor(qk_cos[:, t % 2].rearrange("p (h d) -> p h d", d=HD),
                                            qk[:, t % 2].rearrange("p (h d) -> p h d", d=HD),
                                            cos_sb[:, st.position(0), :].unsqueeze(1).to_broadcast([P, 4 * H1, HD]),
                                            ALU.mult).then_inc(cos_done, 1)
                if st.exists(4):
                    w.upto(stats_made, t + 5)
                    nc.vector.bn_aggr(mv[:, st.slot(4), :], stats[:, st.slot(4), :]).then_inc(mv_made, 1)
                if st.exists(-1):
                    w.upto(sin_done, t)
                    for dst, a in ((QO, 0), (K1, C)):
                        nc.vector.tensor_tensor(dst[:, heads_of(t - 1), st.position(-1), :],
                                                qk_cos[:, (t - 1) % 2, a:a + C].rearrange("p (h d) -> p h d", h=H1),
                                                qk_sin[:, (t - 1) % 2, a:a + C].rearrange("p (h d) -> p h d", h=H1), ALU.add)

        @block.gpsimd
        def _(pool):
            w = Waiter(pool)
            for s_ in (mv_made, var_made, cos_done):
                w.on(s_, 1)
            nc.gpsimd.memset(minus_half[:], -0.5).then_inc(half_made, 1)
            pool.wait_ge(half_made, 1)
            for st in walk(w, PROJECT_SEGMENTS, NT):
                if st.exists(4):
                    v, s = st.t + 4, st.slot(4)
                    w.upto(mv_made, v + 1)
                    nc.gpsimd.tensor_scalar(var_eps[:, s:s + 1], mv[:, s, 1:2], EPS, None, ALU.add).then_inc(var_made, 1)
                    w.upto(var_made, v + 1)
                    nc.gpsimd.tensor_tensor(out=rstd[:, s:s + 1], in0=var_eps[:, s:s + 1], in1=minus_half[:], op=ALU.pow).then_inc(rstd_made, 1)
                if st.exists(0):
                    if st.t == 0 and st.turn is None:
                        pool.wait_ge(sin_loaded, 16)
                    w.upto(cos_done, st.t + 1)
                    v = qk[:, st.t % 2].rearrange("p (h s d) -> p h s d", s=2, d=HD)
                    o = qk_sin[:, st.t % 2].rearrange("p (h s d) -> p h s d", s=2, d=HD)
                    for half in range(2):
                        sn = sin_sb[:, st.position(0), half, :].unsqueeze(1).to_broadcast([P, 2 * H1, HD])
                        last = nc.gpsimd.tensor_tensor(out=o[:, :, half], in0=v[:, :, 1 - half], in1=sn, op=ALU.mult)
                    last.then_inc(sin_done, 1)

        @block.tensor
        def _(pe):
            w = Waiter(pe)
            w.on(xn_made, 1), w.on(xnT_copied, 1), w.on(v_read, 1)
            pe.wait_ge(ident_made, 3)
            for st in walk(w, PROJECT_SEGMENTS, NT):
                if st.exists(1):
                    w.upto(xn_made, st.t + 2)
                    for k in range(NC):
                        last = nc.tensor.transpose(psT[:, (st.t + 1) % 2, k * P:(k + 1) * P], xn[:, st.slot(1), k * P:(k + 1) * P], ident[:])
                    last.then_inc(xnT_in_psum, 1)
                if st.exists(0):
                    s = st.slot(0)
                    if st.t == 0 and st.turn is None:
                        pe.wait_ge(weights_loaded, 16)
                    w.upto(xnT_copied, st.t + 1)
                    for k in range(NC):
                        nc.tensor.matmul(psQK[:, s], xnT[:, s, k * P:(k + 1) * P], w_sb[:, k, 0:2 * C], start=(k == 0), stop=(k == NC - 1))
                    if st.exists(-2):
                        w.upto(v_read, st.t - 1)
                    for k in range(NC):
                        last = nc.tensor.matmul(psV[:, st.t % 2, 0:C], xnT[:, s, k * P:(k + 1) * P], w_sb[:, k, 2 * C:], start=(k == 0), stop=(k == NC - 1))
                    last.then_inc(proj_done, 1)

        @block.scalar
        def _(act):
            w = Waiter(act)
            w.on(nmr_made, 1), w.on(xnT_in_psum, 1)
            act.dma_start(w_sb[:], ins["wqkv1"].rearrange("(k p) n -> p k n", p=P)).then_inc(weights_loaded, 16)
            act.dma_start(bias_sb[:], ins["bqkv1"].partition_broadcast(P)).then_inc(tables_loaded, 16)
            act.dma_start(cos_sb[:], ins["cos1"].rearrange("(t p) d -> p t d", p=P)).then_inc(tables_loaded, 16)
            act.dma_start(sin_sb[:], ins["sin1"].rearrange("(t p) (s d) -> p t s d", p=P, s=2)).then_inc(sin_loaded, 16)
            for st in walk(w, PROJECT_SEGMENTS, NT):
                if st.exists(1):
                    w.upto(xnT_in_psum, st.t + 2)
                    nc.scalar.copy(xnT[:, st.slot(1)], psT[:, (st.t + 1) % 2, 0:C]).then_inc(xnT_copied, 1)
                if st.exists(2):
                    s = st.slot(2)
                    w.upto(nmr_made, st.t + 3)
                    nc.scalar.activation(xn[:, s], x_sb[:, st.tile(2), :], ACT.Identity, bias=nmr[:, s:s + 1], scale=rstd[:, s:s + 1]).then_inc(xn_made, 1)


SLOTS = 6
STACK = SLOTS * D1
SPLIT_Q = (slice(0, 3), slice(3, 6, 2), slice(4, 5))
SPLIT_K = (slice(2, 5), slice(1, 6, 4), slice(0, 1))
AUX = 3
PROBS = 4
W2 = 1024
BODY = 3
VW = 32


def mask_and_shift(nc, pool, mask_sb, shift_sb):
    mask_made, shift_made = nc.alloc_semaphore("mask_made"), nc.alloc_semaphore("shift_made")
    nc.gpsimd.memset(shift_sb[:], 0.0).then_inc(shift_made, 1)
    pool.wait_ge(shift_made, 1)
    nc.gpsimd.affine_select(out=shift_sb[:, 0], in_=shift_sb[:, 0], compare_op=ALU.not_equal, fill=1.0,
                            base=1, pattern=[[-1, P]], channel_multiplier=1)
    nc.gpsimd.affine_select(out=shift_sb[:, 1], in_=shift_sb[:, 1], compare_op=ALU.not_equal, fill=1.0,
                            base=-(P - 1), pattern=[[-1, P]], channel_multiplier=1)
    nc.gpsimd.memset(mask_sb[:], 0.0).then_inc(mask_made, 1)
    pool.wait_ge(mask_made, 1)
    nc.gpsimd.affine_select(out=mask_sb[:, :, 0:P], in_=mask_sb[:, :, 0:P], compare_op=ALU.is_ge, fill=NO_KEY,
                            base=0, pattern=[[0, 2], [1, P]], channel_multiplier=-1)
    nc.gpsimd.affine_select(out=mask_sb[:, :, P:], in_=mask_sb[:, :, P:], compare_op=ALU.is_ge, fill=NO_KEY,
                            base=0, pattern=[[0, 2], [-1, P]], channel_multiplier=1)


def attention_phase(nc, QO, K1, V1, mask_sb, shift_sb, ident, identb):
    with ExitStack() as ctx:
        sb = lambda n, s, d=F32: ctx.enter_context(nc.sbuf_tensor(n, s, d))
        ps = lambda n, s, d=F32: ctx.enter_context(nc.psum_tensor(n, s, d))
        sem = nc.alloc_semaphore
        q_parts = sb("q_parts", [P, TB, P], BF16)
        k_parts = sb("k_parts", [P, TB, P], BF16)
        m_parts = sb("m_parts", [P, TB, 32], BF16)
        rest1 = sb("rest1", [P, 2, TB, D1])
        rest2 = sb("rest2", [P, 2, TB, D1])
        m_rest = sb("m_rest", [P, 2, TB])
        q_stack = sb("q_stack", [P, BODY, T], BF16)
        k_stack = sb("k_stack", [P, BODY, T], BF16)
        v_ones = sb("v_ones", [P, BODY, TB, VW])
        probs = sb("probs", [P, PROBS, W2])
        mx4 = sb("mx4", [P, BODY, TB, 4])
        negmax = sb("negmax", [P, BODY, TB])
        o_stage = sb("o_stage", [P, 512])
        rsum = sb("rsum", [P, BODY, TB])
        scores = ps("scores", [P, 4, 512])
        aux = ps("aux", [P, AUX, 512])
        pv = ps("pv", [P, 512])

        parts_made, parts_read = sem("parts_made"), sem("parts_read")
        consts_made, k_consts_made, split_step, first_split_step = sem("consts_made"), sem("k_consts_made"), sem("split_step"), sem("first_split_step")
        scores_ready, probs_ready = sem("scores_ready"), sem("probs_ready")
        pv_done, pv_copied, v_made = sem("pv_done"), sem("pv_copied"), sem("v_made")
        max_in_psum, max_taken = sem("max_in_psum"), sem("max_taken")
        head_max, m_parts_made = sem("head_max"), sem("m_parts_made")
        stack_in_psum, stack_copied = sem("stack_in_psum"), sem("stack_copied")
        rsum_made, maxima_written = sem("rsum_made"), sem("maxima_written")

        block = ctx.enter_context(nc.Block())

        K_STEPS, Q_STEPS, M_STEPS, O_STEP = (8, 9), (10, 11), (TB - 2, TB - 1), 2
        LEAD = 3
        DVE_ITEMS, ACT_ITEMS = 4 * TB + 1, 6

        def steps():
            return [(0, s) for s in range(LEAD, TB)] + [(1, s) for s in range(LEAD)]

        def ahead(d, s):
            return (d + 1, s + LEAD) if s < TB - LEAD else (d + 2, s + LEAD - TB)

        def aux_items(left):
            items = []
            for d, s in steps():
                a, tile = ahead(d, s)
                if d == 0 and left == 2 and s in K_STEPS + Q_STEPS:
                    items.append((d, s, "stack", (K_STEPS + Q_STEPS).index(s)))
                if d == 0 and left >= 1 and s in M_STEPS:
                    items.append((d, s, "maxrow", M_STEPS.index(s)))
                if left >= a:
                    items += [(d, s, "max", (a, tile, q)) for q in range(4)]
                if d == 1 and s == O_STEP:
                    items.append((d, s, "out", None))
            return items

        PROLOGUE_ITEMS = 4 + 4 * TB + 4 + 2 + 4 * 2 * LEAD

        def banks(r, left):
            first = PROLOGUE_ITEMS + (r * len(aux_items(2)) if left == 2 else len(aux_items(1)) if left == 0 else 0)
            return [(first + i) % AUX for i in range(len(aux_items(left)))]

        assert len(aux_items(2)) == DVE_ITEMS + ACT_ITEMS and BODY * len(aux_items(2)) % AUX == 0

        def all_heads(eng, head, per_head):
            with eng.Fori(0, (NH - 2) // BODY) as m:
                for r in range(BODY):
                    head(r, m * BODY + r, 2)
                for semaphore, rises in per_head:
                    eng.sem_inc(semaphore, -BODY * rises)
            head(0, NH - 2, 1)
            head(1, NH - 1, 0)

        def split_head(engine, chain, n):
            for j, (src, parts, (hi, mid, lo)) in enumerate(((K1, k_parts, SPLIT_K), (QO, q_parts, SPLIT_Q))):
                slots = parts[:, :, 0:STACK].rearrange("p t (s d) -> p t s d", d=D1)
                x = src[:, n]
                chain(engine.tensor_copy(slots[:, :, hi, :], x.unsqueeze(2).to_broadcast([P, TB, 3, D1])))
                chain(engine.tensor_tensor(out=rest1[:, j], in0=x, in1=slots[:, :, hi.start, :], op=ALU.subtract))
                chain(engine.tensor_copy(slots[:, :, mid, :], rest1[:, j].unsqueeze(2).to_broadcast([P, TB, 2, D1])))
                chain(engine.tensor_tensor(out=rest2[:, j], in0=rest1[:, j], in1=slots[:, :, mid.start, :], op=ALU.subtract))
                engine.tensor_copy(slots[:, :, lo.start, :], rest2[:, j]).then_inc(parts_made, 1)

        @block.gpsimd
        def _(pool):
            nc.gpsimd.memset(k_parts[:, :, STACK:], 0.0).then_inc(consts_made, 1)
            pool.wait_ge(consts_made, 1)
            nc.gpsimd.memset(k_parts[:, :, STACK:STACK + 3], 1.0).then_inc(k_consts_made, 1)
            nc.gpsimd.memset(m_parts[:], 0.0).then_inc(consts_made, 1)
            nc.gpsimd.memset(v_ones[:], 0.0).then_inc(consts_made, 1)
            pool.wait_ge(consts_made, 3)
            nc.gpsimd.memset(v_ones[:, :, :, D1:D1 + 1], 1.0)

            def chain(instruction):
                instruction.then_inc(split_step, 1)
                pool.wait_ge(split_step, 1)
                pool.sem_inc(split_step, -1)

            def split_qk(r, n):
                pool.wait_ge(parts_read, r)
                split_head(nc.gpsimd, chain, n)

            def split_max_and_v(r, slot, n):
                pool.wait_ge(head_max, r + 1)
                x = negmax[:, slot]
                chain(nc.gpsimd.tensor_copy(m_parts[:, :, 0], x))
                chain(nc.gpsimd.tensor_tensor(out=m_rest[:, 0], in0=x, in1=m_parts[:, :, 0], op=ALU.subtract))
                chain(nc.gpsimd.tensor_copy(m_parts[:, :, 1], m_rest[:, 0]))
                chain(nc.gpsimd.tensor_tensor(out=m_rest[:, 1], in0=m_rest[:, 0], in1=m_parts[:, :, 1], op=ALU.subtract))
                nc.gpsimd.tensor_copy(m_parts[:, :, 2], m_rest[:, 1]).then_inc(m_parts_made, 1)
                nc.gpsimd.tensor_copy(v_ones[:, slot, :, 0:D1], V1[:, n]).then_inc(v_made, 1)

            def head(r, n, left):
                if left > 1:
                    split_qk(r + 2, n + 2)
                if left > 0:
                    split_max_and_v(r + 1, (r + 1) % BODY, n + 1)

            split_qk(1, 1)
            split_max_and_v(0, 0, 0)
            all_heads(pool, head, ((parts_read, 1), (head_max, 1)))
            mask_and_shift(nc, pool, mask_sb, shift_sb)

        @block.tensor
        def _(pe):
            ring = dict(item=0, dve=0, act=0, last=[])

            def ring_bank():
                if len(ring["last"]) == AUX:
                    pe.wait_ge(*ring["last"].pop(0))
                ring["item"] += 1
                return (ring["item"] - 1) % AUX

            def for_dve():
                ring["dve"] += 1
                ring["last"].append((max_taken, ring["dve"]))

            def for_act():
                ring["act"] += 1
                ring["last"].append((stack_copied, ring["act"]))

            def stack_item(parts, rows, row0, half):
                bank = ring_bank()
                dst = aux[row0:row0 + rows, bank].bitcast(BF16).rearrange("k (t c) -> k t c", c=P)
                for t in range(8):
                    last = nc.tensor.transpose(dst[:, t], parts[:, half * 8 + t, 0:rows], identb[:])
                last.then_inc(stack_in_psum, 1)
                for_act()

            def stack_items(r, halves=(0, 1, 2, 3)):
                for h in halves:
                    if h % 2 == 0:
                        pe.wait_ge(parts_made, 2 * r + 1 + h // 2)
                    stack_item(k_parts if h < 2 else q_parts, P if h < 2 else STACK, 0, h % 2)

            def max_item(r, half):
                pe.wait_ge(m_parts_made, r + 1)
                stack_item(m_parts, 32, STACK, half)

            def score_for_max(r, t, quarters, first_half_signals=None):
                if t == 0:
                    pe.wait_ge(stack_copied, ring["act"])
                for q in quarters:
                    bank = ring_bank()
                    lhsT = q_stack[0:STACK, r % BODY, t * P:(t + 1) * P]
                    if first_half_signals is not None and q == 0:
                        nc.tensor.matmul(aux[:, bank, 0:256], lhsT, k_stack[0:STACK, r % BODY, 0:256],
                                         start=True, stop=True).then_inc(first_half_signals, 1)
                        nc.tensor.matmul(aux[:, bank, 256:512], lhsT, k_stack[0:STACK, r % BODY, 256:512],
                                         start=True, stop=True).then_inc(max_in_psum, 1)
                    else:
                        nc.tensor.matmul(aux[:, bank], lhsT, k_stack[0:STACK, r % BODY, q * 512:(q + 1) * 512],
                                         start=True, stop=True).then_inc(max_in_psum, 1)
                    for_dve()

            def score(r, s, h, signal=None):
                unit = 2 * TB * r + 2 * s + h
                if unit >= 2:
                    pe.wait_ge(probs_ready, unit - 1)
                if s == 0:
                    pe.wait_ge(stack_copied, ring["act"])
                for j in range(2):
                    last = nc.tensor.matmul(scores[:, 2 * h + j], k_stack[:, r % BODY, s * P:(s + 1) * P],
                                            q_stack[:, r % BODY, (2 * h + j) * 512:(2 * h + j + 1) * 512], start=True, stop=True)
                    if j == 0 and signal is not None:
                        last.then_inc(signal, 1)
                last.then_inc(scores_ready, 1)

            def weigh(r, s):
                if s == 0:
                    pe.wait_ge(v_made, r + 1)
                    if r:
                        pe.wait_ge(pv_copied, r)
                pe.wait_ge(probs_ready, 2 * TB * r + 2 * s + 2)
                for j in range(4):
                    last = nc.tensor.matmul(pv[VW * j:VW * (j + 1), :], v_ones[:, r % BODY, s, :],
                                            probs[:, (2 * s + j // 2) % PROBS, (j % 2) * 512:(j % 2 + 1) * 512],
                                            start=(s == 0), stop=(s == TB - 1), tile_position=(0, VW * j))
                last.then_inc(pv_done, 1)

            def output_item(r):
                pe.wait_ge(pv_copied, r + 1)
                bank = ring_bank()
                for c in range(4):
                    last = nc.tensor.transpose(aux[:, bank, c * P:(c + 1) * P], o_stage[:, c * P:(c + 1) * P], ident[:])
                last.then_inc(max_in_psum, 1)
                for_dve()

            def step(r, d, s, left):
                ahead_d, tile = ahead(d, s)
                scored, maxima = left >= d, left >= ahead_d
                here = r + d
                if d == 0 and left == 2 and s in K_STEPS + Q_STEPS:
                    stack_items(r + 2, [(K_STEPS + Q_STEPS).index(s)])
                if d == 0 and left >= 1 and s in M_STEPS:
                    max_item(r + 1, M_STEPS.index(s))
                if scored:
                    score(here, s, 0)
                if maxima:
                    score_for_max(r + ahead_d, tile, (0, 1))
                if scored:
                    score(here, s, 1, parts_read if d == 0 and left == 2 and s == Q_STEPS[1] else None)
                if maxima:
                    score_for_max(r + ahead_d, tile, (2, 3))
                if s == 0:
                    weigh(here - 1, TB - 1)
                elif scored:
                    weigh(here, s - 1)
                if d == 1 and s == O_STEP:
                    output_item(r)

            def head(r, n, left):
                if r == 0:
                    ring.update(start, last=list(start["last"]))
                assert ring["item"] % AUX == banks(r, left)[0]
                for d, s in steps():
                    step(r, d, s, left)

            pe.wait_ge(k_consts_made, 1)
            stack_items(0)
            for t in range(TB):
                score_for_max(0, t, range(4), parts_read if t == 0 else None)
            stack_items(1)
            max_item(0, 0)
            max_item(0, 1)
            for t in range(LEAD):
                score_for_max(1, t, range(4))
            for s in range(LEAD):
                score(0, s, 0)
                score_for_max(1, s + LEAD, (0, 1))
                score(0, s, 1, parts_read if s == 0 else None)
                score_for_max(1, s + LEAD, (2, 3))
                if s:
                    weigh(0, s - 1)
            start = dict(ring, last=list(ring["last"]))
            all_heads(pe, head, ((parts_made, 2), (m_parts_made, 1), (v_made, 1), (pv_copied, 1), (probs_ready, 2 * TB),
                                 (max_taken, DVE_ITEMS), (stack_copied, ACT_ITEMS)))

        @block.scalar
        def _(act):
            copied = [0]

            def copy_stack_item(dst, bank, rows, row0):
                copied[0] += 1
                act.wait_ge(stack_in_psum, copied[0])
                nc.scalar.copy(dst, aux[row0:row0 + rows, bank].bitcast(BF16)).then_inc(stack_copied, 1)

            def copy_stack(slot, part, bank):
                stack, rows = (k_stack, P) if part < 2 else (q_stack, STACK)
                copy_stack_item(stack[0:rows, slot, part % 2 * W2:(part % 2 + 1) * W2], bank, rows, 0)

            def copy_maxima(slot, half, bank):
                copy_stack_item(q_stack[STACK:P, slot, half * W2:(half + 1) * W2], bank, P - STACK, STACK)

            def exponentiate(r, s, h):
                unit = 2 * TB * r + 2 * s + h
                act.wait_ge(scores_ready, unit + 1)
                if TB * r + s >= 2:
                    act.wait_ge(pv_done, TB * r + s - 1)
                nc.scalar.activation(probs[:, unit % PROBS], scores[:, 2 * h:2 * h + 2].rearrange("p a n -> p (a n)"),
                                     ACT.Exp, scale=float(D1) ** -0.5).then_inc(probs_ready, 1)

            def head(r, n, left):
                if r == 0:
                    copied[0] = start
                items, bank_of = aux_items(left), banks(r, left)
                for d, s in steps():
                    here = [(kind, what, bank) for (di, si, kind, what), bank in zip(items, bank_of) if (di, si) == (d, s)]
                    for kind, what, bank in here:
                        if kind == "stack":
                            copy_stack((r + 2) % BODY, what, bank)
                        if kind == "maxrow":
                            copy_maxima((r + 1) % BODY, what, bank)
                    if left >= d:
                        exponentiate(r + d, s, 0)
                        exponentiate(r + d, s, 1)
                    if (d, s) == (1, 0):
                        act.wait_ge(pv_done, TB * (r + 1))
                        nc.scalar.copy(o_stage[:], pv[:]).then_inc(pv_copied, 1)

            for part in range(4):
                copy_stack(0, part, part % AUX)
            after = 4 + 4 * TB
            for part in range(4):
                copy_stack(1, part, (after + part) % AUX)
            for half in range(2):
                copy_maxima(0, half, (after + 4 + half) % AUX)
            for s in range(LEAD):
                exponentiate(0, s, 0)
                exponentiate(0, s, 1)
            start = copied[0]
            all_heads(act, head, ((stack_in_psum, ACT_ITEMS), (scores_ready, 2 * TB), (pv_done, TB)))

        @block.vector
        def _(dve):
            taken = [0]

            def next_item():
                taken[0] += 1
                dve.wait_ge(max_in_psum, taken[0])

            def take_max(slot, tile, quarter, bank):
                next_item()
                nc.vector.reduce_max(mx4[:, slot, tile, quarter:quarter + 1], aux[:, bank], AX.X).then_inc(max_taken, 1)
                if (tile, quarter) == (TB - 1, 3):
                    dve.drain().then_inc(maxima_written, 1)
                    dve.wait_ge(maxima_written, 1)
                    dve.sem_inc(maxima_written, -1)
                    nc.vector.tensor_reduce(negmax[:, slot], mx4[:, slot], AX.X, ALU.max, negate=True).then_inc(head_max, 1)

            def write_output(r, n, bank):
                next_item()
                item = aux[:, bank].rearrange("p (c j d) -> p c j d", c=4, j=4)
                nc.vector.reciprocal(rsum[:, r].rearrange("p (c j) -> p c j", c=4), item[:, :, :, D1]).then_inc(rsum_made, 1)
                dve.wait_ge(rsum_made, 1)
                dve.sem_inc(rsum_made, -1)
                nc.vector.tensor_tensor(QO[:, n].rearrange("p (j c) d -> p c j d", j=4), item[:, :, :, 0:D1],
                                        rsum[:, r].rearrange("p (c j) -> p c j", c=4).unsqueeze(3).to_broadcast([P, 4, 4, D1]),
                                        ALU.mult).then_inc(max_taken, 1)

            def head(r, n, left):
                if r == 0:
                    taken[0] = start
                for (d, s, kind, what), bank in zip(aux_items(left), banks(r, left)):
                    if kind == "max":
                        take_max((r + what[0]) % BODY, what[1], what[2], bank)
                    if kind == "out":
                        write_output(r, n, bank)

            def first_chain(instruction):
                instruction.then_inc(first_split_step, 1)
                dve.wait_ge(first_split_step, 1)
                dve.sem_inc(first_split_step, -1)

            split_head(nc.vector, first_chain, 0)
            at = 4
            for t in range(TB):
                for q in range(4):
                    take_max(0, t, q, (at + 4 * t + q) % AUX)
            at += 4 * TB + 6
            for t in range(2 * LEAD):
                for q in range(4):
                    take_max(1, t, q, (at + 4 * t + q) % AUX)
            start = taken[0]
            all_heads(dve, head, ((max_in_psum, DVE_ITEMS),))


OUT_SEGMENTS = ((-2, 6, 0), (4, UNROLL, 6), (28, 8, 0))


def output_phase(nc, ins, x_sb, QO, ident, x1_dram, load_weights):
    with ExitStack() as ctx:
        sb = lambda n, s, d=F32: ctx.enter_context(nc.sbuf_tensor(n, s, d))
        ps = lambda n, s, d=F32: ctx.enter_context(nc.psum_tensor(n, s, d))
        sem = nc.alloc_semaphore
        w_sb = sb("wo1_sb", [P, NC, C])
        bias_sb = sb("bo1_sb", [P, C])
        x1_sb = sb("x1_made_sb", [P, B, TB, C])
        o_tile = sb("o_tile", [P, 4, C])
        oT = sb("oT2", [P, 4, C])
        y_normed = sb("y_normed", [P, 4, C])
        stats = sb("stats2", [P, 2, 4, 6])
        mv = sb("mv2", [P, 2, 4, 2])
        var_eps = sb("var_eps2", [P, 2, 4])
        minus_half = sb("minus_half2", [P, 1])
        rstd = sb("rstd2", [P, 2, 4])
        nmr = sb("nmr2", [P, 2, 4])
        psT = ps("psT2", [P, 4, 512])
        psY = ps("psY2", [P, 4, 512])
        weights_loaded, x1_stored = sem("wo1_loaded"), sem("x1_stored")
        o_made, oT_in_psum, oT_copied, y_done = sem("o2_made"), sem("oT2_in_psum"), sem("oT2_copied"), sem("y2_done")
        half_made, y_normed_made, x1_written, x1_normed = sem("half2_made"), sem("y2_normed_made"), sem("x1_written"), sem("x1_normed")
        stats_made, mv_made, var_made, rstd_made, nmr_made = ([sem(f"{x}2{j}_made") for j in range(2)] for x in ("stats", "mv", "var", "rstd", "nmr"))
        STORES = (0, 6, 11, 14, TB)
        x1_out = x1_dram.rearrange("p (b t) c -> p b t c", b=B)

        block = ctx.enter_context(nc.Block())

        @block.sync
        def _(sp):
            sp.dma_start(w_sb[:], ins["wo1"].rearrange("(k p) n -> p k n", p=P)).then_inc(weights_loaded, 16)
            sp.dma_start(bias_sb[:], ins["bo1"].partition_broadcast(P)).then_inc(weights_loaded, 16)
            load_weights(sp)
            for start, end in zip(STORES, STORES[1:]):
                sp.wait_ge(x1_normed, B * end)
                sp.dma_start(x1_out[:, :, start:end], x1_sb[:, :, start:end]).then_inc(x1_stored, 16)
            sp.wait_ge(x1_stored, 16 * (len(STORES) - 1))

        @block.gpsimd
        def _(pool):
            w = Waiter(pool)
            w.on(mv_made[0], 1), w.on(mv_made[1], 1), w.on(var_made[0], 1), w.on(var_made[1], 1)
            nc.gpsimd.memset(minus_half[:], -0.5).then_inc(half_made, 1)
            pool.wait_ge(half_made, 1)
            for st in walk(w, OUT_SEGMENTS, NT):
                for j, d in ((0, 0), (1, -2)):
                    if st.exists(d):
                        v, s = st.t + d, st.slot(d)
                        w.upto(mv_made[j], v + 1)
                        nc.gpsimd.tensor_scalar(var_eps[:, j, s:s + 1], mv[:, j, s, 1:2], EPS, None, ALU.add).then_inc(var_made[j], 1)
                        w.upto(var_made[j], v + 1)
                        nc.gpsimd.tensor_tensor(out=rstd[:, j, s:s + 1], in0=var_eps[:, j, s:s + 1], in1=minus_half[:], op=ALU.pow).then_inc(rstd_made[j], 1)

        @block.tensor
        def _(pe):
            w = Waiter(pe)
            w.on(o_made, 1), w.on(oT_copied, 1)
            pe.wait_ge(weights_loaded, 32)
            for st in walk(w, OUT_SEGMENTS, NT):
                if st.exists(1):
                    s = st.slot(1)
                    w.upto(o_made, st.t + 2)
                    for k in range(NC):
                        last = nc.tensor.transpose(psT[:, s, k * P:(k + 1) * P], o_tile[:, s, k * P:(k + 1) * P], ident[:])
                    last.then_inc(oT_in_psum, 1)
                if st.exists(0):
                    s = st.slot(0)
                    w.upto(oT_copied, st.t + 1)
                    nc.tensor.matmul(psY[:, s, 0:C], ident[:], bias_sb[:], start=True, stop=False)
                    for k in range(NC):
                        last = nc.tensor.matmul(psY[:, s, 0:C], oT[:, s, k * P:(k + 1) * P], w_sb[:, k], start=False, stop=(k == NC - 1))
                    last.then_inc(y_done, 1)

        @block.scalar
        def _(act):
            w = Waiter(act)
            w.on(oT_in_psum, 1), w.on(nmr_made[0], 1), w.on(nmr_made[1], 1)

            def normalise(dst, src, j, s, made):
                nc.scalar.activation(dst, src, ACT.Identity, bias=nmr[:, j, s:s + 1], scale=rstd[:, j, s:s + 1]).then_inc(made, 1)

            for st in walk(w, OUT_SEGMENTS, NT):
                if st.exists(1):
                    w.upto(oT_in_psum, st.t + 2)
                    nc.scalar.copy(oT[:, st.slot(1)], psT[:, st.slot(1), 0:C]).then_inc(oT_copied, 1)
                if st.exists(2):
                    b = (st.t + 2) % 2
                    nc.scalar.copy(o_tile[:, st.slot(2)].rearrange("p (h d) -> p h d", d=D1),
                                   QO[:, b * H1:(b + 1) * H1, st.position(2), :]).then_inc(o_made, 1)
                if st.exists(-1):
                    w.upto(nmr_made[0], st.t)
                    normalise(y_normed[:, st.slot(-1)], psY[:, st.slot(-1), 0:C], 0, st.slot(-1), y_normed_made)
                if st.exists(-4):
                    w.upto(nmr_made[1], st.t - 3)
                    normalise(x_sb[:, st.tile(-4), :], x1_sb[:, st.t % 2, st.position(-4), :], 1, st.slot(-4), x1_normed)

        @block.vector
        def _(dve):
            w = Waiter(dve)
            for s_ in (y_done, y_normed_made, x1_written, *stats_made, *rstd_made):
                w.on(s_, 1)

            def minus_mean_rstd(j, v, s):
                w.upto(rstd_made[j], v + 1)
                nc.vector.scalar_tensor_tensor(nmr[:, j, s:s + 1], mv[:, j, s, 0:1], -1.0, rstd[:, j, s:s + 1], ALU.mult, ALU.mult).then_inc(nmr_made[j], 1)

            def statistics(j, v, s, src):
                nc.vector.bn_stats(stats[:, j, s, :], src).then_inc(stats_made[j], 1)

            def mean_and_variance(j, v, s):
                w.upto(stats_made[j], v + 1)
                nc.vector.bn_aggr(mv[:, j, s, :], stats[:, j, s, :]).then_inc(mv_made[j], 1)

            for st in walk(w, OUT_SEGMENTS, NT):
                t = st.t
                if st.exists(-1):
                    minus_mean_rstd(0, t - 1, st.slot(-1))
                if st.exists(-4):
                    minus_mean_rstd(1, t - 4, st.slot(-4))
                if st.exists(0):
                    w.upto(y_done, t + 1)
                    statistics(0, t, st.slot(0), psY[:, st.slot(0), 0:C])
                if st.exists(-2):
                    w.upto(y_normed_made, t - 1)
                    x1_tile = x1_sb[:, t % 2, st.position(-2), :]
                    nc.vector.tensor_tensor(x1_tile, y_normed[:, st.slot(-2)], x_sb[:, st.tile(-2), :], ALU.add).then_inc(x1_written, 1)
                if st.exists(0):
                    mean_and_variance(0, t, st.slot(0))
                if st.exists(-2):
                    w.upto(x1_written, t - 1)
                    statistics(1, t - 2, st.slot(-2), x1_tile)
                    mean_and_variance(1, t - 2, st.slot(-2))


LAYERS = 2
H2, D2 = 8, 64
INNER = H2 * D2
HID = 682
HC = -(-HID // P)
NO_KEY = -1e30
PAIRS = ((0, 2), (4, 6), (1, 3), (5, 7))
PLACE = {h: (j, u) for j, pair in enumerate(PAIRS) for u, h in enumerate(pair)}
BANKS = 8
ITEMS = ([("xT", 2, "act", 0), ("qT", 1, "act", 1), ("kT", 1, "act", 2), ("shift", -1, "dve", 3)]
         + [(f"PT{j}", 0, "act" if j % 2 == 0 else "dve", 4 + j) for j in range(4)]
         + [("q", 2, "act", 0), ("k", 2, "act", 1), ("v", 2, "act", 2), ("hT", -1, "act", 3), ("oT", 0, "act", 0)]
         + [(f"H{j}", -1, "act", 1 + j) for j in range(3)]
         + [(f"S{j}", 1, "dve", 4 + j) for j in range(4)]
         + [("Y", 0, "dve", 2), ("F", -1, "dve", 3)])
TILE_OF = {name: d for name, d, _, _ in ITEMS}
READY_FOR = {name: r for name, _, r, _ in ITEMS}
BANK_OF = {name: b for name, _, _, b in ITEMS}
FREES = {"act": ["xT", "qT", "kT", "PT0", "PT2", "hT", "oT", "v"],
         "dve": ["PT1", "PT3", "shift", "q", "k", "H0", "H1", "H2", "S0", "S1", "Y", "S2", "S3", "F"]}
FREED_BY = {name: r for r, names in FREES.items() for name in names}
SEGMENTS = ((-2, 5, 0), (3, UNROLL, 6), (27, 8, 0), (35, UNROLL, 6), (59, 6, 0))


def item_counts():
    ready, freed, n = {}, {}, {"ready": {"act": 0, "dve": 0}, "freed": {"act": 0, "dve": 0}}
    t, skipped = SEGMENTS[0][0], 0
    for first, steps, turns in SEGMENTS:
        for _ in range(steps):
            step = Step(t, skipped, None, LAYERS * NT)
            for name, d, reader, _ in ITEMS:
                if step.exists(d):
                    n["ready"][reader] += 1
                    ready[name, t + d] = n["ready"][reader]
            for reader, names in FREES.items():
                for name in names:
                    if step.exists(TILE_OF[name]):
                        n["freed"][reader] += 1
                        freed[name, t + TILE_OF[name]] = n["freed"][reader]
            t += 1
        skipped += (turns - 1) * steps if turns else 0
    return ready, freed


class Weights:

    def __init__(self, nc, ctx):
        sb = lambda n, s, d=F32: ctx.enter_context(nc.sbuf_tensor(n, s, d))
        sem = nc.alloc_semaphore
        self.wqkv = sb("wqkv2_sb", [P, LAYERS, NC, 3 * INNER])
        self.wo = sb("wo2_sb", [P, LAYERS, INNER // P, C])
        self.w1 = sb("w1_sb", [P, LAYERS, NC, 2 * HC * P])
        self.w2 = sb("w2_sb", [P, LAYERS, HC, C])
        self.qk_scale = sb("qk_scale_sb", [P, LAYERS, 2, D2])
        self.cos = sb("cos2_sb", [P, TB, 2, D2])
        self.sin = sb("sin2_sb", [P, TB, 2, D2])
        self.ln_g = sb("ln_g_sb", [P, LAYERS, NC])
        self.ln_b = sb("ln_b_sb", [P, LAYERS, NC])
        self.b1 = sb("b1_sb", [P, LAYERS, 2 * HC])
        self.b1_dve = sb("b1_dve", [P, LAYERS, 2 * HC])
        self.b2 = sb("b2_sb", [P, LAYERS, C])
        self.loaded_pe = [sem(f"weights{l}_loaded") for l in range(LAYERS)]
        self.loaded_act, self.loaded_dve, self.loaded_pool = (sem(f"loaded3_{x}") for x in ("act", "dve", "pool"))

    def load(self, sp, ins):
        def rows_last(name, l):
            return ins[name][l].rearrange("(k p) n -> p k n", p=P)

        for l in range(LAYERS):
            for name, tile in (("wqkv2", self.wqkv), ("wo2", self.wo), ("w1", self.w1), ("w2", self.w2)):
                sp.dma_start(tile[:, l], rows_last(name, l)).then_inc(self.loaded_pe[l], 16)
            if l == 0:
                sp.dma_start(self.cos[:], ins["cos2"].rearrange("(t p) (a d) -> p t a d", p=P, a=2)).then_inc(self.loaded_dve, 16)
                sp.dma_start(self.sin[:], ins["sin2"].rearrange("(t p) (a d) -> p t a d", p=P, a=2)).then_inc(self.loaded_pool, 16)
                for name, tile, loaded in (("qk_scale", self.qk_scale, self.loaded_dve), ("b2", self.b2, self.loaded_pool)):
                    sp.dma_start(tile[:], ins[name].partition_broadcast(P)).then_inc(loaded, 16)
                for name, tile, loaded in (("ln_g", self.ln_g, self.loaded_act), ("ln_b", self.ln_b, self.loaded_act),
                                           ("b1", self.b1, self.loaded_act), ("b1", self.b1_dve, self.loaded_dve)):
                    sp.dma_start(tile[:], ins[name]).then_inc(loaded, 16)


def feed_forward_phase(nc, weights, x_sb, free_space, final_stats, mask_sb, shift_sb, ident, identb):
    with ExitStack() as ctx:
        sb = lambda n, s, d=F32: ctx.enter_context(nc.sbuf_tensor(n, s, d))
        sem = nc.alloc_semaphore
        wqkv_sb, wo_sb, w1_sb, w2_sb = weights.wqkv, weights.wo, weights.w1, weights.w2
        qks_sb, cos_sb, sin_sb, b2_sb = weights.qk_scale, weights.cos, weights.sin, weights.b2
        lng_sb, lnb_sb, b1_sb, b1_dve = weights.ln_g, weights.ln_b, weights.b1, weights.b1_dve
        at = [0]

        def in_free(*shape):
            n = int(np.prod(shape))
            view = free_space[:, at[0]:at[0] + n]
            at[0] += n
            names = "abc"[:len(shape)]
            return view.rearrange(f"p ({' '.join(names)}) -> p {' '.join(names)}", **dict(zip(names, shape)))

        qks8 = sb("qk_scale8_sb", [P, LAYERS, 2, D2])
        zero_col = sb("zero_col", [P, 1])
        minus_half = sb("minus_half3", [P, 2 * H2])
        x_stage = sb("x_stage", [P, 4, C])
        xT = sb("xT3", [P, 4, 2 * P + 1])
        squares = in_free(2, INNER)
        qk = in_free(2, INNER)
        qk_cos = in_free(2, INNER)
        qk_sin = in_free(2, INNER)
        qk_rot = in_free(2, INNER)
        norm2 = sb("norm2", [P, 2 * H2])
        norm2_min = sb("norm2_min", [P, 2 * H2])
        rnorm = sb("rnorm", [P, 2 * H2])
        qT = sb("qT3", [P, 4, P])
        kT = sb("kT3", [P, 4, 4, P])
        v_sb = in_free(4, INNER)
        probs = sb("probs3", [P, 4, 2, 2 * P])
        negmax = sb("negmax3", [P, 4, 2])
        sums = sb("sums3", [P, 4, 2])
        rsums = sb("rsums3", [P, 4, 2])
        PT = sb("PT3", [P, 4, 2, 2, P])
        oT = sb("oT3", [P, 4, P])
        x_mid = sb("x_mid", [P, 4, C])
        x_b2 = sb("x_b2", [P, C])
        stats = sb("stats3", [P, 2, 6])
        mv = sb("mv3", [P, 2])
        var_eps = sb("var_eps3", [P, 1])
        rstd = sb("rstd3", [P, 1])
        hn = sb("hn3", [P, C])
        hT = sb("hT3", [P, NC, P])
        gate = sb("gate3", [P, HC, P])
        act_T = sb("act_T3", [P, HC, P])
        ps = [ctx.enter_context(nc.psum_tensor(f"bank{b}", [P, 512], F32)) for b in range(BANKS)]
        bank = lambda name: ps[BANK_OF[name]]

        for_act, for_dve = sem("items_for_act"), sem("items_for_dve")
        by_act, by_dve = sem("read_by_act"), sem("read_by_dve")
        ready_sem, freed_sem = {"act": for_act, "dve": for_dve}, {"act": by_act, "dve": by_dve}
        loaded_pe, loaded_act, loaded_dve, loaded_pool = weights.loaded_pe, weights.loaded_act, weights.loaded_dve, weights.loaded_pool
        zero_made, half_made, qscale_made = (sem(f"{x}3_made") for x in ("zero", "half", "qscale"))
        x_staged, rotary_done = sem("x_staged"), sem("rotary_done")
        squares_made, norm2_made, sin_rnorm_made = sem("squares_made"), sem("norm2_made"), sem("sin_rnorm_made")
        cos_made, rot_made = sem("cos3_made"), sem("rot3_made")
        max_made, exps_made, rsums_made = sem("max3_made"), sem("exps3_made"), sem("rsums3_made")
        hstats_made, hmv_made, hrstd_made = sem("hstats_made"), sem("hmv_made"), sem("hrstd_made")
        gate_made, x_b2_made, norm2_floor, var_made = sem("gate_made"), sem("x_b2_made"), sem("norm2_floor_made"), sem("var3_made")
        ready, freed = item_counts()

        block = ctx.enter_context(nc.Block())

        @block.gpsimd
        def _(pool):
            w = Waiter(pool)
            w.on(norm2_made, 1), w.on(hmv_made, 1)
            own = [w.on(norm2_floor, 1), w.on(var_made, 1)]
            nc.gpsimd.memset(minus_half[:], -0.5).then_inc(half_made, 1)
            nc.gpsimd.memset(zero_col[:], 0.0).then_inc(zero_made, 1)
            pool.wait_ge(half_made, 1)
            nc.gpsimd.tensor_copy(x_stage[:, 0], x_sb[:, 0, :]).then_inc(x_staged, 1)
            pool.wait_ge(loaded_pool, 16 * 2)
            for st in walk(w, SEGMENTS, LAYERS * NT):
                t = st.t
                if st.exists(-1):
                    w.upto(hmv_made, t)
                    nc.gpsimd.tensor_scalar(var_eps[:], mv[:, 1:2], EPS, None, ALU.add).then_inc(var_made, 1)
                    w.upto(var_made, t)
                    nc.gpsimd.tensor_tensor(out=rstd[:], in0=var_eps[:], in1=minus_half[:, 0:1], op=ALU.pow).then_inc(hrstd_made, 1)
                    nc.gpsimd.tensor_tensor(out=x_b2[:], in0=x_mid[:, st.slot(-1)], in1=b2_sb[:, st.layer(-1)], op=ALU.add).then_inc(x_b2_made, 1)
                if st.exists(3):
                    nc.gpsimd.tensor_copy(x_stage[:, st.slot(3)], x_sb[:, st.tile(3), :]).then_inc(x_staged, 1)
                if st.exists(2):
                    w.upto(norm2_made, t + 3)
                    q4 = qk[:].rearrange("p a (h d) -> p a h d", d=D2)
                    o4 = qk_sin[:].rearrange("p a (h d) -> p a h d", d=D2)
                    for lo, hi in ((0, D2 // 2), (D2 // 2, 0)):
                        nc.gpsimd.tensor_tensor(out=o4[:, :, :, lo:lo + D2 // 2], in0=q4[:, :, :, hi:hi + D2 // 2],
                                                in1=sin_sb[:, st.position(2), :, lo:lo + D2 // 2].unsqueeze(2).to_broadcast([P, 2, H2, D2 // 2]),
                                                op=ALU.mult).then_inc(sin_rnorm_made, 1)
                    nc.gpsimd.tensor_scalar(norm2_min[:], norm2[:], 1e-24, None, ALU.max).then_inc(norm2_floor, 1)
                    w.upto(norm2_floor, t + 3)
                    nc.gpsimd.tensor_tensor(out=rnorm[:], in0=norm2_min[:], in1=minus_half[:], op=ALU.pow).then_inc(sin_rnorm_made, 1)

        @block.tensor
        def _(pe):
            w = Waiter(pe)
            w.on(by_act, len(FREES["act"])), w.on(by_dve, len(FREES["dve"]))
            w.on(x_staged, 1), w.on(rotary_done, 1)
            last_in_bank = {}
            pe.wait_ge(loaded_pe[0], 16 * 4)

            def read(name, v):
                w.upto(freed_sem[FREED_BY[name]], freed[name, v])

            def begin(name, v):
                before = last_in_bank.get(BANK_OF[name])
                if before:
                    read(*before)
                last_in_bank[BANK_OF[name]] = (name, v)
                return bank(name)

            def end(instruction, name):
                instruction.then_inc(ready_sem[READY_FOR[name]], 1)

            for st in walk(w, SEGMENTS, LAYERS * NT):
                t = st.t
                if st.exists(2):
                    if t + st.skipped + 2 == NT and st.turn is None:
                        pe.wait_ge(loaded_pe[1], 16 * 4)
                    w.upto(x_staged, t + 3)
                    out = begin("xT", t + 2)
                    for k in range(NC):
                        last = nc.tensor.transpose(out[:, k * P:(k + 1) * P], x_stage[:, st.slot(2), k * P:(k + 1) * P], ident[:])
                    end(last, "xT")
                if st.exists(1):
                    w.upto(rotary_done, t + 2)
                    for a, name in enumerate(("qT", "kT")):
                        out = begin(name, t + 1)
                        for c in range(4):
                            last = nc.tensor.transpose(out[:, c * P:(c + 1) * P], qk_rot[:, a, c * P:(c + 1) * P], ident[:])
                        end(last, name)
                if st.exists(-1):
                    read("Y", t - 1)
                    out = begin("shift", t - 1)
                    last = nc.tensor.matmul(out[:, 0:P], shift_sb[:, 0], x_mid[:, st.slot(-1), P:C], start=True, stop=st.first(-1))
                    if not st.first(-1):
                        last = nc.tensor.matmul(out[:, 0:P], shift_sb[:, 1], x_mid[:, st.slot(-3), P:C], start=False, stop=True)
                    end(last, "shift")
                if st.exists(0):
                    for j in range(4):
                        read(f"S{j}", t)
                        out = begin(f"PT{j}", t)
                        for u in range(2):
                            for kb in range(1 if st.first(0) else 0, 2):
                                last = nc.tensor.transpose(out[:, (2 * u + kb) * P:(2 * u + kb + 1) * P], probs[:, j, u, kb * P:(kb + 1) * P], ident[:])
                        end(last, f"PT{j}")
                if st.exists(2):
                    read("xT", t + 2)
                    L = st.layer(2)
                    for a, name in enumerate(("q", "k", "v")):
                        out = begin(name, t + 2)
                        for k in range(NC):
                            last = nc.tensor.matmul(out[:], xT[:, st.slot(2), k * P:(k + 1) * P], wqkv_sb[:, L, k, a * INNER:(a + 1) * INNER],
                                                    start=(k == 0), stop=(k == NC - 1))
                        end(last, name)
                if st.exists(-1):
                    read("shift", t - 1)
                    out = begin("hT", t - 1)
                    for k in range(NC):
                        last = nc.tensor.transpose(out[:, k * P:(k + 1) * P], hn[:, k * P:(k + 1) * P], ident[:])
                    end(last, "hT")
                if st.exists(0):
                    for j in range(4):
                        read(f"PT{j}", t)
                    out = begin("oT", t)
                    for c in range(4):
                        for kb in range(1 if st.first(0) else 0, 2):
                            for half in range(2):
                                j, u = PLACE[2 * c + half]
                                last = nc.tensor.matmul(out[half * D2:(half + 1) * D2, c * P:(c + 1) * P],
                                                        v_sb[:, st.slot(0 if kb else -2), (2 * c + half) * D2:(2 * c + half + 1) * D2], PT[:, j, u, kb],
                                                        start=(kb == 0 or st.first(0)), stop=(kb == 1), tile_position=(0, half * D2))
                    end(last, "oT")
                if st.exists(-1):
                    read("hT", t - 1)
                    for j in range(3):
                        out = begin(f"H{j}", t - 1)
                        for i, chunk in enumerate((2 * j, 2 * j + 1, HC + 2 * j, HC + 2 * j + 1)):
                            for k in range(NC):
                                last = nc.tensor.matmul(out[:, i * P:(i + 1) * P], w1_sb[:, st.layer(-1), k, chunk * P:(chunk + 1) * P], hT[:, k],
                                                        start=(k == 0), stop=(k == NC - 1))
                        end(last, f"H{j}")
                if st.exists(1):
                    read("qT", t + 1)
                    read("kT", t + 1)
                    for j in range(4):
                        out = begin(f"S{j}", t + 1)
                        nc.tensor.matmul(out[:], identb[:], mask_sb[:].rearrange("p a k -> p (a k)"), start=True, stop=False, skip_group_check=True)
                        for u, h in enumerate(PAIRS[j]):
                            rows = slice(h % 2 * D2, (h % 2 + 1) * D2)
                            for kb in range(1 if st.first(1) else 0, 2):
                                last = nc.tensor.matmul(out[:, (2 * u + kb) * P:(2 * u + kb + 1) * P], qT[rows, h // 2, :],
                                                        kT[rows, st.slot(1 if kb else -1), h // 2, :], start=False, stop=(u == 1 and kb == 1), skip_group_check=True)
                        end(last, f"S{j}")
                if st.exists(0):
                    read("oT", t)
                    out = begin("Y", t)
                    for c in range(4):
                        last = nc.tensor.matmul(out[:, 0:C], oT[:, c], wo_sb[:, st.layer(0), c], start=(c == 0), stop=(c == 3))
                    end(last, "Y")
                if st.exists(-1):
                    for j in range(3):
                        read(f"H{j}", t - 1)
                    out = begin("F", t - 1)
                    for c in range(HC):
                        last = nc.tensor.matmul(out[:, 0:C], act_T[:, c], w2_sb[:, st.layer(-1), c], start=(c == 0), stop=(c == HC - 1))
                    end(last, "F")

        @block.scalar
        def _(act):
            w = Waiter(act)
            w.on(for_act, sum(r == "act" for r in READY_FOR.values())), w.on(max_made, 4)
            act.wait_ge(loaded_act, 48)
            act.wait_ge(zero_made, 1)

            def item(name, v):
                w.upto(for_act, ready[name, v])
                return bank(name)

            for st in walk(w, SEGMENTS, LAYERS * NT):
                t = st.t
                if st.exists(2):
                    src = item("xT", t + 2)
                    s = st.slot(2)
                    nc.scalar.copy(xT[:, s, P:P + 1], zero_col[:] if st.first(2) else xT[:, st.slot(0), 2 * P:2 * P + 1])
                    nc.scalar.copy(xT[:, s, 0:P], src[:, 0:P])
                    nc.scalar.copy(xT[:, s, P + 1:2 * P + 1], src[:, P:C]).then_inc(by_act, 1)
                if st.exists(1):
                    src = item("qT", t + 1)
                    nc.scalar.copy(qT[:].rearrange("p c t -> p (c t)"), src[:]).then_inc(by_act, 1)
                    src = item("kT", t + 1)
                    nc.scalar.copy(kT[:, st.slot(1)].rearrange("p c t -> p (c t)"), src[:]).then_inc(by_act, 1)
                if st.exists(0):
                    for j in (0, 2):
                        src = item(f"PT{j}", t).rearrange("p (u b q) -> p u b q", u=2, b=2)
                        b0 = 1 if st.first(0) else 0
                        nc.scalar.copy(PT[:, j, :, b0:], src[:, :, b0:]).then_inc(by_act, 1)
                if st.exists(2):
                    for a, name in enumerate(("q", "k")):
                        src = item(name, t + 2)
                        nc.scalar.activation(squares[:, a], src[:], ACT.Square).then_inc(squares_made, 1)
                if st.exists(-1):
                    src = item("hT", t - 1)
                    for k in range(NC):
                        last = nc.scalar.activation(hT[:, k], src[:, k * P:(k + 1) * P], ACT.Identity,
                                                    bias=lnb_sb[:, st.layer(-1), k:k + 1], scale=lng_sb[:, st.layer(-1), k:k + 1])
                    last.then_inc(by_act, 1)
                if st.exists(0):
                    src = item("oT", t)
                    nc.scalar.copy(oT[:].rearrange("p c t -> p (c t)"), src[:]).then_inc(by_act, 1)
                if st.exists(2):
                    src = item("v", t + 2)
                    nc.scalar.copy(v_sb[:, st.slot(2)], src[:]).then_inc(by_act, 1)
                if st.exists(-1):
                    for j in range(3):
                        src = item(f"H{j}", t - 1)
                        for i in range(2):
                            chunk = 2 * j + i
                            last = nc.scalar.activation(gate[:, chunk], src[:, (2 + i) * P:(3 + i) * P], ACT.Gelu,
                                                        bias=b1_sb[:, st.layer(-1), HC + chunk:HC + chunk + 1])
                        last.then_inc(gate_made, 1)
                if st.exists(1):
                    for j in range(4):
                        w.upto(max_made, 4 * (t + 1) + j + 1)
                        src = bank(f"S{j}")
                        b0 = P if st.first(1) else 0
                        for u, h in enumerate(PAIRS[j]):
                            last = nc.scalar.activation(probs[:, j, u, b0:], src[:, u * 2 * P + b0:(u + 1) * 2 * P], ACT.Exp,
                                                        bias=negmax[:, j, u:u + 1], accum_out=sums[:, j, u:u + 1])
                        last.then_inc(exps_made, 1)

        @block.vector
        def _(dve):
            w = Waiter(dve)
            w.on(for_dve, sum(r == "dve" for r in READY_FOR.values()))
            for s_, n in ((squares_made, 2), (sin_rnorm_made, 3), (gate_made, 3), (hrstd_made, 1), (x_b2_made, 1),
                          (hstats_made, 1), (cos_made, 1), (rot_made, 1), (exps_made, 4), (rsums_made, 4)):
                w.on(s_, n)
            dve.wait_ge(loaded_dve, 48)
            for l in range(LAYERS):
                nc.vector.tensor_scalar(qks8[:, l, 0], qks_sb[:, l, 0], 8.0, None, ALU.mult)
                nc.vector.tensor_scalar(qks8[:, l, 1], qks_sb[:, l, 1], 1.0, None, ALU.mult).then_inc(qscale_made, 1)
            dve.wait_ge(qscale_made, LAYERS)

            def item(name, v):
                w.upto(for_dve, ready[name, v])
                return bank(name)

            def hidden(st, j):
                t = st.t
                w.upto(gate_made, 3 * (t - 1) + j + 1)
                for i in range(2):
                    chunk = 2 * j + i
                    last = nc.vector.scalar_tensor_tensor(act_T[:, chunk], bank(f"H{j}")[:, i * P:(i + 1) * P],
                                                          b1_dve[:, st.layer(-1), chunk:chunk + 1], gate[:, chunk], ALU.add, ALU.mult)
                last.then_inc(by_dve, 1)

            for st in walk(w, SEGMENTS, LAYERS * NT):
                t = st.t
                if st.exists(-1):
                    mid, up = x_mid[:, st.slot(-1)], item("shift", t - 1)
                    nc.vector.bn_stats(stats[:, 0], mid[:, 0:P])
                    nc.vector.bn_stats(stats[:, 1], up[:, 0:P]).then_inc(hstats_made, 1)
                    if st.exists(-2) and st.layer(-2) == LAYERS - 1:
                        nc.vector.bn_stats(final_stats[:, st.tile(-2), :], x_sb[:, st.tile(-2), :])
                    w.upto(hstats_made, t)
                    nc.vector.bn_aggr(mv[:], stats[:]).then_inc(hmv_made, 1)
                if st.exists(0):
                    for j in (1, 3):
                        src = item(f"PT{j}", t).rearrange("p (u b q) -> p u b q", u=2, b=2)
                        b0 = 1 if st.first(0) else 0
                        nc.vector.tensor_copy(PT[:, j, :, b0:], src[:, :, b0:]).then_inc(by_dve, 1)
                if st.exists(-1):
                    w.upto(hrstd_made, t)
                    nc.vector.tensor_scalar(hn[:, 0:P], mid[:, 0:P], mv[:, 0:1], rstd[:], ALU.subtract, ALU.mult)
                    nc.vector.tensor_scalar(hn[:, P:C], up[:, 0:P], mv[:, 0:1], rstd[:], ALU.subtract, ALU.mult).then_inc(by_dve, 1)
                if st.exists(2):
                    for a, name in enumerate(("q", "k")):
                        w.upto(squares_made, 2 * (t + 2) + a + 1)
                        nc.vector.tensor_tensor(qk[:, a].rearrange("p (h d) -> p h d", d=D2), bank(name)[:].rearrange("p (h d) -> p h d", d=D2),
                                                qks8[:, st.layer(2), a].unsqueeze(1).to_broadcast([P, H2, D2]), ALU.mult).then_inc(by_dve, 1)
                    nc.vector.tensor_reduce(norm2[:], squares[:].rearrange("p a (h d) -> p (a h) d", d=D2), AX.X, ALU.add).then_inc(norm2_made, 1)
                if st.exists(2):
                    w.upto(sin_rnorm_made, 3 * (t + 2) + 1)
                    nc.vector.tensor_tensor(qk_cos[:].rearrange("p a (h d) -> p a h d", d=D2), qk[:].rearrange("p a (h d) -> p a h d", d=D2),
                                            cos_sb[:, st.position(2)].unsqueeze(2).to_broadcast([P, 2, H2, D2]), ALU.mult).then_inc(cos_made, 1)
                    w.upto(cos_made, t + 3)
                    w.upto(sin_rnorm_made, 3 * (t + 2) + 2)
                    nc.vector.tensor_tensor(qk_cos[:], qk_cos[:], qk_sin[:], ALU.add).then_inc(rot_made, 1)
                if st.exists(-1):
                    for j in range(3):
                        hidden(st, j)
                for j in range(4):
                    if st.exists(1):
                        src = item(f"S{j}", t + 1).rearrange("p (u k) -> p u k", u=2)
                        nc.vector.tensor_reduce(negmax[:, j], src[:, :, P if st.first(1) else 0:], AX.X, ALU.max, negate=True).then_inc(max_made, 1)
                    if j == 1 and st.exists(2):
                        w.upto(rot_made, t + 3)
                        w.upto(sin_rnorm_made, 3 * (t + 2) + 3)
                        nc.vector.tensor_tensor(qk_rot[:].rearrange("p a (h d) -> p (a h) d", d=D2), qk_cos[:].rearrange("p a (h d) -> p (a h) d", d=D2),
                                                rnorm[:].unsqueeze(2).to_broadcast([P, 2 * H2, D2]), ALU.mult).then_inc(rotary_done, 1)
                for j in range(4):
                    if st.exists(1):
                        w.upto(exps_made, 4 * (t + 1) + j + 1)
                        nc.vector.reciprocal(rsums[:, j], sums[:, j]).then_inc(rsums_made, 1)
                        w.upto(rsums_made, 4 * (t + 1) + j + 1)
                        p4 = probs[:, j, :, P if st.first(1) else 0:]
                        nc.vector.tensor_tensor(p4, p4, rsums[:, j].unsqueeze(2).to_broadcast([P, 2, P if st.first(1) else 2 * P]), ALU.mult).then_inc(by_dve, 1)
                    if j == 1 and st.exists(0):
                        src = item("Y", t)
                        nc.vector.tensor_tensor(x_mid[:, st.slot(0)], src[:, 0:C], x_sb[:, st.tile(0), :], ALU.add).then_inc(by_dve, 1)
                if st.exists(-1):
                    src = item("F", t - 1)
                    w.upto(x_b2_made, t)
                    nc.vector.tensor_tensor(x_sb[:, st.tile(-1), :], src[:, 0:C], x_b2[:], ALU.add).then_inc(by_dve, 1)


def final_phase(nc, x_sb, stats, x1_dram, out):
    with ExitStack() as ctx:
        sb = lambda n, s, d=F32: ctx.enter_context(nc.sbuf_tensor(n, s, d))
        sem = nc.alloc_semaphore
        x1_sb = sb("x1_sb", [P, NT, C])
        mv = sb("mv4", [P, NT, 2])
        var_eps = sb("var_eps4", [P, NT])
        minus_half = sb("minus_half4", [P, NT])
        rstd = sb("rstd4", [P, NT])
        nmr = sb("nmr4", [P, NT])
        CHUNKS = 4
        CH = NT // CHUNKS
        x1_loaded, out_stored = [sem(f"x1_loaded{c}") for c in range(CHUNKS)], sem("out_stored")
        stats_made, mv_made, half_made, var_made, rstd_made, nmr_made = (sem(f"{x}4_made") for x in ("stats", "mv", "half", "var", "rstd", "nmr"))
        normed, out_made = sem("x4_normed"), sem("out4_made")
        block = ctx.enter_context(nc.Block())
        out_tiles = out.rearrange("b (t p) c -> p (b t) c", p=P)

        @block.sync
        def _(sp):
            for c in range(CHUNKS):
                here = slice(c * CH, (c + 1) * CH)
                sp.dma_start(x1_sb[:, here], x1_dram[:, here]).then_inc(x1_loaded[c], 16)
            for c in range(CHUNKS):
                here = slice(c * CH, (c + 1) * CH)
                sp.wait_ge(out_made, c + 1)
                sp.dma_start(out_tiles[:, here], x1_sb[:, here]).then_inc(out_stored, 16)
            sp.wait_ge(out_stored, 16 * CHUNKS)

        @block.gpsimd
        def _(pool):
            nc.gpsimd.memset(minus_half[:], -0.5).then_inc(half_made, 1)
            pool.wait_ge(half_made, 1)
            for c in range(CHUNKS):
                here = slice(c * CH, (c + 1) * CH)
                pool.wait_ge(mv_made, (c + 1) * CH)
                nc.gpsimd.tensor_scalar(var_eps[:, here], mv[:, here, 1], EPS, None, ALU.add).then_inc(var_made, 1)
                pool.wait_ge(var_made, c + 1)
                nc.gpsimd.tensor_tensor(out=rstd[:, here], in0=var_eps[:, here], in1=minus_half[:, here], op=ALU.pow).then_inc(rstd_made, 1)

        @block.scalar
        def _(act):
            for c in range(CHUNKS):
                act.wait_ge(nmr_made, c + 1)
                with act.Fori(0, CH) as g:
                    i = c * CH + g
                    nc.scalar.activation(x_sb[:, i, :], x_sb[:, i, :], ACT.Identity, bias=nmr[:, bass.ds(i, 1)], scale=rstd[:, bass.ds(i, 1)]).then_inc(normed, 1)

        @block.vector
        def _(dve):
            nc.vector.bn_stats(stats[:, NT - 1, :], x_sb[:, NT - 1, :]).then_inc(stats_made, 1)
            dve.wait_ge(stats_made, 1)
            for i in range(NT):
                nc.vector.bn_aggr(mv[:, i, :], stats[:, i, :]).then_inc(mv_made, 1)
            for c in range(CHUNKS):
                here = slice(c * CH, (c + 1) * CH)
                dve.wait_ge(rstd_made, c + 1)
                nc.vector.scalar_tensor_tensor(nmr[:, here], mv[:, here, 0], -1.0, rstd[:, here], ALU.mult, ALU.mult).then_inc(nmr_made, 1)
            for c in range(CHUNKS):
                dve.wait_ge(x1_loaded[c], 16)
                with dve.Fori(0, CH - 1) as g:
                    dve.wait_ge(normed, 1)
                    nc.vector.tensor_tensor(x1_sb[:, c * CH + g, :], x1_sb[:, c * CH + g, :], x_sb[:, c * CH + g, :], ALU.add)
                    dve.sem_inc(normed, -1)
                i = (c + 1) * CH - 1
                dve.wait_ge(normed, 1)
                nc.vector.tensor_tensor(x1_sb[:, i, :], x1_sb[:, i, :], x_sb[:, i, :], ALU.add).then_inc(out_made, 1)
                dve.sem_inc(normed, -1)


def program(nc, ins, out):
    with ExitStack() as ctx:
        hold = lambda c, n, s, d=F32: c.enter_context(nc.sbuf_tensor(n, s, d))
        x_sb = hold(ctx, "x_sb", [P, NT, C])
        ident = hold(ctx, "ident", [P, P])
        identb = hold(ctx, "identb", [P, P], BF16)
        final_stats = hold(ctx, "final_stats", [P, NT, 6])
        mask_sb = hold(ctx, "mask_sb", [P, 2, 2 * P], BF16)
        shift_sb = hold(ctx, "shift_sb", [P, 2, P])
        x1_dram = nc.dram_tensor("x1_dram", (P, NT, C), F32).ap()
        with ExitStack() as till_fed:
            QO = hold(till_fed, "QO", [P, NH, TB, D1])
            with ExitStack() as heads:
                K1, V1 = (hold(heads, n, [P, NH, TB, D1]) for n in ("K1", "V1"))
                project_phase(nc, ins, x_sb, QO, K1, V1, ident, identb)
                attention_phase(nc, QO, K1, V1, mask_sb, shift_sb, ident, identb)
            weights = Weights(nc, till_fed)
            output_phase(nc, ins, x_sb, QO, ident, x1_dram, lambda sp: weights.load(sp, ins))
            feed_forward_phase(nc, weights, x_sb, QO[:].rearrange("p n t d -> p (n t d)"), final_stats, mask_sb, shift_sb, ident, identb)
        final_phase(nc, x_sb, final_stats, x1_dram, out)


def kernel(**inputs):
    import numpy as np
    import concourse.bacc as bacc
    from concourse.bass_utils import run_bass_kernel_spmd

    i = {k.replace("L0_", ""): np.asarray(v) for k, v in inputs.items()}
    f32 = np.float32
    pos = np.arange(T, dtype=f32)
    inv = (f32(1.0) / f32(10000.0) ** (np.arange(0, D1, 2, dtype=f32) / f32(D1))).astype(f32)
    fr = pos[:, None] * inv[None, :]
    half = np.arange(0, D2, 2, dtype=f32)
    inv2 = (f32(1.0) / f32(10000.0) ** (half / f32(D2))).astype(f32)
    fr2 = pos[:, None] * inv2[None, :]
    base = (half + f32(0.4 * D2)) / f32(1.4 * D2)
    power = (pos - f32(T // 2)) / f32(P // 2)
    scale = (base[None, :] ** power[:, None]).astype(f32)
    cos2, sin2 = np.cos(fr2), np.sin(fr2)
    qc, qs, kc, ks = cos2 * scale, sin2 * scale, cos2 / scale, sin2 / scale

    def halves(w, axis):
        parts = np.split(w, 2, axis=axis)
        pad = [(0, 0)] * w.ndim
        pad[axis] = (0, HC * P - HID)
        return np.concatenate([np.pad(p, pad) for p in parts], axis=axis)

    def by_partition(w):
        return w.reshape(LAYERS, -1, P).transpose(2, 0, 1)

    arrays = {
        "x": i["attn_x"],
        "wqkv1": np.concatenate([i["attn_Wq"].T, i["attn_Wk"].T, i["attn_Wv"].T], axis=1),
        "bqkv1": np.concatenate([i["attn_bq"], i["attn_bk"], i["attn_bv"]]),
        "cos1": np.cos(fr).astype(f32),
        "sin1": np.concatenate([-np.sin(fr), np.sin(fr)], axis=1).astype(f32),
        "wo1": i["attn_Wo"].T,
        "bo1": i["attn_bo"],
        "wqkv2": i["ffn_wqkv"],
        "wo2": i["ffn_wo"],
        "w1": halves(i["ffn_w1"], 2),
        "w2": np.pad(i["ffn_w2"], ((0, 0), (0, HC * P - HID), (0, 0))),
        "qk_scale": np.stack([i["ffn_q_scale"], i["ffn_k_scale"]], axis=1),
        "b2": i["ffn_b2"],
        "ln_g": by_partition(i["ffn_ln_g"]),
        "ln_b": by_partition(i["ffn_ln_b"]),
        "b1": by_partition(halves(i["ffn_b1"], 1)),
        "cos2": np.concatenate([qc, qc, kc, kc], axis=1).astype(f32),
        "sin2": np.concatenate([-qs, qs, -ks, ks], axis=1).astype(f32),
    }
    arrays = {k: np.ascontiguousarray(v) for k, v in arrays.items()}
    nc = bacc.Bacc("TRN2", target_bir_lowering=False, num_devices=1)
    ins = {k: nc.dram_tensor("in_" + k, v.shape, mybir.dt.from_np(v.dtype), kind="ExternalInput").ap()
           for k, v in arrays.items()}
    out = nc.dram_tensor("out_0", (B, T, C), F32, kind="ExternalOutput").ap()
    program(nc, ins, out)
    r = run_bass_kernel_spmd(nc, [{"in_" + k: v for k, v in arrays.items()}], core_ids=[0])
    return r.results[0]["out_0"]
```

```python
from contextlib import ExitStack

import concourse.bass as bass
import numpy as np
from concourse import mybir

F32 = mybir.dt.float32
BF16 = mybir.dt.bfloat16
F32R = mybir.dt.float32r
ACT = mybir.ActivationFunctionType
ALU = mybir.AluOpType
AX = mybir.AxisListType

P = 128
B, T, C = 2, 2048, 256
NT = B * T // P
TB = T // P
H1, D1 = 16, 16
NH = B * H1
NC = C // P
EPS = 1e-5



def identities(nc, block, ident, identb, made):
    @block.gpsimd
    def _(pool):
        nc.gpsimd.memset(ident[:], 0.0).then_inc(made, 1)
        pool.wait_ge(made, 1)
        nc.gpsimd.affine_select(out=ident[:], in_=ident[:], compare_op=ALU.not_equal, fill=1.0,
                                base=0, pattern=[[-1, P]], channel_multiplier=1).then_inc(made, 1)
        pool.wait_ge(made, 2)
        nc.gpsimd.tensor_copy(identb[:], ident[:]).then_inc(made, 1)


UNROLL = 4


class Step:

    def __init__(self, t, skipped, turn, tiles):
        self.t, self.skipped, self.turn = t, skipped, turn
        self.tiles = tiles

    def exists(self, d):
        return 0 <= self.t + self.skipped + d < self.tiles

    def layer(self, d):
        return (self.t + self.skipped + d) // NT

    def first(self, d):
        return self.turn is None and (self.t + self.skipped + d) % NT < 2

    def position(self, d):
        v = (self.t + self.skipped + d) % NT // 2
        return v if self.turn is None else v + UNROLL // 2 * self.turn

    def tile(self, d):
        return (self.t + self.skipped + d) % 2 * TB + self.position(d)

    def slot(self, d, n=4):
        return (self.t + d) % n


class Waiter:

    def __init__(self, eng):
        self.eng, self.sems, self.fallen = eng, {}, {}

    def on(self, sem, per_step, when=lambda step: True):
        self.sems[sem.name] = (sem, per_step, when)
        self.fallen[sem.name] = 0
        return sem

    def upto(self, sem, count):
        self.eng.wait_ge(sem, count - self.fallen[sem.name])

    def fall(self, steps):
        for sem, per_step, when in self.sems.values():
            rises = per_step * sum(when(step) for step in steps)
            if rises:
                self.eng.sem_inc(sem, -rises)
                self.fallen[sem.name] += rises


def walk(waiter, segments, tiles):
    t, skipped = segments[0][0], 0
    for first, steps, turns in segments:
        assert first == t + skipped
        if turns:
            with waiter.eng.Fori(0, turns) as turn:
                body = [Step(t + i, skipped, turn, tiles) for i in range(steps)]
                yield from body
                waiter.fall(body)
                t += steps
            skipped += (turns - 1) * steps
        else:
            for _ in range(steps):
                yield Step(t, skipped, None, tiles)
                t += 1


PROJECT_SEGMENTS = ((-4, 8, 0), (4, UNROLL, 6), (28, 5, 0))


def project_phase(nc, ins, x_sb, QO, K1, V1, ident, identb):
    with ExitStack() as ctx:
        sb = lambda n, s, d=F32: ctx.enter_context(nc.sbuf_tensor(n, s, d))
        ps = lambda n, s, d=F32: ctx.enter_context(nc.psum_tensor(n, s, d))
        sem = nc.alloc_semaphore
        HD = D1 // 2
        w_sb = sb("wqkv1_sb", [P, NC, 3 * C])
        bias_sb = sb("bqkv1_sb", [P, 3 * C])
        cos_sb = sb("cos1_sb", [P, TB, HD])
        sin_sb = sb("sin1_sb", [P, TB, 2, HD])
        stats = sb("stats0", [P, 4, 6])
        mv = sb("mv0", [P, 4, 2])
        rstd = sb("rstd0", [P, 4])
        var_eps = sb("var_eps0", [P, 4])
        minus_half = sb("minus_half0", [P, 1])
        nmr = sb("nmr0", [P, 4])
        xn = sb("xn0", [P, 4, C])
        xnT = sb("xnT0", [P, 4, C])
        qk = sb("qk0", [P, 2, 2 * C])
        qk_cos = sb("qk_cos", [P, 2, 2 * C])
        qk_sin = sb("qk_sin", [P, 2, 2 * C])
        psT = ps("psT0", [P, 2, 512])
        psQK = ps("psQK0", [P, 4, 512])
        psV = ps("psV0", [P, 2, 512])
        x_loaded = [sem(f"x_loaded{c}") for c in range(3)]
        weights_loaded, tables_loaded, sin_loaded = sem("w1_loaded"), sem("tables1_loaded"), sem("sin1_loaded")
        ident_made, stats_made, mv_made, rstd_made, nmr_made, xn_made = (sem(n) for n in ("ident_made", "stats0_made", "mv0_made", "rstd0_made", "nmr0_made", "xn0_made"))
        var_made, half_made = sem("var0_made"), sem("half0_made")
        xnT_in_psum, xnT_copied, proj_done, v_read = sem("xnT0_in_psum"), sem("xnT0_copied"), sem("proj0_done"), sem("v0_read")
        qk_biased, cos_done, sin_done = sem("qk0_biased"), sem("cos0_done"), sem("sin0_done")

        block = ctx.enter_context(nc.Block())
        identities(nc, block, ident, identb, ident_made)
        x_tiles = ins["x"].rearrange("b (t p) c -> p b t c", p=P)
        x_batches = x_sb[:].rearrange("p (b t) c -> p b t c", b=B)
        heads_of = lambda v: slice(v % 2 * H1, (v % 2 + 1) * H1)

        @block.sync
        def _(sp):
            for c, here in enumerate((slice(0, 1), slice(1, 4), slice(4, TB))):
                for b in range(B):
                    sp.dma_start(x_batches[:, b, here], x_tiles[:, b, here]).then_inc(x_loaded[c], 16)

        @block.vector
        def _(dve):
            w = Waiter(dve)
            for s_ in (stats_made, rstd_made, proj_done, qk_biased, sin_done):
                w.on(s_, 1)
            for st in walk(w, PROJECT_SEGMENTS, NT):
                t = st.t
                if st.turn is None and t in (-4, -2, 3):
                    dve.wait_ge(x_loaded[(-4, -2, 3).index(t)], 16 * B)
                if st.exists(3):
                    v, s = t + 3, st.slot(3)
                    w.upto(rstd_made, v + 1)
                    nc.vector.scalar_tensor_tensor(nmr[:, s:s + 1], mv[:, s, 0:1], -1.0, rstd[:, s:s + 1], ALU.mult, ALU.mult).then_inc(nmr_made, 1)
                if st.exists(0):
                    if t == 0 and st.turn is None:
                        dve.wait_ge(tables_loaded, 32)
                    w.upto(proj_done, t + 1)
                    nc.vector.tensor_tensor(qk[:, t % 2], psQK[:, st.slot(0)], bias_sb[:, 0:2 * C], ALU.add).then_inc(qk_biased, 1)
                    nc.vector.tensor_tensor(V1[:, heads_of(t), st.position(0), :], psV[:, t % 2, 0:C].rearrange("p (h d) -> p h d", h=H1),
                                            bias_sb[:, 2 * C:].rearrange("p (h d) -> p h d", h=H1), ALU.add).then_inc(v_read, 1)
                if st.exists(4):
                    nc.vector.bn_stats(stats[:, st.slot(4), :], x_sb[:, st.tile(4), :]).then_inc(stats_made, 1)
                if st.exists(0):
                    w.upto(qk_biased, t + 1)
                    nc.vector.tensor_tensor(qk_cos[:, t % 2].rearrange("p (h d) -> p h d", d=HD),
                                            qk[:, t % 2].rearrange("p (h d) -> p h d", d=HD),
                                            cos_sb[:, st.position(0), :].unsqueeze(1).to_broadcast([P, 4 * H1, HD]),
                                            ALU.mult).then_inc(cos_done, 1)
                if st.exists(4):
                    w.upto(stats_made, t + 5)
                    nc.vector.bn_aggr(mv[:, st.slot(4), :], stats[:, st.slot(4), :]).then_inc(mv_made, 1)
                if st.exists(-1):
                    w.upto(sin_done, t)
                    for dst, a in ((QO, 0), (K1, C)):
                        nc.vector.tensor_tensor(dst[:, heads_of(t - 1), st.position(-1), :],
                                                qk_cos[:, (t - 1) % 2, a:a + C].rearrange("p (h d) -> p h d", h=H1),
                                                qk_sin[:, (t - 1) % 2, a:a + C].rearrange("p (h d) -> p h d", h=H1), ALU.add)

        @block.gpsimd
        def _(pool):
            w = Waiter(pool)
            for s_ in (mv_made, var_made, cos_done):
                w.on(s_, 1)
            nc.gpsimd.memset(minus_half[:], -0.5).then_inc(half_made, 1)
            pool.wait_ge(half_made, 1)
            for st in walk(w, PROJECT_SEGMENTS, NT):
                if st.exists(4):
                    v, s = st.t + 4, st.slot(4)
                    w.upto(mv_made, v + 1)
                    nc.gpsimd.tensor_scalar(var_eps[:, s:s + 1], mv[:, s, 1:2], EPS, None, ALU.add).then_inc(var_made, 1)
                    w.upto(var_made, v + 1)
                    nc.gpsimd.tensor_tensor(out=rstd[:, s:s + 1], in0=var_eps[:, s:s + 1], in1=minus_half[:], op=ALU.pow).then_inc(rstd_made, 1)
                if st.exists(0):
                    if st.t == 0 and st.turn is None:
                        pool.wait_ge(sin_loaded, 16)
                    w.upto(cos_done, st.t + 1)
                    v = qk[:, st.t % 2].rearrange("p (h s d) -> p h s d", s=2, d=HD)
                    o = qk_sin[:, st.t % 2].rearrange("p (h s d) -> p h s d", s=2, d=HD)
                    for half in range(2):
                        sn = sin_sb[:, st.position(0), half, :].unsqueeze(1).to_broadcast([P, 2 * H1, HD])
                        last = nc.gpsimd.tensor_tensor(out=o[:, :, half], in0=v[:, :, 1 - half], in1=sn, op=ALU.mult)
                    last.then_inc(sin_done, 1)

        @block.tensor
        def _(pe):
            w = Waiter(pe)
            w.on(xn_made, 1), w.on(xnT_copied, 1), w.on(v_read, 1)
            pe.wait_ge(ident_made, 3)
            for st in walk(w, PROJECT_SEGMENTS, NT):
                if st.exists(1):
                    w.upto(xn_made, st.t + 2)
                    for k in range(NC):
                        last = nc.tensor.transpose(psT[:, (st.t + 1) % 2, k * P:(k + 1) * P], xn[:, st.slot(1), k * P:(k + 1) * P], ident[:])
                    last.then_inc(xnT_in_psum, 1)
                if st.exists(0):
                    s = st.slot(0)
                    if st.t == 0 and st.turn is None:
                        pe.wait_ge(weights_loaded, 16)
                    w.upto(xnT_copied, st.t + 1)
                    for k in range(NC):
                        nc.tensor.matmul(psQK[:, s], xnT[:, s, k * P:(k + 1) * P], w_sb[:, k, 0:2 * C], start=(k == 0), stop=(k == NC - 1))
                    if st.exists(-2):
                        w.upto(v_read, st.t - 1)
                    for k in range(NC):
                        last = nc.tensor.matmul(psV[:, st.t % 2, 0:C], xnT[:, s, k * P:(k + 1) * P], w_sb[:, k, 2 * C:], start=(k == 0), stop=(k == NC - 1))
                    last.then_inc(proj_done, 1)

        @block.scalar
        def _(act):
            w = Waiter(act)
            w.on(nmr_made, 1), w.on(xnT_in_psum, 1)
            act.dma_start(w_sb[:], ins["wqkv1"].rearrange("(k p) n -> p k n", p=P)).then_inc(weights_loaded, 16)
            act.dma_start(bias_sb[:], ins["bqkv1"].partition_broadcast(P)).then_inc(tables_loaded, 16)
            act.dma_start(cos_sb[:], ins["cos1"].rearrange("(t p) d -> p t d", p=P)).then_inc(tables_loaded, 16)
            act.dma_start(sin_sb[:], ins["sin1"].rearrange("(t p) (s d) -> p t s d", p=P, s=2)).then_inc(sin_loaded, 16)
            for st in walk(w, PROJECT_SEGMENTS, NT):
                if st.exists(1):
                    w.upto(xnT_in_psum, st.t + 2)
                    nc.scalar.copy(xnT[:, st.slot(1)], psT[:, (st.t + 1) % 2, 0:C]).then_inc(xnT_copied, 1)
                if st.exists(2):
                    s = st.slot(2)
                    w.upto(nmr_made, st.t + 3)
                    nc.scalar.activation(xn[:, s], x_sb[:, st.tile(2), :], ACT.Identity, bias=nmr[:, s:s + 1], scale=rstd[:, s:s + 1]).then_inc(xn_made, 1)


SLOTS = 6
STACK = SLOTS * D1
SPLIT_Q = (slice(0, 3), slice(3, 6, 2), slice(4, 5))
SPLIT_K = (slice(2, 5), slice(1, 6, 4), slice(0, 1))
AUX = 3
PROBS = 4
W2 = 1024
BODY = 3
VW = 32


def mask_and_shift(nc, pool, mask_sb, shift_sb):
    mask_made, shift_made = nc.alloc_semaphore("mask_made"), nc.alloc_semaphore("shift_made")
    nc.gpsimd.memset(shift_sb[:], 0.0).then_inc(shift_made, 1)
    pool.wait_ge(shift_made, 1)
    nc.gpsimd.affine_select(out=shift_sb[:, 0], in_=shift_sb[:, 0], compare_op=ALU.not_equal, fill=1.0,
                            base=1, pattern=[[-1, P]], channel_multiplier=1)
    nc.gpsimd.affine_select(out=shift_sb[:, 1], in_=shift_sb[:, 1], compare_op=ALU.not_equal, fill=1.0,
                            base=-(P - 1), pattern=[[-1, P]], channel_multiplier=1)
    nc.gpsimd.memset(mask_sb[:], 0.0).then_inc(mask_made, 1)
    pool.wait_ge(mask_made, 1)
    nc.gpsimd.affine_select(out=mask_sb[:, :, 0:P], in_=mask_sb[:, :, 0:P], compare_op=ALU.is_ge, fill=NO_KEY,
                            base=0, pattern=[[0, 2], [1, P]], channel_multiplier=-1)
    nc.gpsimd.affine_select(out=mask_sb[:, :, P:], in_=mask_sb[:, :, P:], compare_op=ALU.is_ge, fill=NO_KEY,
                            base=0, pattern=[[0, 2], [-1, P]], channel_multiplier=1)


def attention_phase(nc, QO, K1, V1, mask_sb, shift_sb, ident, identb):
    with ExitStack() as ctx:
        sb = lambda n, s, d=F32: ctx.enter_context(nc.sbuf_tensor(n, s, d))
        ps = lambda n, s, d=F32: ctx.enter_context(nc.psum_tensor(n, s, d))
        sem = nc.alloc_semaphore
        q_parts = sb("q_parts", [P, TB, P], BF16)
        k_parts = sb("k_parts", [P, TB, P], BF16)
        m_parts = sb("m_parts", [P, TB, 32], BF16)
        rest1 = sb("rest1", [P, 2, TB, D1])
        rest2 = sb("rest2", [P, 2, TB, D1])
        m_rest = sb("m_rest", [P, 2, TB])
        q_stack = sb("q_stack", [P, BODY, T], BF16)
        k_stack = sb("k_stack", [P, BODY, T], BF16)
        v_ones = sb("v_ones", [P, BODY, TB, VW])
        probs = sb("probs", [P, PROBS, W2])
        mx4 = sb("mx4", [P, BODY, TB, 4])
        negmax = sb("negmax", [P, BODY, TB])
        o_stage = sb("o_stage", [P, 512])
        rsum = sb("rsum", [P, BODY, TB])
        scores = ps("scores", [P, 4, 512])
        aux = ps("aux", [P, AUX, 512])
        pv = ps("pv", [P, 512])

        parts_made, parts_read = sem("parts_made"), sem("parts_read")
        consts_made, k_consts_made, split_step, first_split_step = sem("consts_made"), sem("k_consts_made"), sem("split_step"), sem("first_split_step")
        scores_ready, probs_ready = sem("scores_ready"), sem("probs_ready")
        pv_done, pv_copied, v_made = sem("pv_done"), sem("pv_copied"), sem("v_made")
        max_in_psum, max_taken = sem("max_in_psum"), sem("max_taken")
        head_max, m_parts_made = sem("head_max"), sem("m_parts_made")
        stack_in_psum, stack_copied = sem("stack_in_psum"), sem("stack_copied")
        rsum_made, maxima_written = sem("rsum_made"), sem("maxima_written")

        block = ctx.enter_context(nc.Block())

        K_STEPS, Q_STEPS, M_STEPS, O_STEP = (8, 9), (10, 11), (TB - 2, TB - 1), 2
        LEAD = 3
        DVE_ITEMS, ACT_ITEMS = 4 * TB + 1, 6

        def steps():
            return [(0, s) for s in range(LEAD, TB)] + [(1, s) for s in range(LEAD)]

        def ahead(d, s):
            return (d + 1, s + LEAD) if s < TB - LEAD else (d + 2, s + LEAD - TB)

        def aux_items(left):
            items = []
            for d, s in steps():
                a, tile = ahead(d, s)
                if d == 0 and left == 2 and s in K_STEPS + Q_STEPS:
                    items.append((d, s, "stack", (K_STEPS + Q_STEPS).index(s)))
                if d == 0 and left >= 1 and s in M_STEPS:
                    items.append((d, s, "maxrow", M_STEPS.index(s)))
                if left >= a:
                    items += [(d, s, "max", (a, tile, q)) for q in range(4)]
                if d == 1 and s == O_STEP:
                    items.append((d, s, "out", None))
            return items

        STACKS_AT = TB // 2
        PROLOGUE_ITEMS = 4 + 4 * TB + 4 + 2 + 4 * 2 * LEAD

        def banks(r, left):
            first = PROLOGUE_ITEMS + (r * len(aux_items(2)) if left == 2 else len(aux_items(1)) if left == 0 else 0)
            return [(first + i) % AUX for i in range(len(aux_items(left)))]

        assert len(aux_items(2)) == DVE_ITEMS + ACT_ITEMS and BODY * len(aux_items(2)) % AUX == 0

        def all_heads(eng, head, per_head):
            with eng.Fori(0, (NH - 2) // BODY) as m:
                for r in range(BODY):
                    head(r, m * BODY + r, 2)
                for semaphore, rises in per_head:
                    eng.sem_inc(semaphore, -BODY * rises)
            head(0, NH - 2, 1)
            head(1, NH - 1, 0)

        def split_head(engine, chain, n):
            for j, (src, parts, (hi, mid, lo)) in enumerate(((K1, k_parts, SPLIT_K), (QO, q_parts, SPLIT_Q))):
                slots = parts[:, :, 0:STACK].rearrange("p t (s d) -> p t s d", d=D1)
                x = src[:, n]
                chain(engine.tensor_copy(slots[:, :, hi, :], x.unsqueeze(2).to_broadcast([P, TB, 3, D1])))
                chain(engine.tensor_tensor(out=rest1[:, j], in0=x, in1=slots[:, :, hi.start, :], op=ALU.subtract))
                chain(engine.tensor_copy(slots[:, :, mid, :], rest1[:, j].unsqueeze(2).to_broadcast([P, TB, 2, D1])))
                chain(engine.tensor_tensor(out=rest2[:, j], in0=rest1[:, j], in1=slots[:, :, mid.start, :], op=ALU.subtract))
                engine.tensor_copy(slots[:, :, lo.start, :], rest2[:, j]).then_inc(parts_made, 1)

        @block.gpsimd
        def _(pool):
            nc.gpsimd.memset(k_parts[:, :, STACK:], 0.0).then_inc(consts_made, 1)
            pool.wait_ge(consts_made, 1)
            nc.gpsimd.memset(k_parts[:, :, STACK:STACK + 3], 1.0).then_inc(k_consts_made, 1)
            nc.gpsimd.memset(m_parts[:], 0.0).then_inc(consts_made, 1)
            nc.gpsimd.memset(v_ones[:], 0.0).then_inc(consts_made, 1)
            pool.wait_ge(consts_made, 3)
            nc.gpsimd.memset(v_ones[:, :, :, D1:D1 + 1], 1.0)

            def chain(instruction):
                instruction.then_inc(split_step, 1)
                pool.wait_ge(split_step, 1)
                pool.sem_inc(split_step, -1)

            def split_qk(r, n):
                pool.wait_ge(parts_read, r)
                split_head(nc.gpsimd, chain, n)

            def split_max_and_v(r, slot, n):
                pool.wait_ge(head_max, r + 1)
                x = negmax[:, slot]
                chain(nc.gpsimd.tensor_copy(m_parts[:, :, 0], x))
                chain(nc.gpsimd.tensor_tensor(out=m_rest[:, 0], in0=x, in1=m_parts[:, :, 0], op=ALU.subtract))
                chain(nc.gpsimd.tensor_copy(m_parts[:, :, 1], m_rest[:, 0]))
                chain(nc.gpsimd.tensor_tensor(out=m_rest[:, 1], in0=m_rest[:, 0], in1=m_parts[:, :, 1], op=ALU.subtract))
                nc.gpsimd.tensor_copy(m_parts[:, :, 2], m_rest[:, 1]).then_inc(m_parts_made, 1)
                nc.gpsimd.tensor_copy(v_ones[:, slot, :, 0:D1], V1[:, n]).then_inc(v_made, 1)

            def head(r, n, left):
                if left > 1:
                    split_qk(r + 2, n + 2)
                if left > 0:
                    split_max_and_v(r + 1, (r + 1) % BODY, n + 1)

            split_qk(1, 1)
            split_max_and_v(0, 0, 0)
            all_heads(pool, head, ((parts_read, 1), (head_max, 1)))
            mask_and_shift(nc, pool, mask_sb, shift_sb)

        @block.tensor
        def _(pe):
            ring = dict(item=0, dve=0, act=0, last=[])

            def ring_bank():
                if len(ring["last"]) == AUX:
                    pe.wait_ge(*ring["last"].pop(0))
                ring["item"] += 1
                return (ring["item"] - 1) % AUX

            def for_dve():
                ring["dve"] += 1
                ring["last"].append((max_taken, ring["dve"]))

            def for_act():
                ring["act"] += 1
                ring["last"].append((stack_copied, ring["act"]))

            def stack_item(parts, rows, row0, half):
                bank = ring_bank()
                dst = aux[row0:row0 + rows, bank].bitcast(BF16).rearrange("k (t c) -> k t c", c=P)
                for t in range(8):
                    last = nc.tensor.transpose(dst[:, t], parts[:, half * 8 + t, 0:rows], identb[:])
                last.then_inc(stack_in_psum, 1)
                for_act()

            def stack_items(r, halves=(0, 1, 2, 3)):
                for h in halves:
                    if h % 2 == 0:
                        pe.wait_ge(parts_made, 2 * r + 1 + h // 2)
                    stack_item(k_parts if h < 2 else q_parts, P if h < 2 else STACK, 0, h % 2)

            def max_item(r, half):
                pe.wait_ge(m_parts_made, r + 1)
                stack_item(m_parts, 32, STACK, half)

            def score_for_max(r, t, quarters, first_half_signals=None):
                if t == 0:
                    pe.wait_ge(stack_copied, ring["act"])
                for q in quarters:
                    bank = ring_bank()
                    lhsT = q_stack[0:STACK, r % BODY, t * P:(t + 1) * P]
                    if first_half_signals is not None and q == 0:
                        nc.tensor.matmul(aux[:, bank, 0:256], lhsT, k_stack[0:STACK, r % BODY, 0:256],
                                         start=True, stop=True).then_inc(first_half_signals, 1)
                        nc.tensor.matmul(aux[:, bank, 256:512], lhsT, k_stack[0:STACK, r % BODY, 256:512],
                                         start=True, stop=True).then_inc(max_in_psum, 1)
                    else:
                        nc.tensor.matmul(aux[:, bank], lhsT, k_stack[0:STACK, r % BODY, q * 512:(q + 1) * 512],
                                         start=True, stop=True).then_inc(max_in_psum, 1)
                    for_dve()

            def score(r, s, h, signal=None):
                unit = 2 * TB * r + 2 * s + h
                if unit >= 2:
                    pe.wait_ge(probs_ready, unit - 1)
                if s == 0:
                    pe.wait_ge(stack_copied, ring["act"])
                for j in range(2):
                    last = nc.tensor.matmul(scores[:, 2 * h + j], k_stack[:, r % BODY, s * P:(s + 1) * P],
                                            q_stack[:, r % BODY, (2 * h + j) * 512:(2 * h + j + 1) * 512], start=True, stop=True)
                    if j == 0 and signal is not None:
                        last.then_inc(signal, 1)
                last.then_inc(scores_ready, 1)

            def weigh(r, s):
                if s == 0:
                    pe.wait_ge(v_made, r + 1)
                    if r:
                        pe.wait_ge(pv_copied, r)
                pe.wait_ge(probs_ready, 2 * TB * r + 2 * s + 2)
                for j in range(4):
                    last = nc.tensor.matmul(pv[VW * j:VW * (j + 1), :], v_ones[:, r % BODY, s, :],
                                            probs[:, (2 * s + j // 2) % PROBS, (j % 2) * 512:(j % 2 + 1) * 512],
                                            start=(s == 0), stop=(s == TB - 1), tile_position=(0, VW * j))
                last.then_inc(pv_done, 1)

            def output_item(r):
                pe.wait_ge(pv_copied, r + 1)
                bank = ring_bank()
                for c in range(4):
                    last = nc.tensor.transpose(aux[:, bank, c * P:(c + 1) * P], o_stage[:, c * P:(c + 1) * P], ident[:])
                last.then_inc(max_in_psum, 1)
                for_dve()

            def step(r, d, s, left):
                ahead_d, tile = ahead(d, s)
                scored, maxima = left >= d, left >= ahead_d
                here = r + d
                if d == 0 and left == 2 and s in K_STEPS + Q_STEPS:
                    stack_items(r + 2, [(K_STEPS + Q_STEPS).index(s)])
                if d == 0 and left >= 1 and s in M_STEPS:
                    max_item(r + 1, M_STEPS.index(s))
                if scored:
                    score(here, s, 0)
                if maxima:
                    score_for_max(r + ahead_d, tile, (0, 1))
                if scored:
                    score(here, s, 1, parts_read if d == 0 and left == 2 and s == Q_STEPS[1] else None)
                if maxima:
                    score_for_max(r + ahead_d, tile, (2,))
                if s == 0:
                    weigh(here - 1, TB - 1)
                elif scored:
                    weigh(here, s - 1)
                if maxima:
                    score_for_max(r + ahead_d, tile, (3,))
                if d == 1 and s == O_STEP:
                    output_item(r)

            def head(r, n, left):
                if r == 0:
                    ring.update(start, last=list(start["last"]))
                assert ring["item"] % AUX == banks(r, left)[0]
                for d, s in steps():
                    step(r, d, s, left)

            pe.wait_ge(k_consts_made, 1)
            stack_items(0)
            for t in range(TB):
                if STACKS_AT <= t < STACKS_AT + 4:
                    stack_items(1, (t - STACKS_AT,))
                score_for_max(0, t, range(4), parts_read if t == 0 else None)
            for t in range(LEAD):
                score_for_max(1, t, range(4))
                if t == 0:
                    max_item(0, 0)
                    max_item(0, 1)
            for s in range(LEAD):
                score(0, s, 0)
                score_for_max(1, s + LEAD, (0, 1))
                score(0, s, 1, parts_read if s == 0 else None)
                score_for_max(1, s + LEAD, (2, 3))
                if s:
                    weigh(0, s - 1)
            start = dict(ring, last=list(ring["last"]))
            all_heads(pe, head, ((parts_made, 2), (m_parts_made, 1), (v_made, 1), (pv_copied, 1), (probs_ready, 2 * TB),
                                 (max_taken, DVE_ITEMS), (stack_copied, ACT_ITEMS)))

        @block.scalar
        def _(act):
            copied = [0]

            def copy_stack_item(dst, bank, rows, row0):
                copied[0] += 1
                act.wait_ge(stack_in_psum, copied[0])
                nc.scalar.copy(dst, aux[row0:row0 + rows, bank].bitcast(BF16)).then_inc(stack_copied, 1)

            def copy_stack(slot, part, bank):
                stack, rows = (k_stack, P) if part < 2 else (q_stack, STACK)
                copy_stack_item(stack[0:rows, slot, part % 2 * W2:(part % 2 + 1) * W2], bank, rows, 0)

            def copy_maxima(slot, half, bank):
                copy_stack_item(q_stack[STACK:P, slot, half * W2:(half + 1) * W2], bank, P - STACK, STACK)

            def exponentiate(r, s, h):
                unit = 2 * TB * r + 2 * s + h
                act.wait_ge(scores_ready, unit + 1)
                if TB * r + s >= 2:
                    act.wait_ge(pv_done, TB * r + s - 1)
                nc.scalar.activation(probs[:, unit % PROBS], scores[:, 2 * h:2 * h + 2].rearrange("p a n -> p (a n)"),
                                     ACT.Exp, scale=float(D1) ** -0.5).then_inc(probs_ready, 1)

            def head(r, n, left):
                if r == 0:
                    copied[0] = start
                items, bank_of = aux_items(left), banks(r, left)
                for d, s in steps():
                    here = [(kind, what, bank) for (di, si, kind, what), bank in zip(items, bank_of) if (di, si) == (d, s)]
                    for kind, what, bank in here:
                        if kind == "stack":
                            copy_stack((r + 2) % BODY, what, bank)
                        if kind == "maxrow":
                            copy_maxima((r + 1) % BODY, what, bank)
                    if left >= d:
                        exponentiate(r + d, s, 0)
                        exponentiate(r + d, s, 1)
                    if (d, s) == (1, 0):
                        act.wait_ge(pv_done, TB * (r + 1))
                        nc.scalar.copy(o_stage[:], pv[:]).then_inc(pv_copied, 1)

            for part in range(4):
                copy_stack(0, part, part % AUX)
            for part in range(4):
                copy_stack(1, part, (4 + 4 * (STACKS_AT + part) + part) % AUX)
            for half in range(2):
                copy_maxima(0, half, (8 + 4 * TB + 4 + half) % AUX)
            for s in range(LEAD):
                exponentiate(0, s, 0)
                exponentiate(0, s, 1)
            start = copied[0]
            all_heads(act, head, ((stack_in_psum, ACT_ITEMS), (scores_ready, 2 * TB), (pv_done, TB)))

        @block.vector
        def _(dve):
            taken = [0]

            def next_item():
                taken[0] += 1
                dve.wait_ge(max_in_psum, taken[0])

            def take_max(slot, tile, quarter, bank):
                next_item()
                nc.vector.reduce_max(mx4[:, slot, tile, quarter:quarter + 1], aux[:, bank], AX.X).then_inc(max_taken, 1)
                if (tile, quarter) == (TB - 1, 3):
                    dve.drain().then_inc(maxima_written, 1)
                    dve.wait_ge(maxima_written, 1)
                    dve.sem_inc(maxima_written, -1)
                    nc.vector.tensor_reduce(negmax[:, slot], mx4[:, slot], AX.X, ALU.max, negate=True).then_inc(head_max, 1)

            def write_output(r, n, bank):
                next_item()
                item = aux[:, bank].rearrange("p (c j d) -> p c j d", c=4, j=4)
                nc.vector.reciprocal(rsum[:, r].rearrange("p (c j) -> p c j", c=4), item[:, :, :, D1]).then_inc(rsum_made, 1)
                dve.wait_ge(rsum_made, 1)
                dve.sem_inc(rsum_made, -1)
                nc.vector.tensor_tensor(QO[:, n].rearrange("p (j c) d -> p c j d", j=4), item[:, :, :, 0:D1],
                                        rsum[:, r].rearrange("p (c j) -> p c j", c=4).unsqueeze(3).to_broadcast([P, 4, 4, D1]),
                                        ALU.mult).then_inc(max_taken, 1)

            def head(r, n, left):
                if r == 0:
                    taken[0] = start
                for (d, s, kind, what), bank in zip(aux_items(left), banks(r, left)):
                    if kind == "max":
                        take_max((r + what[0]) % BODY, what[1], what[2], bank)
                    if kind == "out":
                        write_output(r, n, bank)

            def first_chain(instruction):
                instruction.then_inc(first_split_step, 1)
                dve.wait_ge(first_split_step, 1)
                dve.sem_inc(first_split_step, -1)

            split_head(nc.vector, first_chain, 0)
            at = 4
            for t in range(TB):
                at += STACKS_AT <= t < STACKS_AT + 4
                for q in range(4):
                    take_max(0, t, q, (at + 4 * t + q) % AUX)
            at += 4 * TB
            for t in range(2 * LEAD):
                at += 2 if t == 1 else 0
                for q in range(4):
                    take_max(1, t, q, (at + 4 * t + q) % AUX)
            start = taken[0]
            all_heads(dve, head, ((max_in_psum, DVE_ITEMS),))


OUT_SEGMENTS = ((-2, 7, 0), (5, UNROLL, 6), (29, 8, 0))


def output_phase(nc, ins, x_sb, QO, ident, x1_dram, load_weights):
    with ExitStack() as ctx:
        sb = lambda n, s, d=F32: ctx.enter_context(nc.sbuf_tensor(n, s, d))
        ps = lambda n, s, d=F32: ctx.enter_context(nc.psum_tensor(n, s, d))
        sem = nc.alloc_semaphore
        w_sb = sb("wo1_sb", [P, NC, C])
        bias_sb = sb("bo1_sb", [P, C])
        x1_sb = sb("x1_made_sb", [P, B, TB, C])
        o_tile = sb("o_tile", [P, 4, C])
        oT = sb("oT2", [P, 4, C])
        y_normed = sb("y_normed", [P, 4, C])
        stats = sb("stats2", [P, 2, 4, 6])
        mv = sb("mv2", [P, 2, 4, 2])
        var_eps = sb("var_eps2", [P, 2, 4])
        minus_half = sb("minus_half2", [P, 1])
        rstd = sb("rstd2", [P, 2, 4])
        nmr = sb("nmr2", [P, 2, 4])
        psT = ps("psT2", [P, 4, 512])
        psY = ps("psY2", [P, 4, 512])
        weights_loaded, x1_stored = sem("wo1_loaded"), sem("x1_stored")
        o_made, oT_in_psum, oT_copied, y_done = sem("o2_made"), sem("oT2_in_psum"), sem("oT2_copied"), sem("y2_done")
        half_made, y_normed_made, x1_written, x1_normed = sem("half2_made"), sem("y2_normed_made"), sem("x1_written"), sem("x1_normed")
        stats_made, mv_made, var_made, rstd_made, nmr_made = ([sem(f"{x}2{j}_made") for j in range(2)] for x in ("stats", "mv", "var", "rstd", "nmr"))
        STORES = (0, 6, 11, 14, TB)
        x1_out = x1_dram.rearrange("p (b t) c -> p b t c", b=B)

        block = ctx.enter_context(nc.Block())

        @block.sync
        def _(sp):
            sp.dma_start(w_sb[:], ins["wo1"].rearrange("(k p) n -> p k n", p=P)).then_inc(weights_loaded, 16)
            sp.dma_start(bias_sb[:], ins["bo1"].partition_broadcast(P)).then_inc(weights_loaded, 16)
            load_weights(sp)
            for start, end in zip(STORES, STORES[1:]):
                sp.wait_ge(x1_normed, B * end)
                sp.dma_start(x1_out[:, :, start:end], x1_sb[:, :, start:end]).then_inc(x1_stored, 16)
            sp.wait_ge(x1_stored, 16 * (len(STORES) - 1))

        @block.gpsimd
        def _(pool):
            w = Waiter(pool)
            w.on(mv_made[0], 1), w.on(mv_made[1], 1), w.on(var_made[0], 1), w.on(var_made[1], 1)
            nc.gpsimd.memset(minus_half[:], -0.5).then_inc(half_made, 1)
            pool.wait_ge(half_made, 1)
            for st in walk(w, OUT_SEGMENTS, NT):
                for j, d in ((0, 0), (1, -3)):
                    if st.exists(d):
                        v, s = st.t + d, st.slot(d)
                        w.upto(mv_made[j], v + 1)
                        nc.gpsimd.tensor_scalar(var_eps[:, j, s:s + 1], mv[:, j, s, 1:2], EPS, None, ALU.add).then_inc(var_made[j], 1)
                        w.upto(var_made[j], v + 1)
                        nc.gpsimd.tensor_tensor(out=rstd[:, j, s:s + 1], in0=var_eps[:, j, s:s + 1], in1=minus_half[:], op=ALU.pow).then_inc(rstd_made[j], 1)

        @block.tensor
        def _(pe):
            w = Waiter(pe)
            w.on(o_made, 1), w.on(oT_copied, 1)
            pe.wait_ge(weights_loaded, 32)
            for st in walk(w, OUT_SEGMENTS, NT):
                if st.exists(1):
                    s = st.slot(1)
                    w.upto(o_made, st.t + 2)
                    for k in range(NC):
                        last = nc.tensor.transpose(psT[:, s, k * P:(k + 1) * P], o_tile[:, s, k * P:(k + 1) * P], ident[:])
                    last.then_inc(oT_in_psum, 1)
                if st.exists(0):
                    s = st.slot(0)
                    w.upto(oT_copied, st.t + 1)
                    nc.tensor.matmul(psY[:, s, 0:C], ident[:], bias_sb[:], start=True, stop=False)
                    for k in range(NC):
                        last = nc.tensor.matmul(psY[:, s, 0:C], oT[:, s, k * P:(k + 1) * P], w_sb[:, k], start=False, stop=(k == NC - 1))
                    last.then_inc(y_done, 1)

        @block.scalar
        def _(act):
            w = Waiter(act)
            w.on(oT_in_psum, 1), w.on(nmr_made[0], 1), w.on(nmr_made[1], 1)

            def normalise(dst, src, j, s, made):
                nc.scalar.activation(dst, src, ACT.Identity, bias=nmr[:, j, s:s + 1], scale=rstd[:, j, s:s + 1]).then_inc(made, 1)

            for st in walk(w, OUT_SEGMENTS, NT):
                if st.exists(1):
                    w.upto(oT_in_psum, st.t + 2)
                    nc.scalar.copy(oT[:, st.slot(1)], psT[:, st.slot(1), 0:C]).then_inc(oT_copied, 1)
                if st.exists(2):
                    b = (st.t + 2) % 2
                    nc.scalar.copy(o_tile[:, st.slot(2)].rearrange("p (h d) -> p h d", d=D1),
                                   QO[:, b * H1:(b + 1) * H1, st.position(2), :]).then_inc(o_made, 1)
                if st.exists(-2):
                    w.upto(nmr_made[0], st.t - 1)
                    normalise(y_normed[:, st.slot(-2)], psY[:, st.slot(-2), 0:C], 0, st.slot(-2), y_normed_made)
                if st.exists(-5):
                    w.upto(nmr_made[1], st.t - 4)
                    normalise(x_sb[:, st.tile(-5), :], x1_sb[:, (st.t - 5) % 2, st.position(-5), :], 1, st.slot(-5), x1_normed)

        @block.vector
        def _(dve):
            w = Waiter(dve)
            for s_ in (y_done, y_normed_made, x1_written, *stats_made, *rstd_made):
                w.on(s_, 1)

            def minus_mean_rstd(j, v, s):
                w.upto(rstd_made[j], v + 1)
                nc.vector.scalar_tensor_tensor(nmr[:, j, s:s + 1], mv[:, j, s, 0:1], -1.0, rstd[:, j, s:s + 1], ALU.mult, ALU.mult).then_inc(nmr_made[j], 1)

            def statistics(j, v, s, src):
                nc.vector.bn_stats(stats[:, j, s, :], src).then_inc(stats_made[j], 1)

            def mean_and_variance(j, v, s):
                w.upto(stats_made[j], v + 1)
                nc.vector.bn_aggr(mv[:, j, s, :], stats[:, j, s, :]).then_inc(mv_made[j], 1)

            for st in walk(w, OUT_SEGMENTS, NT):
                t = st.t
                if st.exists(0):
                    w.upto(y_done, t + 1)
                    statistics(0, t, st.slot(0), psY[:, st.slot(0), 0:C])
                if st.exists(-3):
                    w.upto(y_normed_made, t - 2)
                    x1_tile = x1_sb[:, (t - 3) % 2, st.position(-3), :]
                    nc.vector.tensor_tensor(x1_tile, y_normed[:, st.slot(-3)], x_sb[:, st.tile(-3), :], ALU.add).then_inc(x1_written, 1)
                if st.exists(0):
                    mean_and_variance(0, t, st.slot(0))
                if st.exists(-1):
                    minus_mean_rstd(0, t - 1, st.slot(-1))
                if st.exists(-4):
                    minus_mean_rstd(1, t - 4, st.slot(-4))
                if st.exists(-3):
                    w.upto(x1_written, t - 2)
                    statistics(1, t - 3, st.slot(-3), x1_tile)
                    mean_and_variance(1, t - 3, st.slot(-3))


LAYERS = 2
SPLIT_STEPS = (-2, -1)
H2, D2 = 8, 64
INNER = H2 * D2
HID = 682
HW = HID // P
HR = P // 2
HC = HW + 1
assert HID % P <= HR
W1_CHUNKS = 2 * HW + 1
NO_KEY = -1e30
PAIRS = ((0, 2), (4, 6), (1, 3), (5, 7))
PLACE = {h: (j, u) for j, pair in enumerate(PAIRS) for u, h in enumerate(pair)}
BANKS = 8
ITEMS = ([("xT", 2, "act", 0), ("qT", 1, "act", 1), ("kT", 1, "act", 2), ("shift", -1, "dve", 3)]
         + [(f"PT{j}", 0, "act" if j % 2 == 0 else "dve", 4 + j) for j in range(4)]
         + [("q", 2, "act", 0), ("k", 2, "act", 1), ("v", 2, "act", 2), ("hT", -1, "act", 3), ("oT", 0, "act", 0)]
         + [(f"H{j}", -1, "act", 1 + j) for j in range(3)]
         + [(f"S{j}", 1, "dve", 4 + j) for j in range(4)]
         + [("Y", 0, "dve", 2), ("F", -1, "dve", 3)])
TILE_OF = {name: d for name, d, _, _ in ITEMS}
READY_FOR = {name: r for name, _, r, _ in ITEMS}
BANK_OF = {name: b for name, _, _, b in ITEMS}
FREES = {"act": ["qT", "kT", "PT0", "PT2", "hT", "oT", "v"],
         "dve": ["xT", "PT1", "PT3", "shift", "q", "k", "H0", "H1", "H2", "S0", "S1", "Y", "S2", "S3", "F"]}
FREED_BY = {name: r for r, names in FREES.items() for name in names}
SEGMENTS = ((-2, 5, 0), (3, UNROLL, 6), (27, 8, 0), (35, UNROLL, 6), (59, 8, 0))


def last_layer(d):
    return lambda step: step.exists(d) and step.layer(d) == LAYERS - 1


def nth_last(step, d):
    before = sum((turns - 1) * steps for first, steps, turns in SEGMENTS if turns and first < NT)
    return step.t + before + d - (LAYERS - 1) * NT


def item_counts():
    ready, freed, n = {}, {}, {"ready": {"act": 0, "dve": 0}, "freed": {"act": 0, "dve": 0}}
    t, skipped = SEGMENTS[0][0], 0
    for first, steps, turns in SEGMENTS:
        for _ in range(steps):
            step = Step(t, skipped, None, LAYERS * NT)
            for name, d, reader, _ in ITEMS:
                if step.exists(d):
                    n["ready"][reader] += 1
                    ready[name, t + d] = n["ready"][reader]
            for reader, names in FREES.items():
                for name in names:
                    if step.exists(TILE_OF[name]):
                        n["freed"][reader] += 1
                        freed[name, t + TILE_OF[name]] = n["freed"][reader]
            t += 1
        skipped += (turns - 1) * steps if turns else 0
    return ready, freed


class Weights:

    def __init__(self, nc, ctx):
        sb = lambda n, s, d=F32: ctx.enter_context(nc.sbuf_tensor(n, s, d))
        sem = nc.alloc_semaphore
        self.wqkv = sb("wqkv2_sb", [P, LAYERS, NC, 3 * INNER])
        self.wo = sb("wo2_sb", [P, LAYERS, INNER // P, C])
        self.w1 = sb("w1_sb", [P, LAYERS, NC, W1_CHUNKS * P])
        self.w2 = sb("w2_sb", [P, LAYERS, HC, C])
        self.qk_scale = sb("qk_scale_sb", [P, LAYERS, 2, D2])
        self.cos = sb("cos2_sb", [P, TB, 2, D2 // 2])
        self.sin = sb("sin2_sb", [P, TB, 2, D2 // 2])
        self.ln_g = sb("ln_g_sb", [P, LAYERS, NC])
        self.ln_b = sb("ln_b_sb", [P, LAYERS, NC])
        self.b1 = sb("b1_sb", [P, LAYERS, W1_CHUNKS])
        self.b1_dve = sb("b1_dve", [P, LAYERS, W1_CHUNKS])
        self.b2 = sb("b2_sb", [P, LAYERS, C])
        self.loaded_pe = [sem(f"weights{l}_loaded") for l in range(LAYERS)]
        self.x1_loaded = [sem(f"x1_loaded{c}") for c in range(4)]
        self.loaded_act, self.loaded_dve, self.loaded_pool = (sem(f"loaded3_{x}") for x in ("act", "dve", "pool"))

    def x1_places(self, free_space):
        places, at = [], 0
        spaces = [t[:, 0].rearrange("p k n -> p (k n)") for t in (self.w1, self.w2, self.wo)] + [free_space]
        for space, loaded in zip(spaces, self.x1_loaded):
            n = min(space.shape[1] // C, NT - at)
            places.append((slice(at, at + n), space[:, 0:n * C].rearrange("p (t c) -> p t c", c=C), loaded))
            at += n
        assert at == NT
        return places

    def load(self, sp, ins):
        def rows_last(name, l):
            return ins[name][l].rearrange("(k p) n -> p k n", p=P)

        for l in range(LAYERS):
            for name, tile in (("wqkv2", self.wqkv), ("wo2", self.wo), ("w1", self.w1), ("w2", self.w2)):
                sp.dma_start(tile[:, l], rows_last(name, l)).then_inc(self.loaded_pe[l], 16)
            if l == 0:
                sp.dma_start(self.cos[:], ins["cos2"].rearrange("(t p) (a d) -> p t a d", p=P, a=2)).then_inc(self.loaded_dve, 16)
                sp.dma_start(self.sin[:], ins["sin2"].rearrange("(t p) (a d) -> p t a d", p=P, a=2)).then_inc(self.loaded_pool, 16)
                for name, tile, loaded in (("qk_scale", self.qk_scale, self.loaded_dve), ("b2", self.b2, self.loaded_pool)):
                    sp.dma_start(tile[:], ins[name].partition_broadcast(P)).then_inc(loaded, 16)
                for name, tile, loaded in (("ln_g", self.ln_g, self.loaded_act), ("ln_b", self.ln_b, self.loaded_act),
                                           ("b1", self.b1, self.loaded_act), ("b1", self.b1_dve, self.loaded_dve)):
                    sp.dma_start(tile[:], ins[name]).then_inc(loaded, 16)


def feed_forward_phase(nc, weights, x_sb, free_space, x1_dram, x1_places, mask_sb, shift_sb, ident, identb):
    with ExitStack() as ctx:
        sb = lambda n, s, d=F32: ctx.enter_context(nc.sbuf_tensor(n, s, d))
        sem = nc.alloc_semaphore
        wqkv_sb, wo_sb, w1_sb, w2_sb = weights.wqkv, weights.wo, weights.w1, weights.w2
        qks_sb, cos_sb, sin_sb, b2_sb = weights.qk_scale, weights.cos, weights.sin, weights.b2
        lng_sb, lnb_sb, b1_sb, b1_dve = weights.ln_g, weights.ln_b, weights.b1, weights.b1_dve

        def buffers_in(space):
            used = [0]

            def take(*shape):
                n = int(np.prod(shape))
                view = space[:, used[0]:used[0] + n]
                used[0] += n
                assert used[0] <= space.shape[1]
                names = "abcd"[:len(shape)]
                return view.rearrange(f"p ({' '.join(names)}) -> p {' '.join(names)}", **dict(zip(names, shape)))
            return take

        in_free = buffers_in(free_space)
        after_split = [buffers_in(wqkv_sb[:, l].rearrange("p k n -> p (k n)")) for l in range(LAYERS)]
        zero_col = sb("zero_col", [P, 1])
        minus_half = sb("minus_half3", [P, 2 * H2])
        x_stage = in_free(2, C)
        xT_hi, xT_lo = sb("xT3_hi", [P, 2, 2 * P], F32R), sb("xT3_lo", [P, 2, 2 * P], F32R)
        carry_hi, carry_lo = sb("carry_hi", [P, 4, 1], F32R), sb("carry_lo", [P, 4, 1], F32R)
        wqkv_hi = sb("wqkv3_hi", [P, LAYERS, NC, 3 * INNER], F32R)
        wqkv_lo = sb("wqkv3_lo", [P, LAYERS, NC, 3 * INNER], F32R)
        squares = in_free(2, INNER)
        qk = in_free(2, INNER)
        qk_cos = in_free(2, INNER)
        qk_sin = in_free(2, INNER)
        qk_rot = squares
        norm2 = sb("norm2", [P, 2 * H2])
        norm2_min = sb("norm2_min", [P, 2 * H2])
        rnorm = sb("rnorm", [P, 2 * H2])
        qT = after_split[0](4, P)
        kT = sb("kT3", [P, 4, 4, P])
        v_sb = in_free(4, INNER)
        probs = after_split[0](4, 2, 2 * P)
        negmax = sb("negmax3", [P, 4, 2])
        sums = sb("sums3", [P, 4, 2])
        rsums = sb("rsums3", [P, 4, 2])
        PT = after_split[1](4, 2, 2, P)
        oT = after_split[0](4, P)
        x_mid = in_free(4, C)
        stats = sb("stats3", [P, 2, 6])
        mv = sb("mv3", [P, 2])
        var_eps = sb("var_eps3", [P, 1])
        rstd = sb("rstd3", [P, 1])
        fstats = sb("fstats", [P, 4, 6])
        fmv = sb("fmv", [P, 4, 2])
        fvar_eps = sb("fvar_eps", [P, 1])
        frstd = sb("frstd", [P, 4, 1])
        fnmr = sb("fnmr", [P, 4, 1])
        hn = after_split[1](C)
        hT = in_free(NC, P)
        gate = after_split[1](HC, P)
        act_T = gate
        ps = [ctx.enter_context(nc.psum_tensor(f"bank{b}", [P, 512], F32)) for b in range(BANKS)]
        bank = lambda name: ps[BANK_OF[name]]

        for_act, for_dve = sem("items_for_act"), sem("items_for_dve")
        by_act, by_dve = sem("read_by_act"), sem("read_by_dve")
        ready_sem, freed_sem = {"act": for_act, "dve": for_dve}, {"act": by_act, "dve": by_dve}
        loaded_pe, loaded_act, loaded_dve, loaded_pool = weights.loaded_pe, weights.loaded_act, weights.loaded_dve, weights.loaded_pool
        zero_made, half_made, qscale_made = (sem(f"{x}3_made") for x in ("zero", "half", "qscale"))
        x_staged, rotary_done = sem("x_staged"), sem("rotary_done")
        squares_made, norm2_made, sin_rnorm_made = sem("squares_made"), sem("norm2_made"), sem("sin_rnorm_made")
        cos_made, rot_made = sem("cos3_made"), sem("rot3_made")
        max_made, exps_made, rsums_made = sem("max3_made"), sem("exps3_made"), sem("rsums3_made")
        hstats_made, hmv_made, hrstd_made = sem("hstats_made"), sem("hmv_made"), sem("hrstd_made")
        gate_made, x_b2_made, norm2_floor, var_made = sem("gate_made"), sem("x_b2_made"), sem("norm2_floor_made"), sem("var3_made")
        wqkv_rounded, wqkv_split, xT_rounded = sem("wqkv_rounded"), sem("wqkv_split"), sem("xT_rounded")
        fstats_made, fmv_made, fvar_made, frstd_made, fnmr_made = (sem(f"{x}_made") for x in ("fstats", "fmv", "fvar", "frstd", "fnmr"))
        first_layer_done, last_x_written = sem("first_layer_done"), sem("last_x_written")
        ready, freed = item_counts()

        block = ctx.enter_context(nc.Block())

        @block.sync
        def _(sp):
            sp.wait_ge(first_layer_done, 1)
            for tiles, place, loaded in x1_places[:-1]:
                sp.dma_start(place, x1_dram[:, tiles]).then_inc(loaded, 16)

        @block.gpsimd
        def _(pool):
            w = Waiter(pool)
            w.on(norm2_made, 1), w.on(hmv_made, 1)
            w.on(norm2_floor, 1), w.on(var_made, 1)
            w.on(fmv_made, 1, last_layer(-2)), w.on(fvar_made, 1, last_layer(-2))
            nc.gpsimd.memset(minus_half[:], -0.5).then_inc(half_made, 1)
            nc.gpsimd.memset(zero_col[:], 0.0).then_inc(zero_made, 1)
            pool.wait_ge(half_made, 1)
            nc.gpsimd.tensor_copy(x_stage[:, 0], x_sb[:, 0, :]).then_inc(x_staged, 1)
            pool.wait_ge(loaded_pool, 16 * 2)
            for st in walk(w, SEGMENTS, LAYERS * NT):
                t = st.t
                if st.exists(-1):
                    w.upto(hmv_made, t)
                    nc.gpsimd.tensor_scalar(var_eps[:], mv[:, 1:2], EPS, None, ALU.add).then_inc(var_made, 1)
                    w.upto(var_made, t)
                    nc.gpsimd.tensor_tensor(out=rstd[:], in0=var_eps[:], in1=minus_half[:, 0:1], op=ALU.pow).then_inc(hrstd_made, 1)
                    nc.gpsimd.tensor_tensor(out=x_sb[:, st.tile(-1), :], in0=x_mid[:, st.slot(-1)], in1=b2_sb[:, st.layer(-1)], op=ALU.add).then_inc(x_b2_made, 1)
                if last_layer(-2)(st):
                    n = nth_last(st, -2)
                    w.upto(fmv_made, n + 1)
                    nc.gpsimd.tensor_scalar(fvar_eps[:], fmv[:, st.slot(-2), 1:2], EPS, None, ALU.add).then_inc(fvar_made, 1)
                    w.upto(fvar_made, n + 1)
                    nc.gpsimd.tensor_tensor(out=frstd[:, st.slot(-2)], in0=fvar_eps[:], in1=minus_half[:, 0:1], op=ALU.pow).then_inc(frstd_made, 1)
                if st.exists(3):
                    nc.gpsimd.tensor_copy(x_stage[:, st.slot(3, 2)], x_sb[:, st.tile(3), :]).then_inc(x_staged, 1)
                if st.exists(2):
                    w.upto(norm2_made, t + 3)
                    q4 = qk[:].rearrange("p a (h d) -> p a h d", d=D2)
                    o4 = qk_sin[:].rearrange("p a (h d) -> p a h d", d=D2)
                    for lo, hi in ((0, D2 // 2), (D2 // 2, 0)):
                        nc.gpsimd.tensor_tensor(out=o4[:, :, :, lo:lo + D2 // 2], in0=q4[:, :, :, hi:hi + D2 // 2],
                                                in1=sin_sb[:, st.position(2)].unsqueeze(2).to_broadcast([P, 2, H2, D2 // 2]),
                                                op=ALU.mult).then_inc(sin_rnorm_made, 1)
                    nc.gpsimd.tensor_scalar(norm2_min[:], norm2[:], 1e-24, None, ALU.max).then_inc(norm2_floor, 1)
                    w.upto(norm2_floor, t + 3)
                    nc.gpsimd.tensor_tensor(out=rnorm[:], in0=norm2_min[:], in1=minus_half[:], op=ALU.pow).then_inc(sin_rnorm_made, 1)

        @block.tensor
        def _(pe):
            w = Waiter(pe)
            w.on(by_act, len(FREES["act"])), w.on(by_dve, len(FREES["dve"]))
            w.on(x_staged, 1), w.on(rotary_done, 1)
            last_in_bank = {}
            pe.wait_ge(loaded_pe[0], 16 * 4)

            def read(name, v):
                w.upto(freed_sem[FREED_BY[name]], freed[name, v])

            def begin(name, v):
                before = last_in_bank.get(BANK_OF[name])
                if before:
                    read(*before)
                last_in_bank[BANK_OF[name]] = (name, v)
                return bank(name)

            def end(instruction, name):
                instruction.then_inc(ready_sem[READY_FOR[name]], 1)

            for st in walk(w, SEGMENTS, LAYERS * NT):
                t = st.t
                if st.exists(2):
                    if t + st.skipped + 2 == NT and st.turn is None:
                        pe.wait_ge(loaded_pe[1], 16 * 4)
                    w.upto(x_staged, t + 3)
                    out = begin("xT", t + 2)
                    for k in range(NC):
                        last = nc.tensor.transpose(out[:, k * P:(k + 1) * P], x_stage[:, st.slot(2, 2), k * P:(k + 1) * P], ident[:])
                    end(last, "xT")
                if st.exists(1):
                    w.upto(rotary_done, t + 2)
                    for a, name in enumerate(("qT", "kT")):
                        out = begin(name, t + 1)
                        for c in range(4):
                            last = nc.tensor.transpose(out[:, c * P:(c + 1) * P], qk_rot[:, a, c * P:(c + 1) * P], ident[:])
                        end(last, name)
                if st.exists(-1):
                    read("Y", t - 1)
                    out = begin("shift", t - 1)
                    last = nc.tensor.matmul(out[:, 0:P], shift_sb[:, 0], x_mid[:, st.slot(-1), P:C], start=True, stop=st.first(-1))
                    if not st.first(-1):
                        last = nc.tensor.matmul(out[:, 0:P], shift_sb[:, 1], x_mid[:, st.slot(-3), P:C], start=False, stop=True)
                    end(last, "shift")
                if st.exists(0):
                    for j in range(4):
                        read(f"S{j}", t)
                        out = begin(f"PT{j}", t)
                        for u in range(2):
                            for kb in range(1 if st.first(0) else 0, 2):
                                last = nc.tensor.transpose(out[:, (2 * u + kb) * P:(2 * u + kb + 1) * P], probs[:, j, u, kb * P:(kb + 1) * P], ident[:])
                        end(last, f"PT{j}")
                if st.exists(2):
                    if st.turn is None and t == SPLIT_STEPS[1] + 1:
                        pe.wait_ge(wqkv_split, 6)
                    read("xT", t + 2)
                    L = st.layer(2)
                    for a, name in enumerate(("q", "k", "v")):
                        if st.turn is None and t == SPLIT_STEPS[0]:
                            pe.wait_ge(wqkv_split, a + 1)
                        out = begin(name, t + 2)
                        for k in range(NC):
                            for n, (x_part, w_part) in enumerate(((xT_hi, wqkv_hi), (xT_hi, wqkv_lo), (xT_lo, wqkv_hi))):
                                last = nc.tensor.matmul(out[:], x_part[:, st.slot(2, 2), k * P:(k + 1) * P], w_part[:, L, k, a * INNER:(a + 1) * INNER],
                                                        start=(k == 0 and n == 0), stop=(k == NC - 1 and n == 2))
                        end(last, name)
                if st.exists(-1):
                    read("shift", t - 1)
                    out = begin("hT", t - 1)
                    for k in range(NC):
                        last = nc.tensor.transpose(out[:, k * P:(k + 1) * P], hn[:, k * P:(k + 1) * P], ident[:])
                    end(last, "hT")
                if st.exists(0):
                    for j in range(4):
                        read(f"PT{j}", t)
                    out = begin("oT", t)
                    for c in range(4):
                        for kb in range(1 if st.first(0) else 0, 2):
                            for half in range(2):
                                j, u = PLACE[2 * c + half]
                                last = nc.tensor.matmul(out[half * D2:(half + 1) * D2, c * P:(c + 1) * P],
                                                        v_sb[:, st.slot(0 if kb else -2), (2 * c + half) * D2:(2 * c + half + 1) * D2], PT[:, j, u, kb],
                                                        start=(kb == 0 or st.first(0)), stop=(kb == 1), tile_position=(0, half * D2))
                    end(last, "oT")
                if st.exists(-1):
                    read("hT", t - 1)
                    for j in range(3):
                        out = begin(f"H{j}", t - 1)
                        for i, chunk in enumerate((2 * j, 2 * j + 1, HW + 2 * j, HW + 2 * j + 1) if j < 2 else (HW - 1, 2 * HW, 2 * HW - 1)):
                            for k in range(NC):
                                last = nc.tensor.matmul(out[:, i * P:(i + 1) * P], w1_sb[:, st.layer(-1), k, chunk * P:(chunk + 1) * P], hT[:, k],
                                                        start=(k == 0), stop=(k == NC - 1))
                        end(last, f"H{j}")
                if st.exists(1):
                    read("qT", t + 1)
                    read("kT", t + 1)
                    for j in range(4):
                        out = begin(f"S{j}", t + 1)
                        nc.tensor.matmul(out[:], identb[:], mask_sb[:].rearrange("p a k -> p (a k)"), start=True, stop=False, skip_group_check=True)
                        for u, h in enumerate(PAIRS[j]):
                            rows = slice(h % 2 * D2, (h % 2 + 1) * D2)
                            for kb in range(1 if st.first(1) else 0, 2):
                                last = nc.tensor.matmul(out[:, (2 * u + kb) * P:(2 * u + kb + 1) * P], qT[rows, h // 2, :],
                                                        kT[rows, st.slot(1 if kb else -1), h // 2, :], start=False, stop=(u == 1 and kb == 1), skip_group_check=True)
                        end(last, f"S{j}")
                if st.exists(0):
                    read("oT", t)
                    out = begin("Y", t)
                    for c in range(4):
                        last = nc.tensor.matmul(out[:, 0:C], oT[:, c], wo_sb[:, st.layer(0), c], start=(c == 0), stop=(c == 3))
                    end(last, "Y")
                if st.exists(-1):
                    for j in range(3):
                        read(f"H{j}", t - 1)
                    out = begin("F", t - 1)
                    for c in range(HC):
                        rows = slice(0, P if c < HW else HR)
                        last = nc.tensor.matmul(out[:, 0:C], act_T[rows, c], w2_sb[rows, st.layer(-1), c], start=(c == 0), stop=(c == HC - 1))
                    end(last, "F")

        @block.scalar
        def _(act):
            w = Waiter(act)
            w.on(for_act, sum(r == "act" for r in READY_FOR.values())), w.on(max_made, 4)
            w.on(fnmr_made, 1, last_layer(-3))
            act.wait_ge(loaded_act, 48)
            act.wait_ge(zero_made, 1)

            def item(name, v):
                w.upto(for_act, ready[name, v])
                return bank(name)

            def round_wqkv(layer):
                act.wait_ge(loaded_pe[layer], 16 * 4)
                for a in range(3):
                    columns = slice(a * INNER, (a + 1) * INNER)
                    nc.scalar.copy(wqkv_hi[:, layer, :, columns], wqkv_sb[:, layer, :, columns]).then_inc(wqkv_rounded, 1)

            for st in walk(w, SEGMENTS, LAYERS * NT):
                t = st.t
                if t == SPLIT_STEPS[0] and st.turn is None:
                    round_wqkv(0)
                if st.exists(2):
                    src = item("xT", t + 2)
                    s = st.slot(2, 2)
                    nc.scalar.copy(xT_hi[:, s, P:P + 1], zero_col[:] if st.first(2) else carry_hi[:, st.slot(0)])
                    nc.scalar.copy(xT_hi[:, s, 0:P], src[:, 0:P])
                    nc.scalar.copy(carry_hi[:, st.slot(2)], src[:, C - 1:C])
                    nc.scalar.copy(xT_hi[:, s, P + 1:], src[:, P:C - 1]).then_inc(xT_rounded, 1)
                if st.exists(1):
                    src = item("qT", t + 1)
                    nc.scalar.copy(qT[:].rearrange("p c t -> p (c t)"), src[:]).then_inc(by_act, 1)
                    src = item("kT", t + 1)
                    nc.scalar.copy(kT[:, st.slot(1)].rearrange("p c t -> p (c t)"), src[:]).then_inc(by_act, 1)
                if st.exists(0):
                    for j in (0, 2):
                        src = item(f"PT{j}", t).rearrange("p (u b q) -> p u b q", u=2, b=2)
                        b0 = 1 if st.first(0) else 0
                        nc.scalar.copy(PT[:, j, :, b0:], src[:, :, b0:]).then_inc(by_act, 1)
                if st.exists(2):
                    for a, name in enumerate(("q", "k")):
                        src = item(name, t + 2)
                        nc.scalar.activation(squares[:, a], src[:], ACT.Square).then_inc(squares_made, 1)
                if st.exists(-1):
                    src = item("hT", t - 1)
                    for k in range(NC):
                        last = nc.scalar.activation(hT[:, k], src[:, k * P:(k + 1) * P], ACT.Identity,
                                                    bias=lnb_sb[:, st.layer(-1), k:k + 1], scale=lng_sb[:, st.layer(-1), k:k + 1])
                    last.then_inc(by_act, 1)
                if st.exists(0):
                    src = item("oT", t)
                    nc.scalar.copy(oT[:].rearrange("p c t -> p (c t)"), src[:]).then_inc(by_act, 1)
                if st.exists(2):
                    src = item("v", t + 2)
                    nc.scalar.copy(v_sb[:, st.slot(2)], src[:]).then_inc(by_act, 1)
                if t == SPLIT_STEPS[1] and st.turn is None:
                    round_wqkv(1)
                if last_layer(-3)(st):
                    w.upto(fnmr_made, nth_last(st, -3) + 1)
                    x_tile = x_sb[:, st.tile(-3), :]
                    nc.scalar.activation(x_tile, x_tile, ACT.Identity, bias=fnmr[:, st.slot(-3)], scale=frstd[:, st.slot(-3)])
                if st.exists(-1):
                    for j in range(3):
                        src = item(f"H{j}", t - 1)
                        for i in range(2):
                            chunk = 2 * j + i
                            if chunk < HW:
                                last = nc.scalar.activation(gate[:, chunk], src[:, (2 + i) * P:(3 + i) * P], ACT.Gelu,
                                                            bias=b1_sb[:, st.layer(-1), HW + chunk:HW + chunk + 1])
                            else:
                                last = nc.scalar.activation(gate[0:HR, chunk], src[HR:P, P:2 * P], ACT.Gelu, bias=b1_sb[HR:P, st.layer(-1), 2 * HW:])
                        last.then_inc(gate_made, 1)
                if st.exists(1):
                    for j in range(4):
                        w.upto(max_made, 4 * (t + 1) + j + 1)
                        src = bank(f"S{j}")
                        b0 = P if st.first(1) else 0
                        for u, h in enumerate(PAIRS[j]):
                            last = nc.scalar.activation(probs[:, j, u, b0:], src[:, u * 2 * P + b0:(u + 1) * 2 * P], ACT.Exp,
                                                        bias=negmax[:, j, u:u + 1], accum_out=sums[:, j, u:u + 1])
                        last.then_inc(exps_made, 1)

        @block.vector
        def _(dve):
            w = Waiter(dve)
            w.on(for_dve, sum(r == "dve" for r in READY_FOR.values()))
            for s_, n in ((squares_made, 2), (sin_rnorm_made, 3), (gate_made, 3), (hrstd_made, 1), (x_b2_made, 1),
                          (hstats_made, 1), (cos_made, 1), (rot_made, 1), (exps_made, 4), (rsums_made, 4), (xT_rounded, 1)):
                w.on(s_, n)
            w.on(fstats_made, 1, last_layer(-2)), w.on(frstd_made, 1, last_layer(-3))
            dve.wait_ge(loaded_dve, 48)
            for l in range(LAYERS):
                nc.vector.tensor_scalar(qks_sb[:, l, 0], qks_sb[:, l, 0], 8.0, None, ALU.mult).then_inc(qscale_made, 1)
            dve.wait_ge(qscale_made, LAYERS)

            def item(name, v):
                if READY_FOR[name] == "dve":
                    w.upto(for_dve, ready[name, v])
                return bank(name)

            def split_wqkv(layer):
                for a in range(3):
                    dve.wait_ge(wqkv_rounded, 3 * layer + a + 1)
                    columns = slice(a * INNER, (a + 1) * INNER)
                    nc.vector.tensor_tensor(wqkv_lo[:, layer, :, columns], wqkv_sb[:, layer, :, columns],
                                            wqkv_hi[:, layer, :, columns], ALU.subtract).then_inc(wqkv_split, 1)

            def hidden(st, j):
                t = st.t
                w.upto(gate_made, 3 * (t - 1) + j + 1)
                for i in range(2):
                    chunk = 2 * j + i
                    rows, column = (slice(0, P), chunk) if chunk < HW else (slice(0, HR), 2 * HW)
                    last = nc.vector.scalar_tensor_tensor(act_T[rows, chunk], bank(f"H{j}")[rows, i * P:(i + 1) * P],
                                                          b1_dve[rows, st.layer(-1), column:column + 1], gate[rows, chunk], ALU.add, ALU.mult)
                last.then_inc(by_dve, 1)

            for st in walk(w, SEGMENTS, LAYERS * NT):
                t = st.t
                if t == SPLIT_STEPS[0] and st.turn is None:
                    split_wqkv(0)
                if st.exists(2):
                    w.upto(xT_rounded, t + 3)
                    src, s = item("xT", t + 2), st.slot(2, 2)
                    nc.vector.tensor_copy(xT_lo[:, s, P:P + 1], zero_col[:] if st.first(2) else carry_lo[:, st.slot(0)])
                    nc.vector.tensor_tensor(xT_lo[:, s, 0:P], src[:, 0:P], xT_hi[:, s, 0:P], ALU.subtract)
                    nc.vector.tensor_tensor(carry_lo[:, st.slot(2)], src[:, C - 1:C], carry_hi[:, st.slot(2)], ALU.subtract)
                    nc.vector.tensor_tensor(xT_lo[:, s, P + 1:], src[:, P:C - 1], xT_hi[:, s, P + 1:], ALU.subtract).then_inc(by_dve, 1)
                if st.exists(-1):
                    mid, up = x_mid[:, st.slot(-1)], item("shift", t - 1)
                    first_stats = nc.vector.bn_stats(stats[:, 0], mid[:, 0:P])
                    if t + st.skipped == NT + 1 and st.turn is None:
                        first_stats.then_inc(first_layer_done, 1)
                    nc.vector.bn_stats(stats[:, 1], up[:, 0:P]).then_inc(hstats_made, 1)
                    w.upto(hstats_made, t)
                    nc.vector.bn_aggr(mv[:], stats[:]).then_inc(hmv_made, 1)
                if last_layer(-2)(st):
                    if not st.exists(-1):
                        dve.drain().then_inc(last_x_written, 1)
                        dve.wait_ge(last_x_written, 1)
                    nc.vector.bn_stats(fstats[:, st.slot(-2)], x_sb[:, st.tile(-2), :]).then_inc(fstats_made, 1)
                if last_layer(-3)(st):
                    w.upto(frstd_made, nth_last(st, -3) + 1)
                    nc.vector.scalar_tensor_tensor(fnmr[:, st.slot(-3)], fmv[:, st.slot(-3), 0:1], -1.0, frstd[:, st.slot(-3)], ALU.mult, ALU.mult).then_inc(fnmr_made, 1)
                if last_layer(-2)(st):
                    w.upto(fstats_made, nth_last(st, -2) + 1)
                    nc.vector.bn_aggr(fmv[:, st.slot(-2)], fstats[:, st.slot(-2)]).then_inc(fmv_made, 1)
                if st.exists(0):
                    for j in (1, 3):
                        src = item(f"PT{j}", t).rearrange("p (u b q) -> p u b q", u=2, b=2)
                        b0 = 1 if st.first(0) else 0
                        nc.vector.tensor_copy(PT[:, j, :, b0:], src[:, :, b0:]).then_inc(by_dve, 1)
                if st.exists(-1):
                    w.upto(hrstd_made, t)
                    nc.vector.tensor_scalar(hn[:, 0:P], mid[:, 0:P], mv[:, 0:1], rstd[:], ALU.subtract, ALU.mult)
                    nc.vector.tensor_scalar(hn[:, P:C], up[:, 0:P], mv[:, 0:1], rstd[:], ALU.subtract, ALU.mult).then_inc(by_dve, 1)
                if st.exists(2):
                    for a, name in enumerate(("q", "k")):
                        w.upto(squares_made, 2 * (t + 2) + a + 1)
                        nc.vector.tensor_tensor(qk[:, a].rearrange("p (h d) -> p h d", d=D2), bank(name)[:].rearrange("p (h d) -> p h d", d=D2),
                                                qks_sb[:, st.layer(2), a].unsqueeze(1).to_broadcast([P, H2, D2]), ALU.mult).then_inc(by_dve, 1)
                    nc.vector.tensor_reduce(norm2[:], squares[:].rearrange("p a (h d) -> p (a h) d", d=D2), AX.X, ALU.add).then_inc(norm2_made, 1)
                if st.exists(2):
                    w.upto(sin_rnorm_made, 3 * (t + 2) + 1)
                    nc.vector.tensor_tensor(qk_cos[:].rearrange("p a (h d) -> p a h d", d=D2 // 2), qk[:].rearrange("p a (h d) -> p a h d", d=D2 // 2),
                                            cos_sb[:, st.position(2)].unsqueeze(2).to_broadcast([P, 2, 2 * H2, D2 // 2]), ALU.mult).then_inc(cos_made, 1)
                    w.upto(cos_made, t + 3)
                    w.upto(sin_rnorm_made, 3 * (t + 2) + 2)
                    for half, op in ((0, ALU.subtract), (1, ALU.add)):
                        of_half = lambda a: a.rearrange("p a (h s d) -> p a h s d", s=2, d=D2 // 2)[:, :, :, half]
                        last = nc.vector.tensor_tensor(of_half(qk_cos), of_half(qk_cos), of_half(qk_sin), op)
                    last.then_inc(rot_made, 1)
                if st.exists(-1):
                    for j in range(3):
                        hidden(st, j)
                if t == SPLIT_STEPS[1] and st.turn is None:
                    split_wqkv(1)
                for j in range(4):
                    if st.exists(1):
                        src = item(f"S{j}", t + 1).rearrange("p (u k) -> p u k", u=2)
                        nc.vector.tensor_reduce(negmax[:, j], src[:, :, P if st.first(1) else 0:], AX.X, ALU.max, negate=True).then_inc(max_made, 1)
                    if j == 1 and st.exists(2):
                        w.upto(rot_made, t + 3)
                        w.upto(sin_rnorm_made, 3 * (t + 2) + 3)
                        nc.vector.tensor_tensor(qk_rot[:].rearrange("p a (h d) -> p (a h) d", d=D2), qk_cos[:].rearrange("p a (h d) -> p (a h) d", d=D2),
                                                rnorm[:].unsqueeze(2).to_broadcast([P, 2 * H2, D2]), ALU.mult).then_inc(rotary_done, 1)
                for j in range(4):
                    if st.exists(1):
                        w.upto(exps_made, 4 * (t + 1) + j + 1)
                        nc.vector.reciprocal(rsums[:, j], sums[:, j]).then_inc(rsums_made, 1)
                        w.upto(rsums_made, 4 * (t + 1) + j + 1)
                        p4 = probs[:, j, :, P if st.first(1) else 0:]
                        nc.vector.tensor_tensor(p4, p4, rsums[:, j].unsqueeze(2).to_broadcast([P, 2, P if st.first(1) else 2 * P]), ALU.mult).then_inc(by_dve, 1)
                    if j == 1 and st.exists(0):
                        src = item("Y", t)
                        nc.vector.tensor_tensor(x_mid[:, st.slot(0)], src[:, 0:C], x_sb[:, st.tile(0), :], ALU.add).then_inc(by_dve, 1)
                if st.exists(-1):
                    src = item("F", t - 1)
                    w.upto(x_b2_made, t)
                    nc.vector.tensor_tensor(x_sb[:, st.tile(-1), :], src[:, 0:C], x_sb[:, st.tile(-1), :], ALU.add).then_inc(by_dve, 1)


def final_phase(nc, x_sb, x1_dram, x1_places, out):
    sem = nc.alloc_semaphore
    sum_made_dve, sum_made_pool, out_stored = sem("sum_made_dve"), sem("sum_made_pool"), sem("out_stored")
    out_tiles = out.rearrange("b (t p) c -> p (b t) c", p=P)
    STEP = 3
    pieces = []
    for n, (tiles, place, loaded) in enumerate(x1_places):
        for at in range(tiles.start, tiles.stop, STEP):
            end = min(at + STEP, tiles.stop)
            pieces.append((slice(at, end), place[:, at - tiles.start:end - tiles.start], loaded, n in (1, 2)))
    by_dve, by_pool = ([p for p in pieces if p[3] == late] for late in (False, True))
    with ExitStack() as ctx:
        block = ctx.enter_context(nc.Block())

        @block.sync
        def _(sp):
            tiles, place, loaded = x1_places[-1]
            sp.dma_start(place, x1_dram[:, tiles]).then_inc(loaded, 16)
            for i in range(max(len(by_dve), len(by_pool))):
                for mine, sum_made in ((by_dve, sum_made_dve), (by_pool, sum_made_pool)):
                    if i < len(mine):
                        sp.wait_ge(sum_made, i + 1)
                        here = mine[i][0]
                        sp.dma_start(out_tiles[:, here], x_sb[:, here]).then_inc(out_stored, 16)
            sp.wait_ge(out_stored, 16 * len(pieces))

        @block.gpsimd
        def _(pool):
            for here, place, loaded, _ in by_pool:
                pool.wait_ge(loaded, 16)
                nc.gpsimd.tensor_tensor(out=x_sb[:, here], in0=x_sb[:, here], in1=place, op=ALU.add).then_inc(sum_made_pool, 1)

        @block.vector
        def _(dve):
            for here, place, loaded, _ in by_dve:
                dve.wait_ge(loaded, 16)
                nc.vector.tensor_tensor(x_sb[:, here], x_sb[:, here], place, ALU.add).then_inc(sum_made_dve, 1)


def program(nc, ins, out):
    with ExitStack() as ctx:
        hold = lambda c, n, s, d=F32: c.enter_context(nc.sbuf_tensor(n, s, d))
        x_sb = hold(ctx, "x_sb", [P, NT, C])
        ident = hold(ctx, "ident", [P, P])
        identb = hold(ctx, "identb", [P, P], BF16)
        mask_sb = hold(ctx, "mask_sb", [P, 2, 2 * P], BF16)
        shift_sb = hold(ctx, "shift_sb", [P, 2, P])
        x1_dram = nc.dram_tensor("x1_dram", (P, NT, C), F32).ap()
        with ExitStack() as till_fed:
            QO = hold(till_fed, "QO", [P, NH, TB, D1])
            with ExitStack() as heads:
                K1, V1 = (hold(heads, n, [P, NH, TB, D1]) for n in ("K1", "V1"))
                project_phase(nc, ins, x_sb, QO, K1, V1, ident, identb)
                attention_phase(nc, QO, K1, V1, mask_sb, shift_sb, ident, identb)
            weights = Weights(nc, till_fed)
            output_phase(nc, ins, x_sb, QO, ident, x1_dram, lambda sp: weights.load(sp, ins))
            free_space = QO[:].rearrange("p n t d -> p (n t d)")
            x1_places = weights.x1_places(free_space)
            feed_forward_phase(nc, weights, x_sb, free_space, x1_dram, x1_places, mask_sb, shift_sb, ident, identb)
            final_phase(nc, x_sb, x1_dram, x1_places, out)


def kernel(**inputs):
    import numpy as np
    import concourse.bacc as bacc
    from concourse.bass_utils import run_bass_kernel_spmd

    i = {k.replace("L0_", ""): np.asarray(v) for k, v in inputs.items()}
    f32 = np.float32
    pos = np.arange(T, dtype=f32)
    inv = (f32(1.0) / f32(10000.0) ** (np.arange(0, D1, 2, dtype=f32) / f32(D1))).astype(f32)
    fr = pos[:, None] * inv[None, :]
    half = np.arange(0, D2, 2, dtype=f32)
    inv2 = (f32(1.0) / f32(10000.0) ** (half / f32(D2))).astype(f32)
    fr2 = pos[:, None] * inv2[None, :]
    base = (half + f32(0.4 * D2)) / f32(1.4 * D2)
    power = (pos - f32(T // 2)) / f32(P // 2)
    scale = (base[None, :] ** power[:, None]).astype(f32)
    cos2, sin2 = np.cos(fr2), np.sin(fr2)
    qc, qs, kc, ks = cos2 * scale, sin2 * scale, cos2 / scale, sin2 / scale

    def chunked(w, axis):
        a, gate = np.split(w, 2, axis=axis)
        (a, a_rest), (gate, gate_rest) = (np.split(x, [HW * P], axis=axis) for x in (a, gate))
        pad = [(0, 0)] * w.ndim
        pad[axis] = (0, HR - HID % P)
        return np.concatenate([a, gate, np.pad(a_rest, pad), np.pad(gate_rest, pad)], axis=axis)

    def by_partition(w):
        return w.reshape(LAYERS, -1, P).transpose(2, 0, 1)

    arrays = {
        "x": i["attn_x"],
        "wqkv1": np.concatenate([i["attn_Wq"].T, i["attn_Wk"].T, i["attn_Wv"].T], axis=1),
        "bqkv1": np.concatenate([i["attn_bq"], i["attn_bk"], i["attn_bv"]]),
        "cos1": np.cos(fr).astype(f32),
        "sin1": np.concatenate([-np.sin(fr), np.sin(fr)], axis=1).astype(f32),
        "wo1": i["attn_Wo"].T,
        "bo1": i["attn_bo"],
        "wqkv2": i["ffn_wqkv"],
        "wo2": i["ffn_wo"],
        "w1": chunked(i["ffn_w1"], 2),
        "w2": np.pad(i["ffn_w2"], ((0, 0), (0, HC * P - HID), (0, 0))),
        "qk_scale": np.stack([i["ffn_q_scale"], i["ffn_k_scale"]], axis=1),
        "b2": i["ffn_b2"],
        "ln_g": by_partition(i["ffn_ln_g"]),
        "ln_b": by_partition(i["ffn_ln_b"]),
        "b1": by_partition(chunked(i["ffn_b1"], 1)),
        "cos2": np.concatenate([qc, kc], axis=1).astype(f32),
        "sin2": np.concatenate([qs, ks], axis=1).astype(f32),
    }
    arrays = {k: np.ascontiguousarray(v) for k, v in arrays.items()}
    nc = bacc.Bacc("TRN2", target_bir_lowering=False, num_devices=1)
    ins = {k: nc.dram_tensor("in_" + k, v.shape, mybir.dt.from_np(v.dtype), kind="ExternalInput").ap()
           for k, v in arrays.items()}
    out = nc.dram_tensor("out_0", (B, T, C), F32, kind="ExternalOutput").ap()
    program(nc, ins, out)
    r = run_bass_kernel_spmd(nc, [{"in_" + k: v for k, v in arrays.items()}], core_ids=[0])
    return r.results[0]["out_0"]
```
